# Optimizing a Trainium2 kernel written in Bass

```python
import numpy as np
import jax
import jax.numpy as jnp

def _softmax(x, axis=-1):
    return jax.nn.softmax(x, axis=axis)

def _gelu(x):
    return jax.nn.gelu(x, approximate=True)

def _silu(x):
    return jax.nn.silu(x)

def _sigmoid(x):
    return jax.nn.sigmoid(x)

def _layernorm(x, axis=-1, eps=1e-05):
    m = jnp.mean(x, axis=axis, keepdims=True)
    v = jnp.var(x, axis=axis, keepdims=True)
    return (x - m) / jnp.sqrt(v + eps)

def _scatter_add(tgt, idx, src, axis=0):
    return tgt.at[idx].add(src)

def _segment_sum(src, seg, n):
    return jax.ops.segment_sum(src, seg, n)
kernel_name = 'mk_audio_tower_d1_tok_audfeat256_r4_931172'

def setup_inputs(seed: int=0):
    np.random.seed(seed)
    _w = jnp.asarray

    def _rec_inputs():
        import jax
        import jax.numpy as jnp
        _rk = jax.random.key(seed)
        x = -0.000392918 + 0.999932 * jax.random.normal(jax.random.fold_in(_rk, 1), (16, 750, 64), jnp.float32)
        return x
    x = _rec_inputs()

    def _L0_tok_setup():
        import jax, jax.numpy as jnp
        import numpy as np
        from jax import lax
        B, S, CIN, COUT, K = (32, 512, 64, 64, 16)
        key = jax.random.key(seed)
        k1, k2, k3, k4 = jax.random.split(key, 4)
        x = jax.random.normal(k1, (B, S, CIN), dtype=jnp.float32)
        w_real = jax.random.normal(k2, (COUT, CIN, K), dtype=jnp.float32) * 0.1
        w_imag = jax.random.normal(k3, (COUT, CIN, K), dtype=jnp.float32) * 0.1
        phases = jax.random.normal(k4, (K,), dtype=jnp.float32) * 0.1
        return {'x': x, 'w_real': w_real, 'w_imag': w_imag, 'phases': phases}
    _L0_tok_all = _L0_tok_setup()
    _L0_tok_in = {k: v for k, v in _L0_tok_all.items() if k in ('w_real', 'w_imag', 'phases')}
    del _L0_tok_all

    def _L0_attn_setup():
        import jax, jax.numpy as jnp
        import numpy as np
        I, H, O, L = (64, 128, 64, 2)
        B, S = (16, 512)
        EPS = 1e-05

        def _layernorm(x, w, b):
            mu = jnp.mean(x, axis=-1, keepdims=True)
            var = jnp.mean(jnp.square(x - mu), axis=-1, keepdims=True)
            return (x - mu) * jax.lax.rsqrt(var + EPS) * w + b
        key = jax.random.key(seed)
        ks = jax.random.split(key, 16)
        s_in = 1.0 / np.sqrt(I)
        s_h = 1.0 / np.sqrt(H)
        return {'x': jax.random.normal(ks[0], (B, S, I), dtype=jnp.float32), 'in_W': jax.random.uniform(ks[1], (H, I), minval=-s_in, maxval=s_in, dtype=jnp.float32), 'in_b': jax.random.uniform(ks[2], (H,), minval=-s_in, maxval=s_in, dtype=jnp.float32), 'A_W': jax.random.uniform(ks[3], (L, H, H), minval=-s_h, maxval=s_h, dtype=jnp.float32), 'B_W': jax.random.uniform(ks[4], (L, H, H), minval=-s_h, maxval=s_h, dtype=jnp.float32), 'B_b': jax.random.uniform(ks[5], (L, H), minval=-s_h, maxval=s_h, dtype=jnp.float32), 'C_W': jax.random.uniform(ks[6], (L, H, H), minval=-s_h, maxval=s_h, dtype=jnp.float32), 'C_b': jax.random.uniform(ks[7], (L, H), minval=-s_h, maxval=s_h, dtype=jnp.float32), 'D_W': jax.random.uniform(ks[8], (L, H, H), minval=-s_h, maxval=s_h, dtype=jnp.float32), 'D_b': jax.random.uniform(ks[9], (L, H), minval=-s_h, maxval=s_h, dtype=jnp.float32), 'ln_w': jnp.ones((L, H), dtype=jnp.float32), 'ln_b': jnp.zeros((L, H), dtype=jnp.float32), 'out_W': jax.random.uniform(ks[10], (O, H), minval=-s_h, maxval=s_h, dtype=jnp.float32), 'out_b': jax.random.uniform(ks[11], (O,), minval=-s_h, maxval=s_h, dtype=jnp.float32)}
    _L0_attn_all = _L0_attn_setup()
    _L0_attn_in = {k: v for k, v in _L0_attn_all.items() if k in ('in_W', 'in_b', 'A_W', 'B_W', 'B_b', 'C_W', 'C_b', 'D_W', 'D_b', 'ln_w', 'ln_b', 'out_W', 'out_b')}
    del _L0_attn_all

    def _L0_ffn_setup():
        import jax, jax.numpy as jnp
        import numpy as np
        B, N, D = (16, 1024, 64)
        NUM_EXPERTS, TOP_K, HEADS = (4, 2, 4)
        N_EDGES = 262144
        LN_EPS = 1e-05

        def _layernorm(x, g, b):
            mu = x.mean(-1, keepdims=True)
            var = ((x - mu) ** 2).mean(-1, keepdims=True)
            return (x - mu) * jax.lax.rsqrt(var + LN_EPS) * g + b

        def _forward(x, edge_index, W_gat, att_src, att_dst, b_gat, ln_gamma, ln_beta, W1, b1, W2, b2):
            Bc, Nc, Dc = x.shape
            M = Bc * Nc
            x_flat = x.reshape(M, Dc)
            h = (x_flat @ W_gat).reshape(M, HEADS, NUM_EXPERTS)
            loops = jnp.arange(M, dtype=edge_index.dtype)
            src = jnp.concatenate([edge_index[0], loops])
            dst = jnp.concatenate([edge_index[1], loops])
            a_src = (h * att_src).sum(-1)
            a_dst = (h * att_dst).sum(-1)
            e = jax.nn.leaky_relu(a_src[src] + a_dst[dst], negative_slope=0.2)
            e_max = jax.ops.segment_max(e, dst, num_segments=M)
            ee = jnp.exp(e - e_max[dst])
            denom = jax.ops.segment_sum(ee, dst, num_segments=M)
            alpha = ee / (denom[dst] + 1e-16)
            msg = h[src] * alpha[:, :, None]
            agg = jax.ops.segment_sum(msg, dst, num_segments=M).reshape(M, HEADS * NUM_EXPERTS) + b_gat
            scores = _layernorm(agg, ln_gamma, ln_beta).reshape(M, HEADS, NUM_EXPERTS).mean(1)
            scores = scores.reshape(Bc, Nc, NUM_EXPERTS)
            topk_s, topk_i = jax.lax.top_k(scores, TOP_K)
            w = jax.nn.softmax(topk_s, axis=-1)
            out = jnp.zeros_like(x)
            for ei in range(NUM_EXPERTS):
                g = jnp.where(topk_i == ei, w, 0.0).sum(-1)
                hh = jax.nn.gelu(x @ W1[ei] + b1[ei], approximate=False)
                out = out + g[..., None] * (hh @ W2[ei] + b2[ei])
            return out
        key = jax.random.key(seed)
        ks = jax.random.split(key, 8)
        s = 0.05
        return {'x': jax.random.normal(ks[0], (B, N, D), jnp.float32), 'W_gat': jax.random.normal(ks[1], (D, HEADS * NUM_EXPERTS), jnp.float32) * s, 'att_src': jax.random.normal(ks[2], (HEADS, NUM_EXPERTS), jnp.float32) * s, 'att_dst': jax.random.normal(ks[3], (HEADS, NUM_EXPERTS), jnp.float32) * s, 'b_gat': jnp.zeros((HEADS * NUM_EXPERTS,), jnp.float32), 'ln_gamma': jnp.ones((HEADS * NUM_EXPERTS,), jnp.float32), 'ln_beta': jnp.zeros((HEADS * NUM_EXPERTS,), jnp.float32), 'W1': jax.random.normal(ks[4], (NUM_EXPERTS, D, 2 * D), jnp.float32) * s, 'b1': jnp.zeros((NUM_EXPERTS, 2 * D), jnp.float32), 'W2': jax.random.normal(ks[5], (NUM_EXPERTS, 2 * D, D), jnp.float32) * s, 'b2': jnp.zeros((NUM_EXPERTS, D), jnp.float32), 'edge_index': jax.random.randint(ks[6], (2, N_EDGES), 0, B * N, jnp.int32)}
    _L0_ffn_all = _L0_ffn_setup()
    _L0_ffn_in = {k: v for k, v in _L0_ffn_all.items() if k in ('W_gat', 'att_src', 'att_dst', 'b_gat', 'ln_gamma', 'ln_beta', 'W1', 'b1', 'W2', 'b2', 'edge_index')}
    del _L0_ffn_all
    return {'x': x, 'L0_tok_w_real': _L0_tok_in['w_real'], 'L0_tok_w_imag': _L0_tok_in['w_imag'], 'L0_tok_phases': _L0_tok_in['phases'], 'L0_attn_in_W': _L0_attn_in['in_W'], 'L0_attn_in_b': _L0_attn_in['in_b'], 'L0_attn_A_W': _L0_attn_in['A_W'], 'L0_attn_B_W': _L0_attn_in['B_W'], 'L0_attn_B_b': _L0_attn_in['B_b'], 'L0_attn_C_W': _L0_attn_in['C_W'], 'L0_attn_C_b': _L0_attn_in['C_b'], 'L0_attn_D_W': _L0_attn_in['D_W'], 'L0_attn_D_b': _L0_attn_in['D_b'], 'L0_attn_ln_w': _L0_attn_in['ln_w'], 'L0_attn_ln_b': _L0_attn_in['ln_b'], 'L0_attn_out_W': _L0_attn_in['out_W'], 'L0_attn_out_b': _L0_attn_in['out_b'], 'L0_ffn_W_gat': _L0_ffn_in['W_gat'], 'L0_ffn_att_src': _L0_ffn_in['att_src'], 'L0_ffn_att_dst': _L0_ffn_in['att_dst'], 'L0_ffn_b_gat': _L0_ffn_in['b_gat'], 'L0_ffn_ln_gamma': _L0_ffn_in['ln_gamma'], 'L0_ffn_ln_beta': _L0_ffn_in['ln_beta'], 'L0_ffn_W1': _L0_ffn_in['W1'], 'L0_ffn_b1': _L0_ffn_in['b1'], 'L0_ffn_W2': _L0_ffn_in['W2'], 'L0_ffn_b2': _L0_ffn_in['b2'], 'L0_ffn_edge_index': _L0_ffn_in['edge_index']}

def reference(x, L0_tok_w_real, L0_tok_w_imag, L0_tok_phases, L0_attn_in_W, L0_attn_in_b, L0_attn_A_W, L0_attn_B_W, L0_attn_B_b, L0_attn_C_W, L0_attn_C_b, L0_attn_D_W, L0_attn_D_b, L0_attn_ln_w, L0_attn_ln_b, L0_attn_out_W, L0_attn_out_b, L0_ffn_W_gat, L0_ffn_att_src, L0_ffn_att_dst, L0_ffn_b_gat, L0_ffn_ln_gamma, L0_ffn_ln_beta, L0_ffn_W1, L0_ffn_b1, L0_ffn_W2, L0_ffn_b2, L0_ffn_edge_index):
    import jax
    import jax.numpy as jnp

    def _L0_tok_ref(x, w_real, w_imag, phases):
        import jax, jax.numpy as jnp
        import numpy as np
        from jax import lax
        B, S, CIN, COUT, K = (32, 512, 64, 64, 16)
        w_eff = jnp.cos(phases)[None, None, :] * w_real - jnp.sin(phases)[None, None, :] * w_imag
        y = lax.conv_general_dilated(jnp.transpose(x, (0, 2, 1)), w_eff, window_strides=(1,), padding='VALID', dimension_numbers=('NCH', 'OIH', 'NCH'))
        return jnp.transpose(y, (0, 2, 1))

    def _L0_attn_ref(x, in_W, in_b, A_W, B_W, B_b, C_W, C_b, D_W, D_b, ln_w, ln_b, out_W, out_b):
        import jax, jax.numpy as jnp
        import numpy as np
        I, H, O, L = (64, 128, 64, 2)
        B, S = (16, 512)
        EPS = 1e-05

        def _layernorm(x, w, b):
            mu = jnp.mean(x, axis=-1, keepdims=True)
            var = jnp.mean(jnp.square(x - mu), axis=-1, keepdims=True)
            return (x - mu) * jax.lax.rsqrt(var + EPS) * w + b
        x = jnp.einsum('bsi,hi->bsh', x, in_W) + in_b
        bsz = x.shape[0]
        for l in range(L):
            bx = jnp.einsum('bsh,gh->bsg', x, B_W[l]) + B_b[l]
            dx = jnp.einsum('bsh,gh->bsg', x, D_W[l]) + D_b[l]
            Al = A_W[l]

            def step(h, bxt):
                h = jnp.tanh(h @ Al.T + bxt)
                return (h, h)
            h0 = jnp.zeros((bsz, H), dtype=x.dtype)
            _, hs = jax.lax.scan(step, h0, jnp.swapaxes(bx, 0, 1))
            hs = jnp.swapaxes(hs, 0, 1)
            y = jnp.einsum('bsh,gh->bsg', hs, C_W[l]) + C_b[l] + dx
            x = _layernorm(x + y, ln_w[l], ln_b[l])
        return jnp.einsum('bsh,oh->bso', x, out_W) + out_b

    def _L0_ffn_ref(x, W_gat, att_src, att_dst, b_gat, ln_gamma, ln_beta, W1, b1, W2, b2, edge_index):
        import jax, jax.numpy as jnp
        import numpy as np
        B, N, D = (16, 1024, 64)
        NUM_EXPERTS, TOP_K, HEADS = (4, 2, 4)
        N_EDGES = 262144
        LN_EPS = 1e-05

        def _layernorm(x, g, b):
            mu = x.mean(-1, keepdims=True)
            var = ((x - mu) ** 2).mean(-1, keepdims=True)
            return (x - mu) * jax.lax.rsqrt(var + LN_EPS) * g + b

        def _forward(x, edge_index, W_gat, att_src, att_dst, b_gat, ln_gamma, ln_beta, W1, b1, W2, b2):
            Bc, Nc, Dc = x.shape
            M = Bc * Nc
            x_flat = x.reshape(M, Dc)
            h = (x_flat @ W_gat).reshape(M, HEADS, NUM_EXPERTS)
            loops = jnp.arange(M, dtype=edge_index.dtype)
            src = jnp.concatenate([edge_index[0], loops])
            dst = jnp.concatenate([edge_index[1], loops])
            a_src = (h * att_src).sum(-1)
            a_dst = (h * att_dst).sum(-1)
            e = jax.nn.leaky_relu(a_src[src] + a_dst[dst], negative_slope=0.2)
            e_max = jax.ops.segment_max(e, dst, num_segments=M)
            ee = jnp.exp(e - e_max[dst])
            denom = jax.ops.segment_sum(ee, dst, num_segments=M)
            alpha = ee / (denom[dst] + 1e-16)
            msg = h[src] * alpha[:, :, None]
            agg = jax.ops.segment_sum(msg, dst, num_segments=M).reshape(M, HEADS * NUM_EXPERTS) + b_gat
            scores = _layernorm(agg, ln_gamma, ln_beta).reshape(M, HEADS, NUM_EXPERTS).mean(1)
            scores = scores.reshape(Bc, Nc, NUM_EXPERTS)
            topk_s, topk_i = jax.lax.top_k(scores, TOP_K)
            w = jax.nn.softmax(topk_s, axis=-1)
            out = jnp.zeros_like(x)
            for ei in range(NUM_EXPERTS):
                g = jnp.where(topk_i == ei, w, 0.0).sum(-1)
                hh = jax.nn.gelu(x @ W1[ei] + b1[ei], approximate=False)
                out = out + g[..., None] * (hh @ W2[ei] + b2[ei])
            return out
        return _forward(x, edge_index, W_gat, att_src, att_dst, b_gat, ln_gamma, ln_beta, W1, b1, W2, b2)
    h = _L0_tok_ref(x, L0_tok_w_real, L0_tok_w_imag, L0_tok_phases)
    h = h + _L0_attn_ref(_layernorm(h, axis=-1), L0_attn_in_W, L0_attn_in_b, L0_attn_A_W, L0_attn_B_W, L0_attn_B_b, L0_attn_C_W, L0_attn_C_b, L0_attn_D_W, L0_attn_D_b, L0_attn_ln_w, L0_attn_ln_b, L0_attn_out_W, L0_attn_out_b)
    h = h + _L0_ffn_ref(_layernorm(h, axis=-1), L0_ffn_W_gat, L0_ffn_att_src, L0_ffn_att_dst, L0_ffn_b_gat, L0_ffn_ln_gamma, L0_ffn_ln_beta, L0_ffn_W1, L0_ffn_b1, L0_ffn_W2, L0_ffn_b2, L0_ffn_edge_index)
    return h

_drawn_inputs = setup_inputs


def setup_inputs(seed=0):
    import zlib

    import numpy as np

    out = dict(_drawn_inputs(seed))
    spreads = {'L0_attn_ln_w': (1.0, 0.2),
     'L0_attn_ln_b': (0.0, 0.37),
     'L0_ffn_b_gat': (0.0, 0.44),
     'L0_ffn_ln_gamma': (1.0, 0.6),
     'L0_ffn_ln_beta': (0.0, 0.8),
     'L0_ffn_b1': (0.0, 0.8),
     'L0_ffn_b2': (0.0, 0.387)}
    factors = {'L0_attn_B_b': 6.086,
     'L0_attn_C_b': 3.61,
     'L0_attn_D_b': 3.742,
     'L0_attn_out_b': 3.297,
     'L0_ffn_att_src': 8.0,
     'L0_ffn_att_dst': 8.0}
    for name, (base, spread) in spreads.items():
        noise = np.random.default_rng([zlib.crc32(name.encode()), seed]).standard_normal(out[name].shape)
        drawn = base * np.exp(spread * noise) if base else spread * noise
        out[name] = jnp.asarray(drawn.astype(out[name].dtype))
    for name, factor in factors.items():
        out[name] = (out[name] * factor).astype(out[name].dtype)
    return out
```

```python
import concourse.bass as bass
from concourse import mybir
from contextlib import ExitStack


def audio_tower_program(nc, x_t, conv_wr, conv_wi, phases, in_w, in_b, a_w, b_w, b_b, c_w, c_b, d_w, d_b,
                        ln_w, ln_b, out_w, out_b, w_gat, att_src, att_dst, b_gat, gamma, beta,
                        w1, b1, w2, b2, edges, out):
    fp32, bf16 = mybir.dt.float32, mybir.dt.bfloat16
    u32, i32 = mybir.dt.uint32, mybir.dt.int32
    ALU, ACT, AX = mybir.AluOpType, mybir.ActivationFunctionType, mybir.AxisListType
    ds = bass.ds

    P = 128
    B, T, C, H = 16, 735, 64, 128
    TAPS = 16
    TP = 736
    M = B * T
    MP = B * TP
    NB = MP // P
    XC = 750 * B
    CH = 512
    NC = MP // CH
    HEADS, EXPERTS = 4, 4
    F = HEADS * EXPERTS
    ROW = HEADS + F
    SLOTS = 40
    NE = edges.shape[1] * P // 2
    ET = NE // P
    ITERS = 64
    TI = ET // ITERS
    STEPS = 2 * TP // ITERS
    SC = STEPS * B
    GR, GS = 4, TI // 4
    FAR = float(1 << 23)
    EMPTY = 16383
    EPS = 1e-5
    NONE = -1e30
    assert NC * CH == MP and TI * ITERS == ET and STEPS * ITERS == 2 * TP and SC <= 512

    ell = nc.dram_tensor("ell", (MP * SLOTS, 1), u32, kind="Internal").ap()
    table = nc.dram_tensor("node_rows", (MP, ROW), fp32, kind="Internal").ap()

    ctx = ExitStack()
    with ctx:
        def sb(name, shape, dt=fp32):
            return ctx.enter_context(nc.sbuf_tensor(name, shape, dt))

        def sem(name):
            return ctx.enter_context(nc.semaphore(name))

        XT = sb("XT", [P, XC])
        X = sb("X", [P, MP])
        HS = sb("HS", [P, B + MP])
        src_ids = sb("src_ids", [P, ET], mybir.dt.uint16)
        dst_lohi = sb("dst_lohi", [P, ET + 8, 2], bf16)
        ranks = sb("ranks", [P, ET])
        rows = sb("rows", [P, NB, ROW])
        adst = sb("adst", [P, NB, HEADS])

        free_at = [NB * C]

        def in_x(*dims):
            n = 1
            for d in dims:
                n *= d
            part = X[:, free_at[0]:free_at[0] + n]
            free_at[0] += n
            assert free_at[0] <= MP
            if len(dims) == 1:
                return part
            letters = "abcd"[:len(dims)]
            return part.rearrange(f"p ({' '.join(letters)}) -> p {' '.join(letters)}",
                                  **dict(zip(letters[1:], dims[1:])))

        acc = in_x(NB, ROW)
        mx = in_x(NB, HEADS)
        G = in_x(2, SLOTS, ROW)
        small4 = in_x(4, NB, EXPERTS)
        gm = in_x(4, NB)

        wr = sb("wr", [P, TAPS // 2, P])
        wi = sb("wi", [P, TAPS // 2, C])
        ph = sb("ph", [P, TAPS // 2])
        trig = sb("trig", [P, 4, TAPS // 2])
        trig_i = sb("trig_i", [P, 2, TAPS // 2], i32)
        inw = sb("inw", [P, H])
        aw, bw, cw, dw = [sb(n, [P, 2, H]) for n in ("aw", "bw", "cw", "dw")]
        cols = sb("cols", [P, 16])
        brow = sb("brow", [1, 2 * H])
        outw = sb("outw", [P, P])
        wgat = sb("wgat", [P, F])
        vecs = sb("vecs", [P, 5, F])
        w1s = sb("w1s", [P, EXPERTS, H])
        w2s = sb("w2s", [P, EXPERTS, C])
        b2row = sb("b2row", [1, EXPERTS * C])

        iota = sb("iota", [P, P], bf16)
        ident = sb("ident", [P, P])
        ident_b = sb("ident_b", [P, P], bf16)
        before = sb("before", [P, P])
        ones_row = sb("ones_row", [1, CH])
        mean64 = sb("mean64", [P, P])
        mean128 = sb("mean128", [P, P])
        eps_col = sb("eps_col", [P, 1])

        onehot = sb("onehot", [P, 8, 2, P], bf16)
        onehot_T = sb("onehot_T", [P, 4, P])
        earlier = sb("earlier", [P, 2, P], bf16)
        counts = sb("counts", [P, 2, P])
        junk = sb("junk", [P, 2, P], bf16)
        rank = sb("rank", [P, TI])
        over = sb("over", [P, GS])
        slot_f = sb("slot_f", [P, GS])
        slot_ix = sb("slot_ix", [P, TI], u32)
        src_st = sb("src_st", [P, TI], u32)

        s_a = sb("s_a", [P, CH])
        s_b = sb("s_b", [P, CH])
        s_c = sb("s_c", [P, CH])
        s_d = sb("s_d", [P, CH])

        EL = sb("EL", [P, 2, SLOTS], u32)
        FILL = HS[:, 2 * ET:2 * ET + MP * SLOTS // P].bitcast(u32)
        CONSTS = 21
        ATT_STEPS = 15
        RG = ET // GS
        MAX_ROUNDS = -(-ET * P // SLOTS)
        window = sb("window", [P, 1])
        degree = sb("degree", [P, 2])
        degrees = sb("degrees", [P, 2, NB])
        block_degree = sb("block_degree", [P, NB], i32)
        PAIR = 2
        rounds_i = sb("rounds_i", [P, 1], i32)
        s_rounds = sem("rounds_known")
        s_deg = sem("degree_ready")
        s_dve_round = sem("vector_round_step")
        s_round_part = sem("round_index_step")
        s_round_empty = sem("round_table_emptied")
        s_round_ix = sem("round_indices_ready")
        s_round_sc = sem("round_scattered")
        s_round_put = sem("round_group_scattered")
        s_round_go = sem("round_block_wanted")
        s_round_el = sem("round_slots_loaded")
        s_round_ga = sem("round_rows_gathered")
        s_round_rows = sem("round_block_gathered")
        s_round_used = sem("round_rows_used")
        past = B + EXPERTS * CH + 4 * NB * F
        pexp, parg = [HS[:, past + k * HEADS * (SLOTS + 1):past + (k + 1) * HEADS * (SLOTS + 1)] for k in range(2)]
        pmask = sb("pmask", [P, SLOTS])
        pe_ = sb("pe_", [P, HEADS, SLOTS])
        small = sb("small", [P, 4, F])
        hid = HS[:, 0:EXPERTS * CH].rearrange("p (e c) -> p e c", e=EXPERTS)
        work = HS[:, B + EXPERTS * CH:B + EXPERTS * CH + 4 * NB * F].rearrange("p (k n f) -> p k n f", k=4, f=F)
        msg = HS[:, 0:F * SLOTS].rearrange("p (h j k) -> p h j k", h=HEADS, k=SLOTS)
        order = sb("order", [P, EXPERTS])

        bank = [ctx.enter_context(nc.psum_tensor(f"bank{k}", [P, 512], fp32)) for k in range(8)]

        IN_B, C_B, D_B, LN_W, LN_B, OUT_B, B1, CD_B = 0, 1, 3, 5, 7, 9, 10, 14
        ATT_S, ATT_D, BGAT, GAMMA, BETA = range(5)

        s_par = sem("params_loaded")
        s_edge = sem("edges_loaded")
        s_x = [sem(f"x_loaded{k}") for k in range(2)]
        s_const = sem("constants_made")
        s_ellfill = sem("ell_filled_sbuf")
        s_ell0 = sem("ell_emptied")
        s_dve = sem("vector_step")
        s_act = sem("scalar_step")
        s_weff = sem("conv_weights_ready")
        s_prep = sem("edges_prepared")

        s_oh = sem("onehot_ready")
        s_tr = sem("onehot_transposed")
        s_te = sem("onehot_T_copied")
        s_pair = sem("pairs_ready")
        s_early = sem("earlier_ready")
        s_rps = sem("rank_products_ready")
        s_cnt = sem("counts_updated")
        s_cc = sem("counts_copied")
        s_rk = sem("ranks_ready")
        s_ix = sem("slot_indices_ready")
        s_sc = [sem(f"scattered{g}") for g in range(GR)]
        s_bx = sem("scan_input_ready")
        s_pre = sem("scan_product_ready")
        s_h = sem("state_ready")
        s_tab = sem("table_stored")
        s_el = [sem(f"slots_loaded{k}") for k in range(2)]
        s_ga = [sem(f"rows_gathered{k}") for k in range(2)]
        s_used = sem("rows_used")
        s_arg = sem("exp_arguments_ready")
        s_exp = sem("exp_ready")
        s_out = sem("out_stored")

        block = ctx.enter_context(nc.Block())

        class Steps:

            def __init__(self, eng, sem):
                self.eng, self.sem, self.n, self.off, self.loops = eng, sem, 0, None, []

            def did(self, ins):
                ins.then_inc(self.sem, 1)
                self.n += 1
                return ins

            def last(self):
                self.eng.wait_ge(self.sem, self.n if self.off is None else self.off + self.n)

            def link(self, ins):
                self.did(ins)
                self.last()

            def enter(self, off, per):
                self.loops.append((self.off, per, self.n))
                self.off = off

            def leave(self, times):
                self.off, per, at = self.loops.pop()
                assert self.n - at == per, (self.n - at, per)
                self.n = at + times * per

        names = {}

        def ev(name):
            if name not in names:
                names[name] = sem(name)
            return names[name]

        for n in ("conv_ready", "y_ready", "s1_mean", "s1_square", "s1_var", "s1_root", "s1_norm", "s1_in",
                  "x1_ready"):
            ev(n)
        for l in range(2):
            for n in ("mix", "sum", "mean", "square", "var", "root", "norm"):
                ev(f"l{l}_{n}")
        for n in ("o_product", "h1_ready", "h1_turned", "h1_kept", "o_mean", "o_square", "o_var", "o_root",
                  "xn_ready", "xn_kept", "gat_product", "gat_kept"):
            ev(n)
        for n in ("hidden_product", "hidden_ready", "expert_product", "expert_used", "gate_ready",
                  "gate_root", "gate_var", "gate_arg", "gate_exp", "out_ready"):
            ev(n)

        NPAR = 26

        @block.sync
        def _(sp):
            sp.dma_start(HS[:, 0:2 * ET].bitcast(i32), edges).then_inc(s_edge, 16)
            sp.dma_start(XT[0:C, :], x_t).then_inc(s_x[0], 16)
            sp.dma_start(XT[C:P, 0:XC - B], x_t[:, B:XC]).then_inc(s_x[1], 16)

            sp.wait_ge(s_ix, 4 * ITERS)
            for g in range(GR):
                sp.wait_ge(s_sc[g], ITERS * GS * 16)
            blocks = ell.rearrange("(b p k) o -> b p (k o)", p=P, k=SLOTS)
            for k in range(2):
                sp.dma_start(EL[:, k, :], blocks[k, :, :]).then_inc(s_el[k], 16)
            with sp.Fori(1, NB // 2) as i:
                for k in range(2):
                    sp.wait_ge(s_used, i * 2 + (k - 1))
                    sp.dma_start(EL[:, k, :], blocks[ds(i * 2 + k, 1), :, :].rearrange("a p k -> (a p) k"))\
                        .then_inc(s_el[k], 16)

            sp.wait_ge(s_rounds, 1)
            rounds = sp.value_load(rounds_i[0:1, 0:1], min_val=0, max_val=MAX_ROUNDS)
            with sp.If(rounds > 1):
                sp.wait_ge(s_used, NB)
                with sp.Fori(1, rounds) as r:
                    with sp.Fori(0, NB) as b:
                        sp.wait_ge(s_round_go, (r - 1) * NB + b + 1)
                        sp.dma_start(EL[:, 0, :], blocks[ds(b, 1), :, :].rearrange("a p k -> (a p) k"))\
                          .then_inc(s_round_el, 16)

            sp.wait_ge(ev("out_ready"), NC)
            h1 = X[:, 0:NB * C].rearrange("p (n c) -> p n c", c=C)
            for tl in range(8):
                n = len(range(tl, T, 8))
                sp.dma_start(out[:, tl:T:8, :], h1[B * tl:B * tl + B, 0:n, :]).then_inc(s_out, 16)
            sp.wait_ge(s_out, 8 * 16)


        @block.gpsimd
        def _(pool):
            link = Steps(pool, s_const)
            link.did(pool.memset(FILL, EMPTY))
            link.last()
            pool.dma_start(ell.rearrange("(p n) o -> p (n o)", p=P), FILL).then_inc(s_ell0, 16)
            link.last()
            link.link(pool.memset(XT[C:P, XC - B:XC], 0.0))
            link.did(pool.memset(ident[:, :], 0.0))
            link.did(pool.memset(before[:, :], 1.0))
            link.did(pool.memset(ones_row[:, :], 1.0))
            link.did(pool.memset(mean64[:, :], 0.0))
            link.did(pool.memset(wr[:, :, C:P], 0.0))
            link.did(pool.memset(outw[:, C:P], 0.0))
            link.did(pool.memset(cols[:, OUT_B:OUT_B + 1], 0.0))
            link.last()
            link.link(pool.memset(mean64[0:C, 0:C], 1.0 / C))
            link.link(pool.memset(inw[C:P, :], 0.0))
            link.link(pool.memset(wgat[C:P, :], 0.0))
            link.link(pool.memset(w1s[C:P, :, :], 0.0))
            link.did(pool.memset(mean128[:, :], 1.0 / H))
            link.did(pool.memset(eps_col[:, :], EPS))
            link.did(pool.memset(dst_lohi[:, ET:ET + 8, :], 200.0))
            link.did(pool.iota(iota[:, :], [[1, P]], base=0, channel_multiplier=0,
                               allow_small_or_imprecise_dtypes=True))
            link.last()
            link.did(pool.affine_select(out=ident[:, :], in_=ident[:, :], compare_op=ALU.not_equal, fill=1.0,
                                        base=0, pattern=[[-1, P]], channel_multiplier=1))
            link.did(pool.affine_select(out=before[:, :], in_=before[:, :], compare_op=ALU.is_gt, fill=0.0,
                                        base=0, pattern=[[1, P]], channel_multiplier=-1))
            link.last()
            link.did(pool.tensor_copy(ident_b[:, :], ident[:, :]))
            link.did(pool.memset(s_d[:, :], 0.0))

            none = pool.alloc_register("none")
            last_slot = pool.alloc_register("last_slot")
            last_row = pool.alloc_register("last_row")
            pool.reg_mov(none, 0)
            pool.wait_ge(s_ell0, 16)
            with pool.Fori(0, ITERS) as i:
                for g in range(GR):
                    pool.wait_ge(s_ix, i * GR + (g + 1))
                    pool.reg_add(last_slot, none, MP * SLOTS - 1)
                    for u in range(g * GS, g * GS + GS):
                        pool.indirect_dma_start(ell, bass.IndirectOffsetOnAxis(ap=slot_ix[:, u:u + 1], axis=0),
                                                src_st[:, u:u + 1], None, bounds_check=last_slot,
                                                oob_is_err=False).then_inc(s_sc[g], 16)

            pool.wait_ge(s_deg, 1)
            pool.partition_all_reduce(degrees[:, 1, :], degrees[:, 0, :], P, bass.bass_isa.ReduceOp.max).then_inc(s_deg, 1)
            pool.wait_ge(s_rounds, 1)
            pool.wait_ge(ev("gat_kept"), NC + 1)
            link.did(pool.memset(G[:, :, :, :], 0.0))
            link.last()
            pool.wait_ge(s_tab, 16)

            def gather(b, k, done):
                filled = pool.value_load(block_degree[0:1, ds(b, 1)], min_val=0, max_val=ET * P)
                for s0 in range(0, SLOTS, PAIR):
                    with pool.If(filled > s0):
                        for s in range(s0, s0 + PAIR):
                            pool.indirect_dma_start(G[:, k, s, :], None, table,
                                                    bass.IndirectOffsetOnAxis(ap=EL[:, k, s:s + 1], axis=0),
                                                    bounds_check=last_row, oob_is_err=False).then_inc(done, 16)
                    with pool.Else():
                        pool.inc_swdge_sem([done], [16 * PAIR], mode="add")

            pool.reg_add(last_row, none, MP - 1)
            for k in range(2):
                pool.wait_ge(s_el[k], 16)
                gather(k, k, s_ga[k])
            with pool.Fori(1, NB // 2) as i:
                for k in range(2):
                    pool.wait_ge(s_el[k], i * 16 + 16)
                    pool.reg_add(last_row, none, MP - 1)
                    gather(i * 2 + k, k, s_ga[k])

            pool.wait_ge(s_rounds, 1)
            rounds = pool.value_load(rounds_i[0:1, 0:1], min_val=0, max_val=MAX_ROUNDS)
            with pool.If(rounds > 1):
                for k in range(2):
                    pool.wait_ge(s_ga[k], NB // 2 * 16 * SLOTS)
                link.link(pool.memset(FILL, EMPTY))
                with pool.Fori(1, rounds) as r:
                    pool.dma_start(ell.rearrange("(p n) o -> p (n o)", p=P), FILL).then_inc(s_round_empty, 16)
                    pool.wait_ge(s_round_empty, 16)
                    pool.inc_swdge_sem([s_round_empty], [16], mode="sub")
                    with pool.Fori(0, RG) as g:
                        pool.wait_ge(s_round_ix, (r - 1) * RG + g + 1)
                        pool.reg_add(last_slot, none, MP * SLOTS - 1)
                        for u in range(GS):
                            pool.indirect_dma_start(ell, bass.IndirectOffsetOnAxis(ap=slot_ix[:, u:u + 1], axis=0),
                                                    src_st[:, u:u + 1], None, bounds_check=last_slot,
                                                    oob_is_err=False).then_inc(s_round_sc, 16)
                        pool.wait_ge(s_round_sc, GS * 16)
                        pool.inc_swdge_sem([s_round_sc], [GS * 16], mode="sub")
                        pool.sem_inc(s_round_put, 1)
                    with pool.Fori(0, NB) as b:
                        pool.wait_ge(s_round_used, (r - 1) * NB + b)
                        pool.sem_inc(s_round_go, 1)
                        pool.wait_ge(s_round_el, ((r - 1) * NB + b + 1) * 16)
                        pool.reg_add(last_row, none, MP - 1)
                        for s in range(SLOTS):
                            pool.indirect_dma_start(G[:, 0, s, :], None, table,
                                                    bass.IndirectOffsetOnAxis(ap=EL[:, 0, s:s + 1], axis=0),
                                                    bounds_check=last_row, oob_is_err=False)\
                                .then_inc(s_round_ga, 16)
                        pool.wait_ge(s_round_ga, SLOTS * 16)
                        pool.inc_swdge_sem([s_round_ga], [SLOTS * 16], mode="sub")
                        pool.sem_inc(s_round_rows, 1)

        @block.scalar
        def _(act):
            def col(v):
                return v.rearrange("(n o) -> n o", o=1)

            def bc(v, n):
                return v.rearrange("(o n) -> o n", o=1).to_broadcast([n, v.shape[0]])

            loads = [(wr[:, :, 0:C], conv_wr), (wi[:, :, :], conv_wi), (ph[:, :], phases), (inw[0:C, :], in_w),
                     (cols[:, IN_B:IN_B + 1], col(in_b)), (outw[:, 0:C], out_w), 
                     (wgat[0:C, :], w_gat), (brow[:, :], b_b), (b2row[:, :], b2),
                     (cols[:, C_B:C_B + 2], c_b), (cols[:, D_B:D_B + 2], d_b), (cols[:, LN_W:LN_W + 2], ln_w),
                     (cols[:, LN_B:LN_B + 2], ln_b), (cols[:, B1:B1 + 4], b1),
                     (w1s[0:C, :, :], w1), (w2s[:, :, :], w2),
                     (aw[:, :, :], a_w), (bw[:, :, :], b_w), (cw[:, :, :], c_w), (dw[:, :, :], d_w),
                     (vecs[:, ATT_S, :], bc(att_src, P)), (vecs[:, ATT_D, :], bc(att_dst, P)),
                     (vecs[:, BGAT, :], bc(b_gat, P)), (vecs[:, GAMMA, :], bc(gamma, P)),
                     (vecs[:, BETA, :], bc(beta, P))]
            assert len(loads) == NPAR - 1
            for dst, src in loads:
                act.dma_start(dst, src).then_inc(s_par, 16)
            act.wait_ge(s_const, CONSTS)
            act.dma_start(cols[0:C, OUT_B:OUT_B + 1], col(out_b)).then_inc(s_par, 16)
            act.wait_ge(s_weff, 1)
            act.activation(trig[:, 0:2, :], trig[:, 2:4, :], ACT.Sin).then_inc(s_weff, 1)

            act.wait_ge(s_const, CONSTS)
            def s1(c):
                act.wait_ge(ev("conv_ready"), c + 1)
                act.activation(XT[:, ds(c * CH, CH)], bank[5][:, :], ACT.Copy).then_inc(ev("y_ready"), 1)
                act.wait_ge(ev("s1_var"), c + 1)
                act.activation(s_c[:, :], bank[7][:, :], ACT.Sqrt, bias=eps_col[:, :]).then_inc(ev("s1_root"), 1)
                act.wait_ge(ev("s1_in"), c + 1)
                act.activation(X[:, ds(c * CH, CH)], bank[0][:, :], ACT.Identity, bias=cols[:, IN_B:IN_B + 1])\
                    .then_inc(ev("x1_ready"), 1)
            act.wait_ge(s_prep, 1)
            with act.Fori(0, NC) as c:
                s1(c)

            def onehot_copy(k):
                act.activation(onehot_T[:, k % 4, :], bank[2 + k % 2][:, :].bitcast(bf16)[:, 0:P],
                               ACT.Copy).then_inc(s_te, 1)

            def count_copy(k):
                act.activation(counts[:, k % 2, :], bank[1][:, 0:P], ACT.Copy).then_inc(s_cc, 1)

            for l in range(2):
                if l == 0:
                    act.wait_ge(s_cnt, 1)
                    count_copy(0)
                    for k in range(2):
                        act.wait_ge(s_tr, k + 1)
                        onehot_copy(k)
                with act.Fori(l * 32, l * 32 + 32) as i:
                    col0 = act.snap(i * SC + (B - l * MP))
                    for j in range(TI):
                        if j < STEPS:
                            act.wait_ge(s_pre, i * STEPS + (j + 1))
                            act.activation(HS[:, ds(col0 + j * B, B)], bank[0][:, j * B:j * B + B], ACT.Tanh)\
                               .then_inc(s_h, 1)
                        act.wait_ge(s_tr, i * TI + (j + 3))
                        onehot_copy(j + 2)
                        act.wait_ge(s_cnt, i * TI + (j + 2))
                        count_copy(j + 1)
                def root(c):
                    act.wait_ge(ev(f"l{l}_var"), c + 1)
                    act.activation(s_c[:, :], bank[7][:, :], ACT.Sqrt, bias=eps_col[:, :])\
                       .then_inc(ev(f"l{l}_root"), 1)
                with act.Fori(0, NC) as c:
                    root(c)
                    if l == 1:
                        act.wait_ge(ev("h1_turned"), c + 1)
                        act.activation(X[:, ds(c * (4 * C), 4 * C)].rearrange("p (q c) -> p q c", q=4),
                                       bank[5][:, :].rearrange("p (q c) -> p q c", q=4)[:, :, 0:C], ACT.Copy)\
                           .then_inc(ev("h1_kept"), 1)
                        act.wait_ge(ev("o_var"), c + 1)
                        act.activation(s_c[:, :], bank[7][:, :], ACT.Sqrt, bias=eps_col[:, :])\
                           .then_inc(ev("o_root"), 1)
                        act.wait_ge(ev("xn_ready"), c + 1)
                        act.activation(XT[:, ds(c * CH, CH)], s_d[:, :], ACT.Copy).then_inc(ev("xn_kept"), 1)

            act.wait_ge(ev("gat_kept"), NC + 1)
            act.dma_start(table.rearrange("(b p) f -> p b f", p=P), rows[:, :, :]).then_inc(s_tab, 16)

            with act.Fori(0, NB) as b:
                act.wait_ge(s_arg, b + 1)
                act.activation(pexp[:, :], parg[:, :], ACT.Exp).then_inc(s_exp, 1)

            act.wait_ge(s_rounds, 1)
            rounds = act.value_load(rounds_i[0:1, 0:1], min_val=0, max_val=MAX_ROUNDS)
            with act.If(rounds > 1):
                with act.Fori(1, rounds) as r:
                    with act.Fori(0, NB) as b:
                        act.wait_ge(s_arg, r * NB + b + 1)
                        act.activation(pexp[:, :], parg[:, :], ACT.Exp).then_inc(s_exp, 1)

            act.wait_ge(ev("gate_var"), 1)
            act.activation(gm[:, 1, :], gm[:, 0, :], ACT.Sqrt, bias=eps_col[:, :]).then_inc(ev("gate_root"), 1)
            act.wait_ge(ev("gate_arg"), 1)
            act.activation(gm[:, 1, :], gm[:, 0, :], ACT.Exp).then_inc(ev("gate_exp"), 1)

            with act.Fori(0, NC) as c:
                for e in range(EXPERTS):
                    act.wait_ge(ev("hidden_product"), c * EXPERTS + (e + 1))
                    act.activation(hid[:, e, :], bank[e][:, :], ACT.Gelu, bias=cols[:, B1 + e:B1 + e + 1])\
                       .then_inc(ev("hidden_ready"), 1)


        @block.vector
        def _(dve):
            me = Steps(dve, s_dve)
            link, did = me.link, me.did

            TAU = 6.283185307179586
            dve.wait_ge(s_par, 16 * NPAR)
            did(dve.tensor_scalar(trig[:, 0, :], ph[:, :], TAU / 4, None, ALU.add))
            link(dve.tensor_copy(trig[:, 1, :], ph[:, :]))
            link(dve.tensor_scalar(trig_i[:, :, :], trig[:, 0:2, :], 1 / TAU, None, ALU.mult))
            link(dve.tensor_copy(trig[:, 2:4, :], trig_i[:, :, :]))
            link(dve.scalar_tensor_tensor(out=trig[:, 2:4, :], in0=trig[:, 2:4, :], scalar=-TAU,
                                          in1=trig[:, 0:2, :], op0=ALU.mult, op1=ALU.add))
            for side, op in ((-TAU, ALU.is_gt), (TAU, ALU.is_lt)):
                link(dve.tensor_scalar(trig[:, 0:2, :], trig[:, 2:4, :], -side / 2, side, op, ALU.mult))
                link(dve.tensor_tensor(out=trig[:, 2:4, :], in0=trig[:, 2:4, :], in1=trig[:, 0:2, :], op=ALU.add))
            link(dve.tensor_scalar(trig[:, 2:4, :], trig[:, 2:4, :], 3.1415925, -3.1415925, ALU.min, ALU.max))
            dve.tensor_tensor(out=cols[:, CD_B:CD_B + 2], in0=cols[:, C_B:C_B + 2], in1=cols[:, D_B:D_B + 2],
                              op=ALU.add).then_inc(s_weff, 1)
            dve.wait_ge(s_weff, 2)
            cos = trig[:, 0, :].unsqueeze(2).to_broadcast([P, TAPS // 2, C])
            sin = trig[:, 1, :].unsqueeze(2).to_broadcast([P, TAPS // 2, C])
            did(dve.tensor_tensor(out=wr[:, :, 0:C], in0=wr[:, :, 0:C], in1=cos, op=ALU.mult))
            link(dve.tensor_tensor(out=wi[:, :, :], in0=wi[:, :, :], in1=sin, op=ALU.mult))
            dve.tensor_tensor(out=wr[:, :, 0:C], in0=wr[:, :, 0:C], in1=wi[:, :, :], op=ALU.subtract).then_inc(s_weff, 1)

            dve.wait_ge(s_edge, 16)
            Nn, Q, R, Z = [X[:, k * ET:(k + 1) * ET] for k in range(4)]
            QI = X[:, 4 * ET:5 * ET].bitcast(i32)

            def divide(n, by, half):
                link(dve.tensor_scalar(QI, n, half, 1.0 / by, ALU.add, ALU.mult))
                link(dve.tensor_copy(Q, QI))
                link(dve.scalar_tensor_tensor(out=R, in0=Q, scalar=-float(by), in1=n, op0=ALU.mult, op1=ALU.add))
                link(dve.tensor_scalar(Z, R, 0.0, None, ALU.is_lt))
                did(dve.tensor_tensor(out=Q, in0=Q, in1=Z, op=ALU.subtract))
                link(dve.scalar_tensor_tensor(out=R, in0=Z, scalar=float(by), in1=R, op0=ALU.mult, op1=ALU.add))

            for side in range(2):
                ids = HS[:, side * ET:(side + 1) * ET].bitcast(i32)
                link(dve.tensor_copy(Nn, ids))
                if side == 0:
                    link(dve.tensor_scalar(Nn, Nn, float(M - 1), None, ALU.min))
                divide(Nn, T, 0.25)
                link(dve.scalar_tensor_tensor(out=R, in0=R, scalar=float(B), in1=Q, op0=ALU.mult, op1=ALU.add))
                if side == 0:
                    link(dve.tensor_copy(src_ids[:, :], R))
            link(dve.tensor_scalar(Z, Nn, float(M), 16384.0, ALU.is_ge, ALU.mult))
            link(dve.tensor_tensor(out=Nn, in0=R, in1=Z, op=ALU.add))
            divide(Nn, P, 0.5)
            link(dve.tensor_copy(dst_lohi[:, 0:ET, 0], R))
            did(dve.tensor_copy(dst_lohi[:, 0:ET, 1], Q))
            me.last()
            dve.memset(HS[:, 0:B], 0.0).then_inc(s_prep, 1)

            dve.wait_ge(s_const, CONSTS)
            with dve.Fori(0, NC) as c:
                me.enter(c * 2, 2)
                dve.wait_ge(ev("y_ready"), c + 1)
                dve.wait_ge(ev("s1_mean"), c + 1)
                link(dve.tensor_tensor(out=s_a[:, :], in0=XT[:, ds(c * CH, CH)], in1=bank[6][:, :],
                                       op=ALU.subtract))
                dve.tensor_tensor(out=s_b[:, :], in0=s_a[:, :], in1=s_a[:, :], op=ALU.mult)\
                   .then_inc(ev("s1_square"), 1)
                dve.wait_ge(ev("s1_root"), c + 1)
                link(dve.reciprocal(s_c[:, :], s_c[:, :]))
                dve.tensor_tensor(out=s_b[:, :], in0=s_a[:, :], in1=s_c[:, :], op=ALU.mult)\
                   .then_inc(ev("s1_norm"), 1)
            me.leave(NC)

            def make_onehot(t, k):
                dve.tensor_tensor(out=onehot[:, k % 8, :, :],
                                  in0=iota[:, :].unsqueeze(1).to_broadcast([P, 2, P]),
                                  in1=dst_lohi[:, ds(t, 1), :].rearrange("p a b -> p (a b)").unsqueeze(2)
                                  .to_broadcast([P, 2, P]), op=ALU.is_equal).then_inc(s_oh, 1)

            def keep_earlier(k):
                dve.tensor_tensor(out=earlier[:, k % 2, :], in0=bank[4 + k % 2][:, 0:P],
                                  in1=before[:, :], op=ALU.mult).then_inc(s_early, 1)

            for l in range(2):
                if l == 0:
                    for k in range(3):
                        make_onehot(k, k)
                    dve.wait_ge(s_pair, 1)
                    keep_earlier(0)
                with dve.Fori(l * 32, l * 32 + 32) as i:
                    me.enter((i - l * 32) * (4 * GR + 1), 4 * GR + 1)
                    for j in range(TI):
                        dve.wait_ge(s_cnt, i * TI + (j + 1))
                        make_onehot(i * TI + (j + 3), j + 3)
                        dve.wait_ge(s_pair, i * TI + (j + 2))
                        keep_earlier(j + 1)
                        dve.wait_ge(s_rps, i * TI + (j + 1))
                        dve.tensor_tensor_reduce(out=junk[:, j % 2, :], in0=bank[6 + j % 2][:, 0:P],
                                                 in1=onehot[:, j % 8, 1, :], scale=1.0, scalar=0.0,
                                                 op0=ALU.mult, op1=ALU.add, accum_out=rank[:, j:j + 1])\
                           .then_inc(s_rk, 1)
                        if j % GS == GS - 1:
                            g = j // GS
                            part = slice(g * GS, g * GS + GS)
                            dve.wait_ge(s_rk, i * TI + (j + 1))
                            dve.wait_ge(s_sc[g], i * (GS * 16))
                            did(dve.tensor_scalar(over[:, :], rank[:, part], float(SLOTS), FAR, ALU.is_ge, ALU.mult))
                            lohi = dst_lohi[:, ds(i * TI + g * GS, GS), :]
                            link(dve.scalar_tensor_tensor(out=slot_f[:, :], in0=lohi[:, :, 1], scalar=float(P),
                                                          in1=lohi[:, :, 0], op0=ALU.mult, op1=ALU.add))
                            did(dve.scalar_tensor_tensor(out=slot_f[:, :], in0=slot_f[:, :],
                                                         scalar=float(SLOTS), in1=rank[:, part],
                                                         op0=ALU.mult, op1=ALU.add))
                            link(dve.tensor_scalar(src_st[:, part], src_ids[:, ds(i * TI + g * GS, GS)], 1.0, None, ALU.mult))
                            dve.tensor_tensor(out=slot_ix[:, part], in0=slot_f[:, :], in1=over[:, :], op=ALU.add)\
                               .then_inc(s_ix, 1)
                    link(dve.tensor_scalar(ranks[:, ds(i * TI, TI)], rank[:, :], 1.0, None, ALU.mult))
                me.leave(32)

                with dve.Fori(0, NC) as c:
                    me.enter(c * (3 if l == 0 else 8), 3 if l == 0 else 8)
                    chunk = X[:, ds(c * CH, CH)]
                    dve.wait_ge(ev(f"l{l}_mix"), c + 1)
                    dve.scalar_tensor_tensor(out=s_b[:, :], in0=bank[0][:, :], scalar=cols[:, CD_B + l:CD_B + l + 1],
                                             in1=chunk, op0=ALU.add, op1=ALU.add).then_inc(ev(f"l{l}_sum"), 1)
                    dve.wait_ge(ev(f"l{l}_mean"), c + 1)
                    link(dve.tensor_tensor(out=s_a[:, :], in0=s_b[:, :], in1=bank[6][:, :], op=ALU.subtract))
                    dve.tensor_tensor(out=s_b[:, :], in0=s_a[:, :], in1=s_a[:, :], op=ALU.mult)\
                       .then_inc(ev(f"l{l}_square"), 1)
                    dve.wait_ge(ev(f"l{l}_root"), c + 1)
                    link(dve.reciprocal(s_c[:, :], s_c[:, :]))
                    link(dve.tensor_tensor(out=s_a[:, :], in0=s_a[:, :], in1=s_c[:, :], op=ALU.mult))
                    dve.tensor_scalar(chunk, s_a[:, :], cols[:, LN_W + l:LN_W + l + 1],
                                      cols[:, LN_B + l:LN_B + l + 1], ALU.mult, ALU.add)\
                       .then_inc(ev(f"l{l}_norm"), 1)
                    if l == 1:
                        y = XT[:, ds(c * CH, CH)]
                        dve.wait_ge(ev("o_product"), c + 1)
                        dve.scalar_tensor_tensor(out=s_b[:, :], in0=bank[0][:, :],
                                                 scalar=cols[:, OUT_B:OUT_B + 1], in1=y,
                                                 op0=ALU.add, op1=ALU.add).then_inc(ev("h1_ready"), 1)
                        dve.wait_ge(ev("o_mean"), c + 1)
                        link(dve.tensor_tensor(out=s_a[:, :], in0=s_b[:, :], in1=bank[6][:, :],
                                               op=ALU.subtract))
                        dve.wait_ge(ev("h1_turned"), c + 1)
                        dve.tensor_tensor(out=s_b[:, :], in0=s_a[:, :], in1=s_a[:, :], op=ALU.mult)\
                           .then_inc(ev("o_square"), 1)
                        dve.wait_ge(ev("o_root"), c + 1)
                        link(dve.reciprocal(s_c[:, :], s_c[:, :]))
                        dve.tensor_tensor(out=s_d[:, :], in0=s_a[:, :], in1=s_c[:, :], op=ALU.mult)\
                           .then_inc(ev("xn_ready"), 1)
                        dve.wait_ge(ev("gat_product"), c + 1)
                        for q in range(3):
                            did(dve.tensor_scalar(rows[:, ds(c * 4 + q, 1), HEADS:ROW].rearrange("p a f -> p (a f)"),
                                                  bank[4][:, q * F:(q + 1) * F], 1.0, None, ALU.mult))
                        dve.tensor_scalar(rows[:, ds(c * 4 + 3, 1), HEADS:ROW].rearrange("p a f -> p (a f)"),
                                          bank[4][:, 3 * F:4 * F], 1.0, None, ALU.mult).then_inc(ev("gat_kept"), 1)
                        dve.wait_ge(ev("xn_kept"), c + 1)
                me.leave(NC)

            did(dve.memset(window[:, :], 0.0))
            dve.tensor_copy(degrees[:, 0, :], bank[1][:, 0:NB]).then_inc(s_deg, 1)
            dve.wait_ge(s_deg, 2)
            did(dve.tensor_copy(block_degree[:, :], degrees[:, 1, :]))
            link(dve.tensor_reduce(out=degree[:, 0:1], in_=degrees[:, 1, :], axis=AX.X, op=ALU.max))
            link(dve.tensor_scalar(degree[:, 0:1], degree[:, 0:1], -1.0, None, ALU.add))
            link(dve.tensor_scalar(rounds_i[:, :], degree[:, 0:1], 0.5, 1.0 / SLOTS, ALU.add, ALU.mult))
            link(dve.tensor_copy(degree[:, 1:2], rounds_i[:, :]))
            link(dve.scalar_tensor_tensor(out=degree[:, 0:1], in0=degree[:, 1:2], scalar=-float(SLOTS),
                                          in1=degree[:, 0:1], op0=ALU.mult, op1=ALU.add))
            link(dve.tensor_scalar(degree[:, 0:1], degree[:, 0:1], 0.0, None, ALU.is_ge))
            dve.tensor_tensor(out=rounds_i[:, :], in0=degree[:, 1:2], in1=degree[:, 0:1], op=ALU.add)\
               .then_inc(s_rounds, 1)
            dve.wait_ge(s_rounds, 1)

            dve.wait_ge(ev("gat_kept"), NC)
            hh = rows[:, :, HEADS:ROW]

            def all_nodes(v):
                return vecs[:, v, :].unsqueeze(1).to_broadcast([P, NB, F])

            def per_head(a):
                return a.rearrange("p n (h j) -> p n h j", h=HEADS)

            me.last()
            did(dve.tensor_tensor(out=work[:, 0], in0=hh, in1=all_nodes(ATT_S), op=ALU.mult))
            link(dve.tensor_tensor(out=work[:, 1], in0=hh, in1=all_nodes(ATT_D), op=ALU.mult))
            did(dve.tensor_reduce(out=rows[:, :, 0:HEADS], in_=per_head(work[:, 0]), axis=AX.X, op=ALU.add))
            link(dve.tensor_reduce(out=adst[:, :, :], in_=per_head(work[:, 1]), axis=AX.X, op=ALU.add))
            did(dve.tensor_copy(acc[:, :, HEADS:ROW], hh))
            did(dve.memset(acc[:, :, 0:HEADS], 1.0))
            dve.tensor_tensor(out=mx[:, :, :], in0=rows[:, :, 0:HEADS], in1=adst[:, :, :], op=ALU.add)\
               .then_inc(ev("gat_kept"), 1)
            dve.wait_ge(ev("gat_kept"), NC + 1)
            link(dve.scalar_tensor_tensor(out=mx[:, :, :], in0=mx[:, :, :], scalar=0.2, in1=mx[:, :, :],
                                          op0=ALU.mult, op1=ALU.max))

            HK = HEADS * SLOTS

            def attend(me, b, k, nth):
                did, link = me.did, me.link
                a_d = adst[:, ds(b, 1), :].rearrange("p a h -> p (a h)")
                m_b = mx[:, ds(b, 1), :].rearrange("p a h -> p (a h)")
                den = acc[:, ds(b, 1), 0:HEADS].rearrange("p a h -> p (a h)")
                num = acc[:, ds(b, 1), HEADS:ROW].rearrange("p a f -> p (a f)")
                arg = parg[:, 0:HK].rearrange("p (h k) -> p h k", h=HEADS)
                m_new, s_den, s_num = small[:, 0, 0:HEADS], small[:, 1, 0:HEADS], small[:, 2, :]
                did(dve.tensor_scalar(pmask[:, :], EL[:, k, :], float(MP), NONE, ALU.is_ge, ALU.mult))
                link(dve.tensor_tensor(out=pe_[:, :, :], in0=G[:, k, :, 0:HEADS].rearrange("p k h -> p h k"),
                                       in1=a_d.unsqueeze(2).to_broadcast([P, HEADS, SLOTS]), op=ALU.add))
                link(dve.scalar_tensor_tensor(out=pe_[:, :, :], in0=pe_[:, :, :], scalar=0.2,
                                              in1=pe_[:, :, :], op0=ALU.mult, op1=ALU.max))
                link(dve.tensor_tensor(out=pe_[:, :, :], in0=pe_[:, :, :],
                                       in1=pmask[:, :].unsqueeze(1).to_broadcast([P, HEADS, SLOTS]),
                                       op=ALU.add))
                link(dve.tensor_reduce(out=small[:, 3, 0:HEADS], in_=pe_[:, :, :], axis=AX.X, op=ALU.max))
                link(dve.tensor_tensor(out=m_new, in0=small[:, 3, 0:HEADS], in1=m_b, op=ALU.max))
                did(dve.tensor_tensor(out=arg, in0=pe_[:, :, :],
                                      in1=m_new.unsqueeze(2).to_broadcast([P, HEADS, SLOTS]),
                                      op=ALU.subtract))
                dve.tensor_tensor(out=parg[:, HK:HK + HEADS], in0=m_b, in1=m_new, op=ALU.subtract)\
                   .then_inc(s_arg, 1)
                dve.wait_ge(s_arg, nth)
                did(dve.tensor_scalar(m_b, m_new, 1.0, None, ALU.mult))
                dve.wait_ge(s_exp, nth)
                pk = pexp[:, 0:HK].rearrange("p (h k) -> p h k", h=HEADS)
                old = pexp[:, HK:HK + HEADS]
                did(dve.tensor_tensor(out=msg.rearrange("p h j k -> p h j k"),
                                      in0=G[:, k, :, HEADS:ROW].rearrange("p k (h j) -> p h j k", h=HEADS),
                                      in1=pk.unsqueeze(2).to_broadcast([P, HEADS, EXPERTS, SLOTS]),
                                      op=ALU.mult))
                did(dve.tensor_reduce(out=s_den, in_=pk, axis=AX.X, op=ALU.add))
                did(dve.tensor_tensor(out=den, in0=den, in1=old, op=ALU.mult))
                did(dve.tensor_tensor(out=num.rearrange("p (h j) -> p h j", h=HEADS),
                                      in0=num.rearrange("p (h j) -> p h j", h=HEADS),
                                      in1=old.unsqueeze(2).to_broadcast([P, HEADS, EXPERTS]), op=ALU.mult))
                me.last()
                did(dve.tensor_reduce(out=s_num, in_=HS[:, 0:F * SLOTS].rearrange("p (f k) -> p f k", k=SLOTS),
                                      axis=AX.X, op=ALU.add))
                link(dve.tensor_tensor(out=den, in0=den, in1=s_den, op=ALU.add))
                me.did(dve.tensor_tensor(out=num, in0=num, in1=s_num, op=ALU.add))
                me.last()

            with dve.Fori(0, NB // 2) as i:
                me.enter(i * (2 * ATT_STEPS), 2 * ATT_STEPS)
                for k in range(2):
                    dve.wait_ge(s_ga[k], i * (16 * SLOTS) + 16 * SLOTS)
                    attend(me, i * 2 + k, k, i * 2 + (k + 1))
                    dve.tensor_copy(order[:, 0:1], small[:, 0, 0:1]).then_inc(s_used, 1)
            me.leave(NB // 2)

            rounds = dve.value_load(rounds_i[0:1, 0:1], min_val=0, max_val=MAX_ROUNDS)
            with dve.If(rounds > 1):
                again = Steps(dve, s_dve_round)
                with dve.Fori(1, rounds) as r:
                    per_round = 1 + RG * 5 + NB * ATT_STEPS
                    again.enter((r - 1) * per_round, per_round)
                    again.did(dve.tensor_scalar(window[:, :], window[:, :], float(SLOTS), None, ALU.add))
                    with dve.Fori(0, RG) as g:
                        again.enter((r - 1) * per_round + g * 5, 5)
                        lohi = dst_lohi[:, ds(g * GS, GS), :]
                        dve.wait_ge(s_dve_round, (r - 1) * per_round + 1)
                        dve.wait_ge(s_round_put, (r - 1) * RG + g)
                        again.did(dve.tensor_scalar(src_st[:, 0:GS], src_ids[:, ds(g * GS, GS)], 1.0, None, ALU.mult))
                        again.did(dve.scalar_tensor_tensor(out=slot_f[:, :], in0=lohi[:, :, 1], scalar=float(P),
                                                           in1=lohi[:, :, 0], op0=ALU.mult, op1=ALU.add))
                        again.link(dve.tensor_scalar(rank[:, 0:GS], ranks[:, ds(g * GS, GS)], window[:, 0:1], None,
                                                     ALU.subtract))
                        again.did(dve.tensor_scalar(over[:, :], rank[:, 0:GS], float(SLOTS), FAR, ALU.is_ge,
                                                    ALU.mult))
                        dve.tensor_scalar(rank[:, GS:2 * GS], rank[:, 0:GS], 0.0, FAR, ALU.is_lt, ALU.mult)\
                           .then_inc(s_round_part, 1)
                        dve.wait_ge(s_round_part, ((r - 1) * RG + g) * 3 + 1)
                        again.link(dve.tensor_tensor(out=over[:, :], in0=over[:, :], in1=rank[:, GS:2 * GS],
                                                     op=ALU.max))
                        dve.scalar_tensor_tensor(out=slot_f[:, :], in0=slot_f[:, :], scalar=float(SLOTS),
                                                 in1=rank[:, 0:GS], op0=ALU.mult, op1=ALU.add)\
                           .then_inc(s_round_part, 1)
                        dve.wait_ge(s_round_part, ((r - 1) * RG + g) * 3 + 2)
                        dve.tensor_scalar(slot_f[:, :], slot_f[:, :], -FAR / 2, FAR - 1, ALU.max, ALU.min)\
                           .then_inc(s_round_part, 1)
                        dve.wait_ge(s_round_part, ((r - 1) * RG + g) * 3 + 3)
                        dve.tensor_tensor(out=slot_ix[:, 0:GS], in0=slot_f[:, :], in1=over[:, :], op=ALU.add)\
                           .then_inc(s_round_ix, 1)
                    again.leave(RG)
                    with dve.Fori(0, NB) as b:
                        again.enter((r - 1) * per_round + b * ATT_STEPS, ATT_STEPS)
                        dve.wait_ge(s_round_rows, (r - 1) * NB + b + 1)
                        attend(again, b, 0, r * NB + b + 1)
                        dve.tensor_copy(order[:, 0:1], small[:, 0, 0:1]).then_inc(s_round_used, 1)
                    again.leave(NB)
                    again.leave(1)


            W = [work[:, k] for k in range(4)]
            den_all = acc[:, :, 0:HEADS]
            sc4 = small4
            link(dve.tensor_scalar(sc4[:, 0], den_all, 1e-16, None, ALU.add))
            link(dve.reciprocal(sc4[:, 0], sc4[:, 0]))
            link(dve.tensor_tensor(out=per_head(W[0]), in0=per_head(acc[:, :, HEADS:ROW]),
                                   in1=sc4[:, 0].unsqueeze(3).to_broadcast([P, NB, HEADS, EXPERTS]), op=ALU.mult))
            link(dve.tensor_tensor(out=W[0], in0=W[0], in1=all_nodes(BGAT), op=ALU.add))
            link(dve.tensor_reduce(out=gm[:, 0, :], in_=W[0], axis=AX.X, op=ALU.add))
            link(dve.tensor_scalar(gm[:, 0, :], gm[:, 0, :], 1.0 / F, None, ALU.mult))
            link(dve.tensor_tensor(out=W[0], in0=W[0], in1=gm[:, 0, :].unsqueeze(2).to_broadcast([P, NB, F]),
                                   op=ALU.subtract))
            link(dve.tensor_tensor(out=W[1], in0=W[0], in1=W[0], op=ALU.mult))
            link(dve.tensor_reduce(out=gm[:, 0, :], in_=W[1], axis=AX.X, op=ALU.add))
            dve.tensor_scalar(gm[:, 0, :], gm[:, 0, :], 1.0 / F, None, ALU.mult).then_inc(ev("gate_var"), 1)
            dve.wait_ge(ev("gate_root"), 1)
            link(dve.reciprocal(gm[:, 2, :], gm[:, 1, :]))
            link(dve.tensor_tensor(out=W[0], in0=W[0], in1=gm[:, 2, :].unsqueeze(2).to_broadcast([P, NB, F]),
                                   op=ALU.mult))
            link(dve.tensor_tensor(out=W[0], in0=W[0], in1=all_nodes(GAMMA), op=ALU.mult))
            link(dve.tensor_tensor(out=W[0], in0=W[0], in1=all_nodes(BETA), op=ALU.add))
            link(dve.tensor_reduce(out=sc4[:, 0], in_=W[0].rearrange("p n (h j) -> p n j h", h=HEADS),
                                   axis=AX.X, op=ALU.add))
            link(dve.tensor_scalar(sc4[:, 0], sc4[:, 0], 1.0 / HEADS, None, ALU.mult))

            def best(top, pick):
                link(dve.tensor_reduce(out=top, in_=sc4[:, 0], axis=AX.X, op=ALU.max))
                link(dve.tensor_tensor(out=sc4[:, 2], in0=sc4[:, 0],
                                       in1=top.unsqueeze(2).to_broadcast([P, NB, EXPERTS]), op=ALU.is_equal))
                link(dve.tensor_tensor(out=sc4[:, 2], in0=sc4[:, 2],
                                       in1=order[:, :].unsqueeze(1).to_broadcast([P, NB, EXPERTS]), op=ALU.mult))
                link(dve.tensor_reduce(out=gm[:, 3, :], in_=sc4[:, 2], axis=AX.X, op=ALU.max))
                link(dve.tensor_tensor(out=pick, in0=sc4[:, 2],
                                       in1=gm[:, 3, :].unsqueeze(2).to_broadcast([P, NB, EXPERTS]),
                                       op=ALU.is_equal))

            for e in range(EXPERTS):
                did(dve.memset(order[:, e:e + 1], float(EXPERTS - e)))
            me.last()
            best(gm[:, 1, :], sc4[:, 1])
            link(dve.tensor_scalar(sc4[:, 2], sc4[:, 1], NONE, None, ALU.mult))
            link(dve.tensor_tensor(out=sc4[:, 0], in0=sc4[:, 0], in1=sc4[:, 2], op=ALU.add))
            best(gm[:, 2, :], sc4[:, 3])
            dve.tensor_tensor(out=gm[:, 0, :], in0=gm[:, 2, :], in1=gm[:, 1, :], op=ALU.subtract)\
               .then_inc(ev("gate_arg"), 1)
            dve.wait_ge(ev("gate_exp"), 1)
            link(dve.tensor_scalar(gm[:, 2, :], gm[:, 1, :], 1.0, None, ALU.add))
            link(dve.reciprocal(gm[:, 2, :], gm[:, 2, :]))
            link(dve.tensor_tensor(out=gm[:, 3, :], in0=gm[:, 1, :], in1=gm[:, 2, :], op=ALU.mult))
            did(dve.tensor_tensor(out=sc4[:, 1], in0=sc4[:, 1],
                                  in1=gm[:, 2, :].unsqueeze(2).to_broadcast([P, NB, EXPERTS]), op=ALU.mult))
            link(dve.tensor_tensor(out=sc4[:, 3], in0=sc4[:, 3],
                                   in1=gm[:, 3, :].unsqueeze(2).to_broadcast([P, NB, EXPERTS]), op=ALU.mult))
            dve.tensor_tensor(out=sc4[:, 0], in0=sc4[:, 1], in1=sc4[:, 3], op=ALU.add).then_inc(ev("gate_ready"), 1)
            dve.wait_ge(ev("gate_ready"), 1)

            h1 = X[:, 0:NB * C].rearrange("p (n c) -> p n c", c=C)
            with dve.Fori(0, NC) as c:
                me.enter(c * 15, 15)
                for e in range(EXPERTS):
                    for q in range(4):
                        if e == 0:
                            dve.wait_ge(ev("expert_product"), c * 4 + (q + 1))
                        res = h1[:, ds(c * 4 + q, 1), :].rearrange("p a c -> p (a c)")
                        ins = dve.scalar_tensor_tensor(
                            out=res, in0=bank[4 + q][:, e * C:e * C + C],
                            scalar=sc4[:, 0, ds(c * 4 + q, 1), e:e + 1].rearrange("p a e -> p (a e)"),
                            in1=res, op0=ALU.mult, op1=ALU.add)
                        if e == EXPERTS - 1 and q == 3:
                            ins.then_inc(ev("out_ready"), 1)
                        else:
                            did(ins)
                    if e < EXPERTS - 1:
                        me.last()
            me.leave(NC)


        @block.tensor
        def _(pe):
            mm = nc.tensor.matmul

            def conv(c):
                for j in range(TAPS // 2):
                    last = mm(bank[5][:, :], wr[:, j, :], XT[:, ds(c * CH + 2 * j * B, CH)],
                              start=(j == 0), stop=(j == TAPS // 2 - 1))
                last.then_inc(ev("conv_ready"), 1)

            pe.wait_ge(s_x[0], 16)
            pe.wait_ge(s_x[1], 16)
            pe.wait_ge(s_weff, 3)
            pe.wait_ge(s_const, CONSTS)
            conv(0)

            def s1(c, more):
                pe.wait_ge(ev("y_ready"), c + 1)
                mm(bank[6][:, :], mean64[:, :], XT[:, ds(c * CH, CH)], start=True, stop=True)\
                    .then_inc(ev("s1_mean"), 1)
                if more:
                    conv(c + 1)
                pe.wait_ge(ev("s1_square"), c + 1)
                mm(bank[7][:, :], mean64[:, :], s_b[:, :], start=True, stop=True).then_inc(ev("s1_var"), 1)
                pe.wait_ge(ev("s1_norm"), c + 1)
                pe.wait_ge(ev("x1_ready"), c)
                mm(bank[0][:, :], inw[:, :], s_b[:, :], start=True, stop=True).then_inc(ev("s1_in"), 1)

            with pe.Fori(0, NC - 1) as c:
                s1(c, True)
            s1(NC - 1, False)
            pe.wait_ge(ev("x1_ready"), NC)

            def turn(k):
                nc.tensor.transpose(bank[2 + k % 2][:, :].bitcast(bf16)[:, 0:P],
                                    onehot[:, k % 8, 0, :], ident_b[:, :]).then_inc(s_tr, 1)

            def pairs(k):
                mm(bank[4 + k % 2][:, 0:P], onehot_T[:, k % 4, :], onehot_T[:, k % 4, :],
                   start=True, stop=True).then_inc(s_pair, 1)

            for l in range(2):
                if l == 0:
                    pe.wait_ge(s_prep, 1)
                    mm(bank[1][:, 0:P], s_d[0:1, 0:P],
                       ones_row[:, 0:P], start=True, stop=True).then_inc(s_cnt, 1)
                    for k in range(2):
                        pe.wait_ge(s_oh, k + 1)
                        turn(k)
                    pe.wait_ge(s_te, 1)
                    pairs(0)
                with pe.Fori(l * 32, l * 32 + 32) as i:
                    pe.wait_ge(s_h, i * STEPS)
                    mm(bank[0][:, 0:SC], bw[:, l, :], X[:, ds(i * SC - l * MP, SC)], start=True, stop=False)
                    mm(bank[0][:, 0:SC], brow[:, l * H:(l + 1) * H], ones_row[:, 0:SC], start=False, stop=True)
                    col0 = pe.snap(i * SC - l * MP)
                    for j in range(TI):
                        if j < STEPS:
                            if j:
                                pe.wait_ge(s_h, i * STEPS + j)
                            mm(bank[0][:, j * B:j * B + B], aw[:, l, :], HS[:, ds(col0 + j * B, B)],
                               start=False, stop=True, skip_group_check=True).then_inc(s_pre, 1)
                        pe.wait_ge(s_oh, i * TI + (j + 3))
                        turn(j + 2)
                        pe.wait_ge(s_te, i * TI + (j + 2))
                        pairs(j + 1)
                        pe.wait_ge(s_early, i * TI + (j + 1))
                        pe.wait_ge(s_cc, i * TI + (j + 1))
                        r = bank[6 + j % 2][:, 0:P]
                        mm(r, onehot_T[:, j % 4, :], counts[:, j % 2, :], start=True, stop=False)
                        mm(r, earlier[:, j % 2, :], onehot[:, j % 8, 1, :], start=False, stop=True)\
                            .then_inc(s_rps, 1)
                        mm(bank[1][:, 0:P], onehot[:, j % 8, 0, :], onehot[:, j % 8, 1, :],
                           start=False, stop=True, skip_group_check=True).then_inc(s_cnt, 1)
                pe.wait_ge(s_h, (l + 1) * TP)
                pe.wait_ge(s_rk, (l + 1) * 32 * TI)
                pe.wait_ge(s_early, (l + 1) * 32 * TI + 1)
                pe.wait_ge(s_te, (l + 1) * 32 * TI + 2)

                def layer(c):
                    pe.wait_ge(ev(f"l{l}_norm"), c)
                    if l == 1:
                        pe.wait_ge(ev("h1_ready"), c)
                    mm(bank[0][:, :], cw[:, l, :], HS[:, ds(c * CH + B, CH)], start=True, stop=False)
                    mm(bank[0][:, :], dw[:, l, :], X[:, ds(c * CH, CH)], start=False, stop=True)\
                        .then_inc(ev(f"l{l}_mix"), 1)
                    pe.wait_ge(ev(f"l{l}_sum"), c + 1)
                    mm(bank[6][:, :], mean128[:, :], s_b[:, :], start=True, stop=True)\
                        .then_inc(ev(f"l{l}_mean"), 1)
                    pe.wait_ge(ev(f"l{l}_square"), c + 1)
                    mm(bank[7][:, :], mean128[:, :], s_b[:, :], start=True, stop=True).then_inc(ev(f"l{l}_var"), 1)

                with pe.Fori(0, NC) as c:
                    layer(c)
                    if l == 1:
                        pe.wait_ge(ev("l1_norm"), c + 1)
                        mm(bank[0][:, :], outw[:, :], X[:, ds(c * CH, CH)], start=True, stop=True)\
                            .then_inc(ev("o_product"), 1)
                        pe.wait_ge(ev("h1_ready"), c + 1)
                        mm(bank[6][:, :], mean64[:, :], s_b[:, :], start=True, stop=True)\
                            .then_inc(ev("o_mean"), 1)
                        pe.wait_ge(ev("h1_kept"), c)
                        for q in range(4):
                            last = nc.tensor.transpose(bank[5][:, q * P:(q + 1) * P], s_b[:, q * P:(q + 1) * P],
                                                       ident[:, :])
                        last.then_inc(ev("h1_turned"), 1)
                        pe.wait_ge(ev("o_square"), c + 1)
                        mm(bank[7][:, :], mean64[:, :], s_b[:, :], start=True, stop=True)\
                            .then_inc(ev("o_var"), 1)
                        pe.wait_ge(ev("xn_ready"), c + 1)
                        pe.wait_ge(ev("gat_kept"), c)
                        for q in range(4):
                            last = mm(bank[4][:, q * F:(q + 1) * F], s_d[:, q * P:(q + 1) * P], wgat[:, :],
                                      start=True, stop=True)
                        last.then_inc(ev("gat_product"), 1)

            pe.wait_ge(s_deg, 1)
            pe.wait_ge(s_rk, ITERS * TI)
            pe.wait_ge(ev("xn_kept"), NC)
            pe.wait_ge(ev("gat_kept"), NC + 1)
            with pe.Fori(0, NC) as c:
                for e in range(EXPERTS):
                    pe.wait_ge(ev("hidden_ready"), c * EXPERTS + e)
                    mm(bank[e][:, :], w1s[:, e, :], XT[:, ds(c * CH, CH)], start=True, stop=True)\
                        .then_inc(ev("hidden_product"), 1)
                pe.wait_ge(ev("hidden_ready"), c * EXPERTS + EXPERTS)
                pe.wait_ge(ev("out_ready"), c)
                for q in range(4):
                    for e in range(EXPERTS):
                        mm(bank[4 + q][:, e * C:(e + 1) * C], hid[:, e, q * P:(q + 1) * P], w2s[:, e, :],
                           start=True, stop=False)
                        last = mm(bank[4 + q][:, e * C:(e + 1) * C], ones_row[:, 0:P],
                                  b2row[:, e * C:(e + 1) * C], start=False, stop=True)
                    last.then_inc(ev("expert_product"), 1)



_INS = ["x_t", "conv_wr", "conv_wi", "phases", "in_w", "in_b", "a_w", "b_w", "b_b", "c_w", "c_b", "d_w", "d_b",
        "ln_w", "ln_b", "out_w", "out_b", "w_gat", "att_src", "att_dst", "b_gat", "gamma", "beta",
        "w1", "b1", "w2", "b2", "edges"]


def _laid_out(i):
    import numpy as np

    a = {k.removeprefix("L0_"): np.asarray(v) for k, v in i.items()}
    P = 128

    def taps(w):
        return w.transpose(1, 2, 0).reshape(64, 8, 2, 64).transpose(2, 0, 1, 3).reshape(P, 8, 64)

    def turned(w):
        return w.transpose(2, 0, 1)

    return {
        "x_t": a["x"].transpose(2, 1, 0).reshape(64, 750 * 16),
        "conv_wr": taps(a["tok_w_real"]), "conv_wi": taps(a["tok_w_imag"]),
        "phases": np.repeat(a["tok_phases"].reshape(8, 2).T, 64, axis=0),
        "in_w": a["attn_in_W"].T, "in_b": a["attn_in_b"],
        "a_w": turned(a["attn_A_W"]), "b_w": turned(a["attn_B_W"]), "b_b": a["attn_B_b"].reshape(1, 256),
        "c_w": turned(a["attn_C_W"]), "c_b": a["attn_C_b"].T, "d_w": turned(a["attn_D_W"]), "d_b": a["attn_D_b"].T,
        "ln_w": a["attn_ln_w"].T, "ln_b": a["attn_ln_b"].T,
        "out_w": a["attn_out_W"].T, "out_b": a["attn_out_b"],
        "w_gat": a["ffn_W_gat"], "att_src": a["ffn_att_src"].reshape(16), "att_dst": a["ffn_att_dst"].reshape(16),
        "b_gat": a["ffn_b_gat"], "gamma": a["ffn_ln_gamma"], "beta": a["ffn_ln_beta"],
        "w1": a["ffn_W1"].transpose(1, 0, 2), "b1": a["ffn_b1"].T,
        "w2": a["ffn_W2"].transpose(1, 0, 2), "b2": a["ffn_b2"].reshape(1, 256),
        "edges": a["ffn_edge_index"].reshape(2, P, -1).transpose(1, 0, 2).reshape(P, -1),
    }


def kernel(**inputs):
    import numpy as np
    import concourse.bacc as bacc
    from concourse.bass_utils import run_bass_kernel_spmd

    laid = _laid_out(inputs)
    nc = bacc.Bacc("TRN2", target_bir_lowering=False, num_devices=1)
    arrays, args = {}, []
    for name in _INS:
        a = np.ascontiguousarray(laid[name])
        arrays[f"in_{name}"] = a
        args.append(nc.dram_tensor(f"in_{name}", a.shape, mybir.dt.from_np(a.dtype), kind="ExternalInput").ap())
    out = nc.dram_tensor("out_h", (16, 735, 64), mybir.dt.float32, kind="ExternalOutput").ap()
    audio_tower_program(nc, *args, out)
    r = run_bass_kernel_spmd(nc, [arrays], core_ids=[0])
    return r.results[0]["out_h"]
```

```python
import concourse.bass as bass
from concourse import mybir
from contextlib import ExitStack


def audio_tower_program(nc, x_t, conv_wr, conv_wi, phases, in_w, in_b, a_w, b_w, b_b, c_w, c_b, d_w, d_b,
                        ln_w, ln_b, out_w, out_b, w_gat, att_src, att_dst, b_gat, gamma, beta,
                        w1, b1, w2, b2, edges, out):
    fp32, bf16 = mybir.dt.float32, mybir.dt.bfloat16
    u32, i32 = mybir.dt.uint32, mybir.dt.int32
    ALU, ACT, AX = mybir.AluOpType, mybir.ActivationFunctionType, mybir.AxisListType
    ds = bass.ds

    P = 128
    B, T, C, H = 16, 735, 64, 128
    TAPS = 16
    TP = 736
    M = B * T
    MP = B * TP
    NB = MP // P
    XC = 750 * B
    CH = 512
    NC = MP // CH
    HEADS, EXPERTS = 4, 4
    F = HEADS * EXPERTS
    ROW = HEADS + F
    SLOTS = 40
    NE = edges.shape[1] * P // 2
    ET = NE // P
    ITERS = 64
    TI = ET // ITERS
    STEPS = 2 * TP // ITERS
    SC = STEPS * B
    GR, GS = 4, TI // 4
    FAR = float(1 << 23)
    EMPTY = 16383
    EPS = 1e-5
    NONE = -1e30
    assert NC * CH == MP and TI * ITERS == ET and STEPS * ITERS == 2 * TP and SC <= 512

    ell = nc.dram_tensor("ell", (MP * SLOTS, 1), u32, kind="Internal").ap()
    table = nc.dram_tensor("node_rows", (MP, ROW), fp32, kind="Internal").ap()
    experts_out = nc.dram_tensor("experts_out", (P, NB * EXPERTS * C), fp32, kind="Internal").ap()

    ctx = ExitStack()
    with ctx:
        def sb(name, shape, dt=fp32):
            return ctx.enter_context(nc.sbuf_tensor(name, shape, dt))

        def sem(name):
            return ctx.enter_context(nc.semaphore(name))

        XT = sb("XT", [P, XC])
        X = sb("X", [P, MP])
        HS = sb("HS", [P, B + MP])
        src_ids = sb("src_ids", [P, ET], mybir.dt.uint16)
        dst_lohi = sb("dst_lohi", [P, ET + 8, 2], bf16)
        ranks = sb("ranks", [P, ET])
        rows = sb("rows", [P, NB, ROW])
        adst = sb("adst", [P, NB, HEADS])

        free_at = [NB * C]

        def in_x(*dims):
            n = 1
            for d in dims:
                n *= d
            part = X[:, free_at[0]:free_at[0] + n]
            free_at[0] += n
            assert free_at[0] <= MP
            if len(dims) == 1:
                return part
            letters = "abcd"[:len(dims)]
            return part.rearrange(f"p ({' '.join(letters)}) -> p {' '.join(letters)}",
                                  **dict(zip(letters[1:], dims[1:])))

        acc = in_x(NB, ROW)
        mx = in_x(NB, HEADS)
        G = in_x(2, SLOTS, ROW)
        small4 = in_x(4, NB, EXPERTS)
        gm = in_x(4, NB)

        wr = sb("wr", [P, TAPS // 2, P])
        wi = sb("wi", [P, TAPS // 2, C])
        ph = sb("ph", [P, TAPS // 2])
        trig = sb("trig", [P, 4, TAPS // 2])
        trig_i = sb("trig_i", [P, 2, TAPS // 2], i32)
        inw = sb("inw", [P, H])
        aw, bw, cw, dw = [sb(n, [P, 2, H]) for n in ("aw", "bw", "cw", "dw")]
        cols = sb("cols", [P, 16])
        brow = sb("brow", [1, 2 * H])
        outw = sb("outw", [P, P])
        wgat = sb("wgat", [P, F])
        vecs = sb("vecs", [P, 5, F])
        w1s = sb("w1s", [P, EXPERTS, H])
        w2s = sb("w2s", [P, EXPERTS, C])
        b2row = sb("b2row", [1, EXPERTS * C])

        iota = sb("iota", [P, P], bf16)
        ident = sb("ident", [P, P])
        ident_b = sb("ident_b", [P, P], bf16)
        before = sb("before", [P, P])
        ones_row = sb("ones_row", [1, CH])
        mean64 = sb("mean64", [P, P])
        mean128 = sb("mean128", [P, P])
        eps_col = sb("eps_col", [P, 1])

        onehot = sb("onehot", [P, 8, 2, P], bf16)
        onehot_T = sb("onehot_T", [P, 4, P])
        earlier = sb("earlier", [P, 2, P], bf16)
        counts = sb("counts", [P, 2, P])
        junk = sb("junk", [P, 2, P], bf16)
        rank = sb("rank", [P, TI])
        over = sb("over", [P, GS])
        slot_f = sb("slot_f", [P, GS])
        slot_ix = sb("slot_ix", [P, TI], u32)
        src_st = sb("src_st", [P, TI], u32)

        space = sb("space", [P, 4 * CH])
        s_a, s_b, s_c, n_b, n_c = [space[:, k * SC:(k + 1) * SC] for k in range(5)]
        turned_in = [space[:, k * CH:(k + 1) * CH] for k in range(2)]

        EL = sb("EL", [P, 2, SLOTS], u32)
        FILL = HS[:, 2 * ET:2 * ET + MP * SLOTS // P].bitcast(u32)
        CONSTS = 18
        ATT_STEPS = 15
        RG = ET // GS
        MAX_ROUNDS = -(-ET * P // SLOTS)
        window = sb("window", [P, 1])
        degree = sb("degree", [P, 2])
        degrees = sb("degrees", [P, 2, NB])
        block_degree = sb("block_degree", [P, NB], i32)
        PAIR = 2
        rounds_i = sb("rounds_i", [P, 1], i32)
        s_rounds = sem("rounds_known")
        s_deg = sem("degree_ready")
        s_dve_round = sem("vector_round_step")
        s_round_part = sem("round_index_step")
        s_round_empty = sem("round_table_emptied")
        s_round_ix = sem("round_indices_ready")
        s_round_sc = sem("round_scattered")
        s_round_put = sem("round_group_scattered")
        s_round_go = sem("round_block_wanted")
        s_round_el = sem("round_slots_loaded")
        s_round_ga = sem("round_rows_gathered")
        s_round_rows = sem("round_block_gathered")
        s_round_used = sem("round_rows_used")
        past = 2 * ET + MP * SLOTS // P
        assert F * SLOTS + 4 * NB * F <= past
        pexp, parg = [HS[:, past + k * HEADS * (SLOTS + 1):past + (k + 1) * HEADS * (SLOTS + 1)] for k in range(2)]
        pmask = sb("pmask", [P, SLOTS])
        pe_ = sb("pe_", [P, HEADS, SLOTS])
        small = sb("small", [P, 4, F])
        work = HS[:, F * SLOTS:F * SLOTS + 4 * NB * F].rearrange("p (k n f) -> p k n f", k=4, f=F)
        hid = HS[:, F * SLOTS:F * SLOTS + EXPERTS * CH].rearrange("p (e c) -> p e c", e=EXPERTS)
        stage_at = past + 2 * HEADS * (SLOTS + 1)
        out_stage = HS[:, stage_at:stage_at + 4 * EXPERTS * C]
        PIECES = 4
        PN = NB // PIECES
        PW = PN * EXPERTS * C
        back = [XT[:, 0:PW], XT[:, PW:2 * PW], HS[:, 0:PW], XT[:, 0:PW]]
        msg = HS[:, 0:F * SLOTS].rearrange("p (h j k) -> p h j k", h=HEADS, k=SLOTS)
        order = sb("order", [P, EXPERTS])

        bank = [ctx.enter_context(nc.psum_tensor(f"bank{k}", [P, 512], fp32)) for k in range(8)]

        IN_B, C_B, D_B, LN_W, LN_B, OUT_B, B1, CD_B = 0, 1, 3, 5, 7, 9, 10, 14
        ATT_S, ATT_D, BGAT, GAMMA, BETA = range(5)

        s_par = sem("params_loaded")
        s_edge = sem("edges_loaded")
        s_x = [sem(f"x_loaded{k}") for k in range(2)]
        s_const = sem("constants_made")
        s_ellfill = sem("ell_filled_sbuf")
        s_ell0 = sem("ell_emptied")
        s_dve = sem("vector_step")
        s_act = sem("scalar_step")
        s_weff = sem("conv_weights_ready")
        s_prep = sem("edges_prepared")

        s_oh = sem("onehot_ready")
        s_tr = sem("onehot_transposed")
        s_te = sem("onehot_T_copied")
        s_pair = sem("pairs_ready")
        s_early = sem("earlier_ready")
        s_rps = sem("rank_products_ready")
        s_cnt = sem("counts_updated")
        s_cc = sem("counts_copied")
        s_rk = sem("ranks_ready")
        s_ix = sem("slot_indices_ready")
        s_sc = [sem(f"scattered{g}") for g in range(GR)]
        s_bx = sem("scan_input_ready")
        s_pre = sem("scan_product_ready")
        s_h = sem("state_ready")
        s_tab = sem("table_stored")
        s_el = [sem(f"slots_loaded{k}") for k in range(2)]
        s_ga = [sem(f"rows_gathered{k}") for k in range(2)]
        s_used = sem("rows_used")
        s_arg = sem("exp_arguments_ready")
        s_exp = sem("exp_ready")
        s_parked = sem("experts_out_stored")
        s_back = [sem(f"experts_out_loaded{k}") for k in range(3)]
        s_out = sem("out_stored")

        block = ctx.enter_context(nc.Block())

        class Steps:

            def __init__(self, eng, sem):
                self.eng, self.sem, self.n, self.off, self.loops = eng, sem, 0, None, []

            def did(self, ins):
                ins.then_inc(self.sem, 1)
                self.n += 1
                return ins

            def last(self):
                self.eng.wait_ge(self.sem, self.n if self.off is None else self.off + self.n)

            def link(self, ins):
                self.did(ins)
                self.last()

            def enter(self, off, per):
                self.loops.append((self.off, per, self.n))
                self.off = off

            def leave(self, times):
                self.off, per, at = self.loops.pop()
                assert self.n - at == per, (self.n - at, per)
                self.n = at + times * per

        names = {}

        def ev(name):
            if name not in names:
                names[name] = sem(name)
            return names[name]

        for n in ("conv_ready", "y_ready", "s1_mean", "s1_centered", "s1_square", "s1_var", "s1_root", "s1_norm",
                  "s1_in", "x1_ready"):
            ev(n)
        for l in range(2):
            for n in ("mix", "sum", "mean", "centered", "square", "var", "root", "norm"):
                ev(f"l{l}_{n}")
        for n in ("o_product", "h1_ready", "o_mean", "o_centered", "o_square", "o_var", "o_root", "xn_ready",
                  "xn_staged", "gat_product", "gat_kept", "h1_staged", "h1_turned", "h1_kept"):
            ev(n)
        for n in ("hidden_product", "hidden_ready", "expert_product", "expert_kept", "gate_ready",
                  "gate_root", "gate_var", "gate_arg", "gate_exp", "out_ready"):
            ev(n)

        NPAR = 28

        S1 = dict(P_mean=10, V_centered=10, A_y=8, A_square=11, P_var=13, A_root=24, V_recip=26, V_norm=27,
                  P_in=29, A_x1=29)
        MIX = dict(P_mix=23, V_sum=23, P_mean=25, V_centered=25, A_square=26, P_var=28, A_root=28, V_recip=30,
                   V_norm=31)
        OUT = dict(P_out=1, V_h1=1, P_mean=3, V_centered=3, A_square=4, P_var=6, A_root=24, V_recip=26, V_xn=27)

        @block.sync
        def _(sp):
            sp.dma_start(HS[:, 0:2 * ET].bitcast(i32), edges).then_inc(s_edge, 16)
            sp.dma_start(XT[0:C, :], x_t).then_inc(s_x[0], 16)
            sp.dma_start(XT[C:P, 0:XC - B], x_t[:, B:XC]).then_inc(s_x[1], 16)

            sp.wait_ge(s_ix, 4 * ITERS)
            for g in range(GR):
                sp.wait_ge(s_sc[g], ITERS * GS * 16)
            blocks = ell.rearrange("(b p k) o -> b p (k o)", p=P, k=SLOTS)
            for k in range(2):
                sp.dma_start(EL[:, k, :], blocks[k, :, :]).then_inc(s_el[k], 16)
            with sp.Fori(1, NB // 2) as i:
                for k in range(2):
                    sp.wait_ge(s_used, i * 2 + (k - 1))
                    sp.dma_start(EL[:, k, :], blocks[ds(i * 2 + k, 1), :, :].rearrange("a p k -> (a p) k"))\
                        .then_inc(s_el[k], 16)

            sp.wait_ge(s_rounds, 1)
            rounds = sp.value_load(rounds_i[0:1, 0:1], min_val=0, max_val=MAX_ROUNDS)
            with sp.If(rounds > 1):
                sp.wait_ge(s_used, NB)
                with sp.Fori(1, rounds) as r:
                    with sp.Fori(0, NB) as b:
                        sp.wait_ge(s_round_go, (r - 1) * NB + b + 1)
                        sp.dma_start(EL[:, 0, :], blocks[ds(b, 1), :, :].rearrange("a p k -> (a p) k"))\
                          .then_inc(s_round_el, 16)

            def bring(p):
                sp.dma_start(back[p], experts_out[:, p * PW:(p + 1) * PW]).then_inc(s_back[p % 3], 16)

            sp.wait_ge(s_parked, 16 * NC)
            bring(0)
            bring(1)
            sp.wait_ge(ev("gate_ready"), 1)
            bring(2)

            h1 = X[:, 0:NB * C].rearrange("p (n c) -> p n c", c=C)
            for p in range(PIECES):
                sp.wait_ge(ev("out_ready"), p + 1)
                if p == 0:
                    bring(3)
                for tl in range(8):
                    first = 8 * PN * p + tl
                    n = len(range(first, min(T, 8 * PN * (p + 1)), 8))
                    sp.dma_start(out[:, first:first + 8 * (n - 1) + 1:8, :], h1[B * tl:B * tl + B, PN * p:PN * p + n, :])\
                      .then_inc(s_out, 16)
            sp.wait_ge(s_out, PIECES * 8 * 16)


        @block.gpsimd
        def _(pool):
            link = Steps(pool, s_const)
            link.did(pool.memset(FILL, EMPTY))
            link.last()
            pool.dma_start(ell.rearrange("(p n) o -> p (n o)", p=P), FILL).then_inc(s_ell0, 16)
            link.last()
            link.link(pool.memset(XT[C:P, XC - B:XC], 0.0))
            link.did(pool.memset(ident[:, :], 0.0))
            link.did(pool.memset(before[:, :], 1.0))
            link.did(pool.memset(ones_row[:, :], 1.0))
            link.did(pool.memset(mean64[:, :], 0.0))
            link.last()
            link.link(pool.memset(mean64[0:C, :], 1.0 / C))
            link.link(pool.memset(inw[C:P, :], 0.0))
            link.link(pool.memset(wgat[C:P, :], 0.0))
            link.link(pool.memset(w1s[C:P, :, :], 0.0))
            link.did(pool.memset(mean128[:, :], 1.0 / H))
            link.did(pool.memset(eps_col[:, :], EPS))
            link.did(pool.memset(dst_lohi[:, ET:ET + 8, :], 200.0))
            link.did(pool.iota(iota[:, :], [[1, P]], base=0, channel_multiplier=0,
                               allow_small_or_imprecise_dtypes=True))
            link.last()
            link.did(pool.affine_select(out=ident[:, :], in_=ident[:, :], compare_op=ALU.not_equal, fill=1.0,
                                        base=0, pattern=[[-1, P]], channel_multiplier=1))
            link.did(pool.affine_select(out=before[:, :], in_=before[:, :], compare_op=ALU.is_gt, fill=0.0,
                                        base=0, pattern=[[1, P]], channel_multiplier=-1))
            link.last()
            link.did(pool.tensor_copy(ident_b[:, :], ident[:, :]))
            link.did(pool.memset(space[:, :], 0.0))

            none = pool.alloc_register("none")
            last_slot = pool.alloc_register("last_slot")
            last_row = pool.alloc_register("last_row")
            pool.reg_mov(none, 0)
            pool.wait_ge(s_ell0, 16)
            with pool.Fori(0, ITERS) as i:
                for g in range(GR):
                    pool.wait_ge(s_ix, i * GR + (g + 1))
                    pool.reg_add(last_slot, none, MP * SLOTS - 1)
                    for u in range(g * GS, g * GS + GS):
                        pool.indirect_dma_start(ell, bass.IndirectOffsetOnAxis(ap=slot_ix[:, u:u + 1], axis=0),
                                                src_st[:, u:u + 1], None, bounds_check=last_slot,
                                                oob_is_err=False).then_inc(s_sc[g], 16)

            pool.wait_ge(s_deg, 1)
            pool.partition_all_reduce(degrees[:, 1, :], degrees[:, 0, :], P, bass.bass_isa.ReduceOp.max).then_inc(s_deg, 1)
            pool.wait_ge(s_rounds, 1)
            pool.wait_ge(ev("gat_kept"), NC + 1)
            link.did(pool.memset(G[:, :, :, :], 0.0))
            link.last()
            pool.wait_ge(s_tab, 16)

            def gather(b, k, done):
                filled = pool.value_load(block_degree[0:1, ds(b, 1)], min_val=0, max_val=ET * P)
                for s0 in range(0, SLOTS, PAIR):
                    with pool.If(filled > s0):
                        for s in range(s0, s0 + PAIR):
                            pool.indirect_dma_start(G[:, k, s, :], None, table,
                                                    bass.IndirectOffsetOnAxis(ap=EL[:, k, s:s + 1], axis=0),
                                                    bounds_check=last_row, oob_is_err=False).then_inc(done, 16)
                    with pool.Else():
                        pool.inc_swdge_sem([done], [16 * PAIR], mode="add")

            pool.reg_add(last_row, none, MP - 1)
            for k in range(2):
                pool.wait_ge(s_el[k], 16)
                gather(k, k, s_ga[k])
            with pool.Fori(1, NB // 2) as i:
                for k in range(2):
                    pool.wait_ge(s_el[k], i * 16 + 16)
                    pool.reg_add(last_row, none, MP - 1)
                    gather(i * 2 + k, k, s_ga[k])

            pool.wait_ge(s_rounds, 1)
            rounds = pool.value_load(rounds_i[0:1, 0:1], min_val=0, max_val=MAX_ROUNDS)
            with pool.If(rounds > 1):
                for k in range(2):
                    pool.wait_ge(s_ga[k], NB // 2 * 16 * SLOTS)
                link.link(pool.memset(FILL, EMPTY))
                with pool.Fori(1, rounds) as r:
                    pool.dma_start(ell.rearrange("(p n) o -> p (n o)", p=P), FILL).then_inc(s_round_empty, 16)
                    pool.wait_ge(s_round_empty, 16)
                    pool.inc_swdge_sem([s_round_empty], [16], mode="sub")
                    with pool.Fori(0, RG) as g:
                        pool.wait_ge(s_round_ix, (r - 1) * RG + g + 1)
                        pool.reg_add(last_slot, none, MP * SLOTS - 1)
                        for u in range(GS):
                            pool.indirect_dma_start(ell, bass.IndirectOffsetOnAxis(ap=slot_ix[:, u:u + 1], axis=0),
                                                    src_st[:, u:u + 1], None, bounds_check=last_slot,
                                                    oob_is_err=False).then_inc(s_round_sc, 16)
                        pool.wait_ge(s_round_sc, GS * 16)
                        pool.inc_swdge_sem([s_round_sc], [GS * 16], mode="sub")
                        pool.sem_inc(s_round_put, 1)
                    with pool.Fori(0, NB) as b:
                        pool.wait_ge(s_round_used, (r - 1) * NB + b)
                        pool.sem_inc(s_round_go, 1)
                        pool.wait_ge(s_round_el, ((r - 1) * NB + b + 1) * 16)
                        pool.reg_add(last_row, none, MP - 1)
                        for s in range(SLOTS):
                            pool.indirect_dma_start(G[:, 0, s, :], None, table,
                                                    bass.IndirectOffsetOnAxis(ap=EL[:, 0, s:s + 1], axis=0),
                                                    bounds_check=last_row, oob_is_err=False)\
                                .then_inc(s_round_ga, 16)
                        pool.wait_ge(s_round_ga, SLOTS * 16)
                        pool.inc_swdge_sem([s_round_ga], [SLOTS * 16], mode="sub")
                        pool.sem_inc(s_round_rows, 1)

        @block.scalar
        def _(act):
            def col(v):
                return v.rearrange("(n o) -> n o", o=1)

            def bc(v, n):
                return v.rearrange("(o n) -> o n", o=1).to_broadcast([n, v.shape[0]])

            loads = [(wr[:, :, 0:C], conv_wr), (wi[:, :, :], conv_wi), (ph[:, :], phases), (inw[0:C, :], in_w),
                     (cols[:, IN_B:IN_B + 1], col(in_b)), (outw[:, 0:C], out_w),
                     (outw[:, C:P], out_w), (cols[0:C, OUT_B:OUT_B + 1], col(out_b)),
                     (cols[C:P, OUT_B:OUT_B + 1], col(out_b)),
                     (wgat[0:C, :], w_gat), (brow[:, :], b_b), (b2row[:, :], b2),
                     (cols[:, C_B:C_B + 2], c_b), (cols[:, D_B:D_B + 2], d_b), (cols[:, LN_W:LN_W + 2], ln_w),
                     (cols[:, LN_B:LN_B + 2], ln_b), (cols[:, B1:B1 + 4], b1),
                     (w1s[0:C, :, :], w1), (w2s[:, :, :], w2),
                     (aw[:, :, :], a_w), (bw[:, :, :], b_w), (cw[:, :, :], c_w), (dw[:, :, :], d_w),
                     (vecs[:, ATT_S, :], bc(att_src, P)), (vecs[:, ATT_D, :], bc(att_dst, P)),
                     (vecs[:, BGAT, :], bc(b_gat, P)), (vecs[:, GAMMA, :], bc(gamma, P)),
                     (vecs[:, BETA, :], bc(beta, P))]
            assert len(loads) == NPAR
            for dst, src in loads:
                act.dma_start(dst, src).then_inc(s_par, 16)
            act.wait_ge(s_weff, 1)
            act.activation(trig[:, 0:2, :], trig[:, 2:4, :], ACT.Sin).then_inc(s_weff, 1)

            act.wait_ge(s_const, CONSTS)

            def s1(c, j):
                if j == S1["A_y"]:
                    act.wait_ge(ev("conv_ready"), c + 1)
                    act.activation(XT[:, ds(c * SC, SC)], bank[3][:, 0:SC], ACT.Copy).then_inc(ev("y_ready"), 1)
                if j == S1["A_square"]:
                    act.wait_ge(ev("s1_centered"), c + 1)
                    act.activation(s_b, s_a, ACT.Square).then_inc(ev("s1_square"), 1)
                if j == S1["A_root"]:
                    act.wait_ge(ev("s1_var"), c + 1)
                    act.activation(s_c, bank[3][:, 0:SC], ACT.Sqrt, bias=eps_col[:, :]).then_inc(ev("s1_root"), 1)
                if j == S1["A_x1"]:
                    act.wait_ge(ev("s1_in"), c + 1)
                    act.activation(X[:, ds(c * SC, SC)], bank[3][:, 0:SC], ACT.Identity,
                                   bias=cols[:, IN_B:IN_B + 1]).then_inc(ev("x1_ready"), 1)

            def mix(l, c, j):
                if j == MIX["A_square"]:
                    act.wait_ge(ev(f"l{l}_centered"), c + 1)
                    act.activation(n_b, X[:, ds(c * SC, SC)], ACT.Square).then_inc(ev(f"l{l}_square"), 1)
                if j == MIX["A_root"]:
                    act.wait_ge(ev(f"l{l}_var"), c + 1)
                    act.activation(n_c, bank[0][:, 0:SC], ACT.Sqrt, bias=eps_col[:, :])\
                       .then_inc(ev(f"l{l}_root"), 1)

            def output(c, j):
                if j == OUT["A_square"]:
                    act.wait_ge(ev("o_centered"), c + 1)
                    act.activation(s_b, s_a, ACT.Square).then_inc(ev("o_square"), 1)
                if j == OUT["A_root"]:
                    act.wait_ge(ev("o_var"), c + 1)
                    act.activation(s_c, bank[3][:, 0:SC], ACT.Sqrt, bias=eps_col[:, :]).then_inc(ev("o_root"), 1)

            act.wait_ge(s_prep, 1)
            for j in range(TI):
                s1(0, j)

            def onehot_copy(k):
                act.activation(onehot_T[:, k % 4, :], bank[2][:, :].bitcast(bf16)[:, 0:P],
                               ACT.Copy).then_inc(s_te, 1)

            def count_copy(k):
                act.activation(counts[:, k % 2, :], bank[1][:, 0:P], ACT.Copy).then_inc(s_cc, 1)

            act.wait_ge(s_cnt, 1)
            count_copy(0)
            for k in range(2):
                act.wait_ge(s_tr, k + 1)
                onehot_copy(k)

            def iteration(l, i, beside):
                col0 = i * SC + (B - l * MP)
                if not isinstance(i, int):
                    col0 = act.snap(col0)
                for j in range(TI):
                    if j < STEPS:
                        act.wait_ge(s_pre, i * STEPS + (j + 1))
                        act.activation(HS[:, ds(col0 + j * B, B)], bank[0][:, j * B:j * B + B], ACT.Tanh)\
                           .then_inc(s_h, 1)
                    act.wait_ge(s_tr, i * TI + (j + 3))
                    onehot_copy(j + 2)
                    act.wait_ge(s_cnt, i * TI + (j + 2))
                    count_copy(j + 1)
                    mix(l, i - 32 * l, j)
                    if beside and l == 0:
                        s1(i + 1, j)
                    if beside and l == 1:
                        output(i - 33, j)

            with act.Fori(0, 31) as i:
                iteration(0, i, True)
            iteration(0, 31, False)
            iteration(1, 32, False)
            with act.Fori(33, 64) as i:
                iteration(1, i, True)
            for j in range(TI):
                output(31, j)

            def stage_xn(c, k):
                act.activation(turned_in[k], XT[:, ds(c * CH, CH)], ACT.Copy).then_inc(ev("xn_staged"), 1)

            act.wait_ge(ev("xn_ready"), 32)
            stage_xn(0, 0)
            stage_xn(1, 1)
            with act.Fori(1, NC // 2) as i:
                for k in range(2):
                    act.wait_ge(ev("gat_product"), i * 2 + (k - 1))
                    stage_xn(i * 2 + k, k)
            act.wait_ge(ev("gat_product"), NC - 2)
            stage_xn(NC - 1, 0)

            act.wait_ge(ev("gat_kept"), NC + 1)
            act.dma_start(table.rearrange("(b p) f -> p b f", p=P), rows[:, :, :]).then_inc(s_tab, 16)

            with act.Fori(0, NC) as c:
                act.activation(turned_in[0], XT[:, ds(c * CH, CH)], ACT.Copy).then_inc(ev("h1_staged"), 1)
                act.wait_ge(ev("h1_turned"), c + 1)
                act.activation(X[:, ds(c * (4 * C), 4 * C)].rearrange("p (q c) -> p q c", q=4),
                               bank[4][:, :].rearrange("p (q c) -> p q c", q=4)[:, :, C:P], ACT.Copy)\
                   .then_inc(ev("h1_kept"), 1)
                for q in range(4):
                    act.wait_ge(s_arg, c * 4 + (q + 1))
                    act.activation(pexp[:, :], parg[:, :], ACT.Exp).then_inc(s_exp, 1)
                    act.wait_ge(ev("hidden_product"), c * 4 + (q + 1))
                    act.activation(hid[:, q, :], bank[q][:, :], ACT.Gelu, bias=cols[:, B1 + q:B1 + q + 1])\
                       .then_inc(ev("hidden_ready"), 1)
                act.wait_ge(s_parked, c * 16)
                for q in range(4):
                    act.wait_ge(ev("expert_product"), c * 4 + (q + 1))
                    act.activation(out_stage[:, q * EXPERTS * C:(q + 1) * EXPERTS * C], bank[4 + q][:, 0:EXPERTS * C],
                                   ACT.Copy).then_inc(ev("expert_kept"), 1)
                act.wait_ge(ev("expert_kept"), c * 4 + 4)
                act.dma_start(experts_out[:, ds(c * (4 * EXPERTS * C), 4 * EXPERTS * C)], out_stage)\
                   .then_inc(s_parked, 16)

            act.wait_ge(s_rounds, 1)
            rounds = act.value_load(rounds_i[0:1, 0:1], min_val=0, max_val=MAX_ROUNDS)
            with act.If(rounds > 1):
                with act.Fori(1, rounds) as r:
                    with act.Fori(0, NB) as b:
                        act.wait_ge(s_arg, r * NB + b + 1)
                        act.activation(pexp[:, :], parg[:, :], ACT.Exp).then_inc(s_exp, 1)

            act.wait_ge(ev("gate_var"), 1)
            act.activation(gm[:, 1, :], gm[:, 0, :], ACT.Sqrt, bias=eps_col[:, :]).then_inc(ev("gate_root"), 1)
            act.wait_ge(ev("gate_arg"), 1)
            act.activation(gm[:, 1, :], gm[:, 0, :], ACT.Exp).then_inc(ev("gate_exp"), 1)

        @block.vector
        def _(dve):
            me = Steps(dve, s_dve)
            link, did = me.link, me.did

            TAU = 6.283185307179586
            dve.wait_ge(s_par, 16 * NPAR)
            did(dve.tensor_scalar(trig[:, 0, :], ph[:, :], TAU / 4, None, ALU.add))
            link(dve.tensor_copy(trig[:, 1, :], ph[:, :]))
            link(dve.tensor_scalar(trig_i[:, :, :], trig[:, 0:2, :], 1 / TAU, None, ALU.mult))
            link(dve.tensor_copy(trig[:, 2:4, :], trig_i[:, :, :]))
            link(dve.scalar_tensor_tensor(out=trig[:, 2:4, :], in0=trig[:, 2:4, :], scalar=-TAU,
                                          in1=trig[:, 0:2, :], op0=ALU.mult, op1=ALU.add))
            for side, op in ((-TAU, ALU.is_gt), (TAU, ALU.is_lt)):
                link(dve.tensor_scalar(trig[:, 0:2, :], trig[:, 2:4, :], -side / 2, side, op, ALU.mult))
                link(dve.tensor_tensor(out=trig[:, 2:4, :], in0=trig[:, 2:4, :], in1=trig[:, 0:2, :], op=ALU.add))
            link(dve.tensor_scalar(trig[:, 2:4, :], trig[:, 2:4, :], 3.1415925, -3.1415925, ALU.min, ALU.max))
            dve.tensor_tensor(out=cols[:, CD_B:CD_B + 2], in0=cols[:, C_B:C_B + 2], in1=cols[:, D_B:D_B + 2],
                              op=ALU.add).then_inc(s_weff, 1)
            dve.wait_ge(s_weff, 2)
            cos = trig[:, 0, :].unsqueeze(2).to_broadcast([P, TAPS // 2, C])
            sin = trig[:, 1, :].unsqueeze(2).to_broadcast([P, TAPS // 2, C])
            did(dve.tensor_tensor(out=wr[:, :, 0:C], in0=wr[:, :, 0:C], in1=cos, op=ALU.mult))
            link(dve.tensor_tensor(out=wi[:, :, :], in0=wi[:, :, :], in1=sin, op=ALU.mult))
            link(dve.tensor_tensor(out=wr[:, :, C:P], in0=wr[:, :, 0:C], in1=wi[:, :, :], op=ALU.subtract))
            dve.tensor_tensor(out=wr[:, :, 0:C], in0=wr[:, :, 0:C], in1=wi[:, :, :], op=ALU.subtract).then_inc(s_weff, 1)

            dve.wait_ge(s_edge, 16)
            Nn, Q, R, Z = [X[:, k * ET:(k + 1) * ET] for k in range(4)]
            QI = X[:, 4 * ET:5 * ET].bitcast(i32)

            def divide(n, by, half):
                link(dve.tensor_scalar(QI, n, half, 1.0 / by, ALU.add, ALU.mult))
                link(dve.tensor_copy(Q, QI))
                link(dve.scalar_tensor_tensor(out=R, in0=Q, scalar=-float(by), in1=n, op0=ALU.mult, op1=ALU.add))
                link(dve.tensor_scalar(Z, R, 0.0, None, ALU.is_lt))
                did(dve.tensor_tensor(out=Q, in0=Q, in1=Z, op=ALU.subtract))
                link(dve.scalar_tensor_tensor(out=R, in0=Z, scalar=float(by), in1=R, op0=ALU.mult, op1=ALU.add))

            for side in range(2):
                ids = HS[:, side * ET:(side + 1) * ET].bitcast(i32)
                link(dve.tensor_copy(Nn, ids))
                if side == 0:
                    link(dve.tensor_scalar(Nn, Nn, float(M - 1), None, ALU.min))
                divide(Nn, T, 0.25)
                link(dve.scalar_tensor_tensor(out=R, in0=R, scalar=float(B), in1=Q, op0=ALU.mult, op1=ALU.add))
                if side == 0:
                    link(dve.tensor_copy(src_ids[:, :], R))
            link(dve.tensor_scalar(Z, Nn, float(M), 16384.0, ALU.is_ge, ALU.mult))
            link(dve.tensor_tensor(out=Nn, in0=R, in1=Z, op=ALU.add))
            divide(Nn, P, 0.5)
            link(dve.tensor_copy(dst_lohi[:, 0:ET, 0], R))
            did(dve.tensor_copy(dst_lohi[:, 0:ET, 1], Q))
            me.last()
            dve.memset(HS[:, 0:B], 0.0).then_inc(s_prep, 1)

            def s1(c, j):
                if j == S1["V_centered"]:
                    dve.wait_ge(ev("s1_mean"), c + 1)
                    dve.tensor_tensor(out=s_a, in0=XT[:, ds(c * SC, SC)], in1=bank[3][:, 0:SC],
                                      op=ALU.subtract).then_inc(ev("s1_centered"), 1)
                if j == S1["V_recip"]:
                    dve.wait_ge(ev("s1_root"), c + 1)
                    did(dve.reciprocal(s_c, s_c))
                if j == S1["V_norm"]:
                    me.last()
                    dve.tensor_tensor(out=s_b, in0=s_a, in1=s_c, op=ALU.mult).then_inc(ev("s1_norm"), 1)

            def mix(l, c, j):
                chunk = X[:, ds(c * SC, SC)]
                if j == MIX["V_sum"]:
                    dve.wait_ge(ev(f"l{l}_mix"), c + 1)
                    dve.scalar_tensor_tensor(out=chunk, in0=bank[0][:, 0:SC], scalar=cols[:, CD_B + l:CD_B + l + 1],
                                             in1=chunk, op0=ALU.add, op1=ALU.add).then_inc(ev(f"l{l}_sum"), 1)
                if j == MIX["V_centered"]:
                    dve.wait_ge(ev(f"l{l}_mean"), c + 1)
                    dve.tensor_tensor(out=chunk, in0=chunk, in1=bank[0][:, 0:SC], op=ALU.subtract)\
                       .then_inc(ev(f"l{l}_centered"), 1)
                if j == MIX["V_recip"]:
                    dve.wait_ge(ev(f"l{l}_root"), c + 1)
                    did(dve.reciprocal(n_c, n_c))
                if j == MIX["V_norm"]:
                    me.last()
                    link(dve.tensor_tensor(out=chunk, in0=chunk, in1=n_c, op=ALU.mult))
                    dve.tensor_scalar(chunk, chunk, cols[:, LN_W + l:LN_W + l + 1],
                                      cols[:, LN_B + l:LN_B + l + 1], ALU.mult, ALU.add)\
                       .then_inc(ev(f"l{l}_norm"), 1)

            def output(c, j):
                if j == OUT["V_h1"]:
                    dve.wait_ge(ev("o_product"), c + 1)
                    y = XT[:, ds(c * SC, SC)]
                    dve.scalar_tensor_tensor(out=y, in0=bank[3][:, 0:SC], scalar=cols[:, OUT_B:OUT_B + 1], in1=y,
                                             op0=ALU.add, op1=ALU.add).then_inc(ev("h1_ready"), 1)
                if j == OUT["V_centered"]:
                    dve.wait_ge(ev("o_mean"), c + 1)
                    dve.tensor_tensor(out=s_a, in0=XT[:, ds(c * SC, SC)], in1=bank[3][:, 0:SC],
                                      op=ALU.subtract).then_inc(ev("o_centered"), 1)
                if j == OUT["V_recip"]:
                    dve.wait_ge(ev("o_root"), c + 1)
                    did(dve.reciprocal(s_c, s_c))
                if j == OUT["V_xn"]:
                    me.last()
                    dve.tensor_tensor(out=XT[0:C, ds(c * SC, SC)], in0=s_a[0:C, :], in1=s_c[0:C, :], op=ALU.mult)\
                       .then_inc(ev("xn_ready"), 1)

            dve.wait_ge(s_const, CONSTS)
            for j in range(TI):
                s1(0, j)

            def make_onehot(t, k):
                dve.tensor_tensor(out=onehot[:, k % 8, :, :],
                                  in0=iota[:, :].unsqueeze(1).to_broadcast([P, 2, P]),
                                  in1=dst_lohi[:, ds(t, 1), :].rearrange("p a b -> p (a b)").unsqueeze(2)
                                  .to_broadcast([P, 2, P]), op=ALU.is_equal).then_inc(s_oh, 1)

            def keep_earlier(k):
                dve.tensor_tensor(out=earlier[:, k % 2, :], in0=bank[4 + k % 2][:, 0:P],
                                  in1=before[:, :], op=ALU.mult).then_inc(s_early, 1)

            for k in range(3):
                make_onehot(k, k)
            dve.wait_ge(s_pair, 1)
            keep_earlier(0)

            def iteration(l, i, beside):
                for j in range(TI):
                    dve.wait_ge(s_cnt, i * TI + (j + 1))
                    make_onehot(i * TI + (j + 3), j + 3)
                    dve.wait_ge(s_pair, i * TI + (j + 2))
                    keep_earlier(j + 1)
                    dve.wait_ge(s_rps, i * TI + (j + 1))
                    dve.tensor_tensor_reduce(out=junk[:, j % 2, :], in0=bank[6 + j % 2][:, 0:P],
                                             in1=onehot[:, j % 8, 1, :], scale=1.0, scalar=0.0,
                                             op0=ALU.mult, op1=ALU.add, accum_out=rank[:, j:j + 1])\
                       .then_inc(s_rk, 1)
                    if j % GS == GS - 1:
                        g = j // GS
                        part = slice(g * GS, g * GS + GS)
                        dve.wait_ge(s_rk, i * TI + (j + 1))
                        dve.wait_ge(s_sc[g], i * (GS * 16))
                        did(dve.tensor_scalar(over[:, :], rank[:, part], float(SLOTS), FAR, ALU.is_ge, ALU.mult))
                        lohi = dst_lohi[:, ds(i * TI + g * GS, GS), :]
                        link(dve.scalar_tensor_tensor(out=slot_f[:, :], in0=lohi[:, :, 1], scalar=float(P),
                                                      in1=lohi[:, :, 0], op0=ALU.mult, op1=ALU.add))
                        did(dve.scalar_tensor_tensor(out=slot_f[:, :], in0=slot_f[:, :],
                                                     scalar=float(SLOTS), in1=rank[:, part],
                                                     op0=ALU.mult, op1=ALU.add))
                        link(dve.tensor_scalar(src_st[:, part], src_ids[:, ds(i * TI + g * GS, GS)], 1.0, None, ALU.mult))
                        dve.tensor_tensor(out=slot_ix[:, part], in0=slot_f[:, :], in1=over[:, :], op=ALU.add)\
                           .then_inc(s_ix, 1)
                    mix(l, i - 32 * l, j)
                    if beside and l == 0:
                        s1(i + 1, j)
                    if beside and l == 1:
                        output(i - 33, j)
                link(dve.tensor_scalar(ranks[:, ds(i * TI, TI)], rank[:, :], 1.0, None, ALU.mult))

            STAGED = 4 * GR + 1 + 2 + 1
            with dve.Fori(0, 31) as i:
                me.enter(i * STAGED, STAGED)
                iteration(0, i, True)
            me.leave(31)
            iteration(0, 31, False)
            iteration(1, 32, False)
            with dve.Fori(33, 64) as i:
                me.enter((i - 33) * STAGED, STAGED)
                iteration(1, i, True)
            me.leave(31)
            for j in range(TI):
                output(31, j)

            def keep_h(c, k):
                dve.wait_ge(ev("gat_product"), c + 1)
                dve.tensor_scalar(rows[:, ds(c * 4, 4), HEADS:ROW],
                                  bank[4 + k][:, 0:4 * F].rearrange("p (q f) -> p q f", f=F), 1.0, None, ALU.mult)\
                   .then_inc(ev("gat_kept"), 1)

            with dve.Fori(0, NC // 2) as i:
                for k in range(2):
                    keep_h(i * 2 + k, k)
            keep_h(NC - 1, 0)

            did(dve.memset(window[:, :], 0.0))
            dve.tensor_copy(degrees[:, 0, :], bank[1][:, 0:NB]).then_inc(s_deg, 1)
            dve.wait_ge(s_deg, 2)
            did(dve.tensor_copy(block_degree[:, :], degrees[:, 1, :]))
            link(dve.tensor_reduce(out=degree[:, 0:1], in_=degrees[:, 1, :], axis=AX.X, op=ALU.max))
            link(dve.tensor_scalar(degree[:, 0:1], degree[:, 0:1], -1.0, None, ALU.add))
            link(dve.tensor_scalar(rounds_i[:, :], degree[:, 0:1], 0.5, 1.0 / SLOTS, ALU.add, ALU.mult))
            link(dve.tensor_copy(degree[:, 1:2], rounds_i[:, :]))
            link(dve.scalar_tensor_tensor(out=degree[:, 0:1], in0=degree[:, 1:2], scalar=-float(SLOTS),
                                          in1=degree[:, 0:1], op0=ALU.mult, op1=ALU.add))
            link(dve.tensor_scalar(degree[:, 0:1], degree[:, 0:1], 0.0, None, ALU.is_ge))
            dve.tensor_tensor(out=rounds_i[:, :], in0=degree[:, 1:2], in1=degree[:, 0:1], op=ALU.add)\
               .then_inc(s_rounds, 1)
            dve.wait_ge(s_rounds, 1)

            dve.wait_ge(ev("gat_kept"), NC)
            hh = rows[:, :, HEADS:ROW]

            def all_nodes(v):
                return vecs[:, v, :].unsqueeze(1).to_broadcast([P, NB, F])

            def per_head(a):
                return a.rearrange("p n (h j) -> p n h j", h=HEADS)

            me.last()
            did(dve.tensor_tensor(out=work[:, 0], in0=hh, in1=all_nodes(ATT_S), op=ALU.mult))
            link(dve.tensor_tensor(out=work[:, 1], in0=hh, in1=all_nodes(ATT_D), op=ALU.mult))
            did(dve.tensor_reduce(out=rows[:, :, 0:HEADS], in_=per_head(work[:, 0]), axis=AX.X, op=ALU.add))
            link(dve.tensor_reduce(out=adst[:, :, :], in_=per_head(work[:, 1]), axis=AX.X, op=ALU.add))
            did(dve.tensor_copy(acc[:, :, HEADS:ROW], hh))
            did(dve.memset(acc[:, :, 0:HEADS], 1.0))
            dve.tensor_tensor(out=mx[:, :, :], in0=rows[:, :, 0:HEADS], in1=adst[:, :, :], op=ALU.add)\
               .then_inc(ev("gat_kept"), 1)
            dve.wait_ge(ev("gat_kept"), NC + 1)
            link(dve.scalar_tensor_tensor(out=mx[:, :, :], in0=mx[:, :, :], scalar=0.2, in1=mx[:, :, :],
                                          op0=ALU.mult, op1=ALU.max))

            HK = HEADS * SLOTS

            def attend(me, b, k, nth):
                did, link = me.did, me.link
                a_d = adst[:, ds(b, 1), :].rearrange("p a h -> p (a h)")
                m_b = mx[:, ds(b, 1), :].rearrange("p a h -> p (a h)")
                den = acc[:, ds(b, 1), 0:HEADS].rearrange("p a h -> p (a h)")
                num = acc[:, ds(b, 1), HEADS:ROW].rearrange("p a f -> p (a f)")
                arg = parg[:, 0:HK].rearrange("p (h k) -> p h k", h=HEADS)
                m_new, s_den, s_num = small[:, 0, 0:HEADS], small[:, 1, 0:HEADS], small[:, 2, :]
                did(dve.tensor_scalar(pmask[:, :], EL[:, k, :], float(MP), NONE, ALU.is_ge, ALU.mult))
                link(dve.tensor_tensor(out=pe_[:, :, :], in0=G[:, k, :, 0:HEADS].rearrange("p k h -> p h k"),
                                       in1=a_d.unsqueeze(2).to_broadcast([P, HEADS, SLOTS]), op=ALU.add))
                link(dve.scalar_tensor_tensor(out=pe_[:, :, :], in0=pe_[:, :, :], scalar=0.2,
                                              in1=pe_[:, :, :], op0=ALU.mult, op1=ALU.max))
                link(dve.tensor_tensor(out=pe_[:, :, :], in0=pe_[:, :, :],
                                       in1=pmask[:, :].unsqueeze(1).to_broadcast([P, HEADS, SLOTS]),
                                       op=ALU.add))
                link(dve.tensor_reduce(out=small[:, 3, 0:HEADS], in_=pe_[:, :, :], axis=AX.X, op=ALU.max))
                link(dve.tensor_tensor(out=m_new, in0=small[:, 3, 0:HEADS], in1=m_b, op=ALU.max))
                did(dve.tensor_tensor(out=arg, in0=pe_[:, :, :],
                                      in1=m_new.unsqueeze(2).to_broadcast([P, HEADS, SLOTS]),
                                      op=ALU.subtract))
                dve.tensor_tensor(out=parg[:, HK:HK + HEADS], in0=m_b, in1=m_new, op=ALU.subtract)\
                   .then_inc(s_arg, 1)
                dve.wait_ge(s_arg, nth)
                did(dve.tensor_scalar(m_b, m_new, 1.0, None, ALU.mult))
                dve.wait_ge(s_exp, nth)
                pk = pexp[:, 0:HK].rearrange("p (h k) -> p h k", h=HEADS)
                old = pexp[:, HK:HK + HEADS]
                did(dve.tensor_tensor(out=msg.rearrange("p h j k -> p h j k"),
                                      in0=G[:, k, :, HEADS:ROW].rearrange("p k (h j) -> p h j k", h=HEADS),
                                      in1=pk.unsqueeze(2).to_broadcast([P, HEADS, EXPERTS, SLOTS]),
                                      op=ALU.mult))
                did(dve.tensor_reduce(out=s_den, in_=pk, axis=AX.X, op=ALU.add))
                did(dve.tensor_tensor(out=den, in0=den, in1=old, op=ALU.mult))
                did(dve.tensor_tensor(out=num.rearrange("p (h j) -> p h j", h=HEADS),
                                      in0=num.rearrange("p (h j) -> p h j", h=HEADS),
                                      in1=old.unsqueeze(2).to_broadcast([P, HEADS, EXPERTS]), op=ALU.mult))
                me.last()
                did(dve.tensor_reduce(out=s_num, in_=HS[:, 0:F * SLOTS].rearrange("p (f k) -> p f k", k=SLOTS),
                                      axis=AX.X, op=ALU.add))
                link(dve.tensor_tensor(out=den, in0=den, in1=s_den, op=ALU.add))
                me.did(dve.tensor_tensor(out=num, in0=num, in1=s_num, op=ALU.add))
                me.last()

            with dve.Fori(0, NB // 2) as i:
                me.enter(i * (2 * ATT_STEPS), 2 * ATT_STEPS)
                for k in range(2):
                    dve.wait_ge(s_ga[k], i * (16 * SLOTS) + 16 * SLOTS)
                    attend(me, i * 2 + k, k, i * 2 + (k + 1))
                    dve.tensor_copy(order[:, 0:1], small[:, 0, 0:1]).then_inc(s_used, 1)
            me.leave(NB // 2)

            rounds = dve.value_load(rounds_i[0:1, 0:1], min_val=0, max_val=MAX_ROUNDS)
            with dve.If(rounds > 1):
                again = Steps(dve, s_dve_round)
                with dve.Fori(1, rounds) as r:
                    per_round = 1 + RG * 5 + NB * ATT_STEPS
                    again.enter((r - 1) * per_round, per_round)
                    again.did(dve.tensor_scalar(window[:, :], window[:, :], float(SLOTS), None, ALU.add))
                    with dve.Fori(0, RG) as g:
                        again.enter((r - 1) * per_round + g * 5, 5)
                        lohi = dst_lohi[:, ds(g * GS, GS), :]
                        dve.wait_ge(s_dve_round, (r - 1) * per_round + 1)
                        dve.wait_ge(s_round_put, (r - 1) * RG + g)
                        again.did(dve.tensor_scalar(src_st[:, 0:GS], src_ids[:, ds(g * GS, GS)], 1.0, None, ALU.mult))
                        again.did(dve.scalar_tensor_tensor(out=slot_f[:, :], in0=lohi[:, :, 1], scalar=float(P),
                                                           in1=lohi[:, :, 0], op0=ALU.mult, op1=ALU.add))
                        again.link(dve.tensor_scalar(rank[:, 0:GS], ranks[:, ds(g * GS, GS)], window[:, 0:1], None,
                                                     ALU.subtract))
                        again.did(dve.tensor_scalar(over[:, :], rank[:, 0:GS], float(SLOTS), FAR, ALU.is_ge,
                                                    ALU.mult))
                        dve.tensor_scalar(rank[:, GS:2 * GS], rank[:, 0:GS], 0.0, FAR, ALU.is_lt, ALU.mult)\
                           .then_inc(s_round_part, 1)
                        dve.wait_ge(s_round_part, ((r - 1) * RG + g) * 3 + 1)
                        again.link(dve.tensor_tensor(out=over[:, :], in0=over[:, :], in1=rank[:, GS:2 * GS],
                                                     op=ALU.max))
                        dve.scalar_tensor_tensor(out=slot_f[:, :], in0=slot_f[:, :], scalar=float(SLOTS),
                                                 in1=rank[:, 0:GS], op0=ALU.mult, op1=ALU.add)\
                           .then_inc(s_round_part, 1)
                        dve.wait_ge(s_round_part, ((r - 1) * RG + g) * 3 + 2)
                        dve.tensor_scalar(slot_f[:, :], slot_f[:, :], -FAR / 2, FAR - 1, ALU.max, ALU.min)\
                           .then_inc(s_round_part, 1)
                        dve.wait_ge(s_round_part, ((r - 1) * RG + g) * 3 + 3)
                        dve.tensor_tensor(out=slot_ix[:, 0:GS], in0=slot_f[:, :], in1=over[:, :], op=ALU.add)\
                           .then_inc(s_round_ix, 1)
                    again.leave(RG)
                    with dve.Fori(0, NB) as b:
                        again.enter((r - 1) * per_round + b * ATT_STEPS, ATT_STEPS)
                        dve.wait_ge(s_round_rows, (r - 1) * NB + b + 1)
                        attend(again, b, 0, r * NB + b + 1)
                        dve.tensor_copy(order[:, 0:1], small[:, 0, 0:1]).then_inc(s_round_used, 1)
                    again.leave(NB)
                    again.leave(1)


            W = [work[:, k] for k in range(4)]
            den_all = acc[:, :, 0:HEADS]
            dve.wait_ge(ev("expert_kept"), 4 * NC)
            sc4 = small4
            link(dve.tensor_scalar(sc4[:, 0], den_all, 1e-16, None, ALU.add))
            link(dve.reciprocal(sc4[:, 0], sc4[:, 0]))
            link(dve.tensor_tensor(out=per_head(W[0]), in0=per_head(acc[:, :, HEADS:ROW]),
                                   in1=sc4[:, 0].unsqueeze(3).to_broadcast([P, NB, HEADS, EXPERTS]), op=ALU.mult))
            link(dve.tensor_tensor(out=W[0], in0=W[0], in1=all_nodes(BGAT), op=ALU.add))
            link(dve.tensor_reduce(out=gm[:, 0, :], in_=W[0], axis=AX.X, op=ALU.add))
            link(dve.tensor_scalar(gm[:, 0, :], gm[:, 0, :], 1.0 / F, None, ALU.mult))
            link(dve.tensor_tensor(out=W[0], in0=W[0], in1=gm[:, 0, :].unsqueeze(2).to_broadcast([P, NB, F]),
                                   op=ALU.subtract))
            link(dve.tensor_tensor(out=W[1], in0=W[0], in1=W[0], op=ALU.mult))
            link(dve.tensor_reduce(out=gm[:, 0, :], in_=W[1], axis=AX.X, op=ALU.add))
            dve.tensor_scalar(gm[:, 0, :], gm[:, 0, :], 1.0 / F, None, ALU.mult).then_inc(ev("gate_var"), 1)
            dve.wait_ge(ev("gate_root"), 1)
            link(dve.reciprocal(gm[:, 2, :], gm[:, 1, :]))
            link(dve.tensor_tensor(out=W[0], in0=W[0], in1=gm[:, 2, :].unsqueeze(2).to_broadcast([P, NB, F]),
                                   op=ALU.mult))
            link(dve.tensor_tensor(out=W[0], in0=W[0], in1=all_nodes(GAMMA), op=ALU.mult))
            link(dve.tensor_tensor(out=W[0], in0=W[0], in1=all_nodes(BETA), op=ALU.add))
            link(dve.tensor_reduce(out=sc4[:, 0], in_=W[0].rearrange("p n (h j) -> p n j h", h=HEADS),
                                   axis=AX.X, op=ALU.add))
            link(dve.tensor_scalar(sc4[:, 0], sc4[:, 0], 1.0 / HEADS, None, ALU.mult))

            def best(top, pick):
                link(dve.tensor_reduce(out=top, in_=sc4[:, 0], axis=AX.X, op=ALU.max))
                link(dve.tensor_tensor(out=sc4[:, 2], in0=sc4[:, 0],
                                       in1=top.unsqueeze(2).to_broadcast([P, NB, EXPERTS]), op=ALU.is_equal))
                link(dve.tensor_tensor(out=sc4[:, 2], in0=sc4[:, 2],
                                       in1=order[:, :].unsqueeze(1).to_broadcast([P, NB, EXPERTS]), op=ALU.mult))
                link(dve.tensor_reduce(out=gm[:, 3, :], in_=sc4[:, 2], axis=AX.X, op=ALU.max))
                link(dve.tensor_tensor(out=pick, in0=sc4[:, 2],
                                       in1=gm[:, 3, :].unsqueeze(2).to_broadcast([P, NB, EXPERTS]),
                                       op=ALU.is_equal))

            for e in range(EXPERTS):
                did(dve.memset(order[:, e:e + 1], float(EXPERTS - e)))
            me.last()
            best(gm[:, 1, :], sc4[:, 1])
            link(dve.tensor_scalar(sc4[:, 2], sc4[:, 1], NONE, None, ALU.mult))
            link(dve.tensor_tensor(out=sc4[:, 0], in0=sc4[:, 0], in1=sc4[:, 2], op=ALU.add))
            best(gm[:, 2, :], sc4[:, 3])
            dve.tensor_tensor(out=gm[:, 0, :], in0=gm[:, 2, :], in1=gm[:, 1, :], op=ALU.subtract)\
               .then_inc(ev("gate_arg"), 1)
            dve.wait_ge(ev("gate_exp"), 1)
            link(dve.tensor_scalar(gm[:, 2, :], gm[:, 1, :], 1.0, None, ALU.add))
            link(dve.reciprocal(gm[:, 2, :], gm[:, 2, :]))
            link(dve.tensor_tensor(out=gm[:, 3, :], in0=gm[:, 1, :], in1=gm[:, 2, :], op=ALU.mult))
            did(dve.tensor_tensor(out=sc4[:, 1], in0=sc4[:, 1],
                                  in1=gm[:, 2, :].unsqueeze(2).to_broadcast([P, NB, EXPERTS]), op=ALU.mult))
            link(dve.tensor_tensor(out=sc4[:, 3], in0=sc4[:, 3],
                                   in1=gm[:, 3, :].unsqueeze(2).to_broadcast([P, NB, EXPERTS]), op=ALU.mult))
            dve.tensor_tensor(out=sc4[:, 0], in0=sc4[:, 1], in1=sc4[:, 3], op=ALU.add).then_inc(ev("gate_ready"), 1)
            dve.wait_ge(ev("gate_ready"), 1)

            h1 = X[:, 0:NB * C].rearrange("p (n c) -> p n c", c=C)
            for p in range(PIECES):
                part = back[p].rearrange("p (n e c) -> p n e c", e=EXPERTS, c=C)
                n0 = p * PN
                dve.wait_ge(s_back[p % 3], 16 * (p // 3 + 1))
                link(dve.tensor_tensor(out=part, in0=part, in1=sc4[:, 0, n0:n0 + PN, :].unsqueeze(3)
                                       .to_broadcast([P, PN, EXPERTS, C]), op=ALU.mult))
                link(dve.tensor_tensor(out=part[:, :, 0:2, :], in0=part[:, :, 0:2, :], in1=part[:, :, 2:4, :],
                                       op=ALU.add))
                link(dve.tensor_tensor(out=part[:, :, 0, :], in0=part[:, :, 0, :], in1=part[:, :, 1, :], op=ALU.add))
                dve.tensor_tensor(out=h1[:, n0:n0 + PN, :], in0=h1[:, n0:n0 + PN, :], in1=part[:, :, 0, :],
                                  op=ALU.add).then_inc(ev("out_ready"), 1)

        @block.tensor
        def _(pe):
            mm = nc.tensor.matmul

            def s1(c, j):
                at3 = bank[3][:, 0:SC]
                if j < TAPS // 2:
                    if j == 0:
                        pe.wait_ge(ev("x1_ready"), c)
                    ins = mm(at3, wr[:, j, :], XT[:, ds(c * SC + 2 * j * B, SC)],
                             start=(j == 0), stop=(j == TAPS // 2 - 1))
                    if j == TAPS // 2 - 1:
                        ins.then_inc(ev("conv_ready"), 1)
                if j == S1["P_mean"]:
                    pe.wait_ge(ev("y_ready"), c + 1)
                    mm(at3, mean64[:, :], XT[:, ds(c * SC, SC)], start=True, stop=True).then_inc(ev("s1_mean"), 1)
                if j == S1["P_var"]:
                    pe.wait_ge(ev("s1_square"), c + 1)
                    mm(at3, mean64[:, :], s_b, start=True, stop=True).then_inc(ev("s1_var"), 1)
                if j == S1["P_in"]:
                    pe.wait_ge(ev("s1_norm"), c + 1)
                    mm(at3, inw[:, :], s_b, start=True, stop=True).then_inc(ev("s1_in"), 1)

            def mix(l, c, j):
                at0 = bank[0][:, 0:SC]
                if j == MIX["P_mix"]:
                    pe.wait_ge(s_h, c * STEPS + (l * TP + STEPS))
                    mm(at0, cw[:, l, :], HS[:, ds(c * SC + B, SC)], start=True, stop=False)
                    mm(at0, dw[:, l, :], X[:, ds(c * SC, SC)], start=False, stop=True).then_inc(ev(f"l{l}_mix"), 1)
                if j == MIX["P_mean"]:
                    pe.wait_ge(ev(f"l{l}_sum"), c + 1)
                    mm(at0, mean128[:, :], X[:, ds(c * SC, SC)], start=True, stop=True)\
                        .then_inc(ev(f"l{l}_mean"), 1)
                if j == MIX["P_var"]:
                    pe.wait_ge(ev(f"l{l}_square"), c + 1)
                    mm(at0, mean128[:, :], n_b, start=True, stop=True).then_inc(ev(f"l{l}_var"), 1)

            def output(c, j):
                at3 = bank[3][:, 0:SC]
                if j == OUT["P_out"]:
                    pe.wait_ge(ev("xn_ready"), c)
                    pe.wait_ge(ev("l1_norm"), c + 1)
                    mm(at3, outw[:, :], X[:, ds(c * SC, SC)], start=True, stop=True).then_inc(ev("o_product"), 1)
                if j == OUT["P_mean"]:
                    pe.wait_ge(ev("h1_ready"), c + 1)
                    mm(at3, mean64[:, :], XT[:, ds(c * SC, SC)], start=True, stop=True).then_inc(ev("o_mean"), 1)
                if j == OUT["P_var"]:
                    pe.wait_ge(ev("o_square"), c + 1)
                    mm(at3, mean64[:, :], s_b, start=True, stop=True).then_inc(ev("o_var"), 1)

            pe.wait_ge(s_const, CONSTS)
            mm(bank[1][:, 0:P], space[0:1, 0:P], ones_row[:, 0:P], start=True, stop=True).then_inc(s_cnt, 1)
            pe.wait_ge(s_x[0], 16)
            pe.wait_ge(s_x[1], 16)
            pe.wait_ge(s_weff, 3)
            for j in range(TI):
                s1(0, j)

            def turn(k):
                nc.tensor.transpose(bank[2][:, :].bitcast(bf16)[:, 0:P],
                                    onehot[:, k % 8, 0, :], ident_b[:, :]).then_inc(s_tr, 1)

            def pairs(k):
                mm(bank[4 + k % 2][:, 0:P], onehot_T[:, k % 4, :], onehot_T[:, k % 4, :],
                   start=True, stop=True).then_inc(s_pair, 1)

            pe.wait_ge(s_oh, 1)
            turn(0)
            pe.wait_ge(s_te, 1)
            pairs(0)
            pe.wait_ge(s_oh, 2)
            turn(1)

            def iteration(l, i, beside):
                c = i - 32 * l
                if l == 0:
                    pe.wait_ge(ev("x1_ready"), c + 1)
                    pe.wait_ge(ev("l0_root"), c)
                elif isinstance(i, int):
                    pe.wait_ge(ev("l0_norm"), 32)
                else:
                    pe.wait_ge(ev("l1_root"), c)
                mm(bank[0][:, 0:SC], bw[:, l, :], X[:, ds(c * SC, SC)], start=True, stop=False)
                mm(bank[0][:, 0:SC], brow[:, l * H:(l + 1) * H], ones_row[:, 0:SC], start=False, stop=True)
                col0 = c * SC if isinstance(i, int) else pe.snap(c * SC)
                for j in range(TI):
                    if j < STEPS:
                        if j:
                            pe.wait_ge(s_h, i * STEPS + j)
                        mm(bank[0][:, j * B:j * B + B], aw[:, l, :], HS[:, ds(col0 + j * B, B)],
                           start=False, stop=True, skip_group_check=True).then_inc(s_pre, 1)
                    mix(l, c, j)
                    if beside and l == 0:
                        s1(i + 1, j)
                    if beside and l == 1:
                        output(i - 33, j)
                    pe.wait_ge(s_te, i * TI + (j + 2))
                    pairs(j + 1)
                    pe.wait_ge(s_oh, i * TI + (j + 3))
                    turn(j + 2)
                    pe.wait_ge(s_early, i * TI + (j + 1))
                    pe.wait_ge(s_cc, i * TI + (j + 1))
                    r = bank[6 + j % 2][:, 0:P]
                    mm(r, onehot_T[:, j % 4, :], counts[:, j % 2, :], start=True, stop=False)
                    mm(r, earlier[:, j % 2, :], onehot[:, j % 8, 1, :], start=False, stop=True)\
                        .then_inc(s_rps, 1)
                    mm(bank[1][:, 0:P], onehot[:, j % 8, 0, :], onehot[:, j % 8, 1, :],
                       start=False, stop=True, skip_group_check=True).then_inc(s_cnt, 1)

            with pe.Fori(0, 31) as i:
                iteration(0, i, True)
            iteration(0, 31, False)
            iteration(1, 32, False)
            with pe.Fori(33, 64) as i:
                iteration(1, i, True)
            for j in range(TI):
                output(31, j)

            def gat(c, k):
                pe.wait_ge(ev("xn_staged"), c + 1)
                for q in range(4):
                    last = mm(bank[4 + k][:, q * F:(q + 1) * F], turned_in[k][:, q * P:(q + 1) * P], wgat[:, :],
                              start=True, stop=True)
                last.then_inc(ev("gat_product"), 1)

            pe.wait_ge(s_early, ITERS * TI + 1)
            gat(0, 0)
            gat(1, 1)
            with pe.Fori(1, NC // 2) as i:
                for k in range(2):
                    pe.wait_ge(ev("gat_kept"), i * 2 + (k - 1))
                    gat(i * 2 + k, k)
            pe.wait_ge(ev("gat_kept"), NC - 2)
            gat(NC - 1, 0)

            pe.wait_ge(s_deg, 1)
            pe.wait_ge(s_rk, ITERS * TI)
            pe.wait_ge(s_te, ITERS * TI + 2)
            pe.wait_ge(ev("gat_kept"), NC + 1)
            with pe.Fori(0, NC) as c:
                pe.wait_ge(ev("expert_kept"), c * 4)
                pe.wait_ge(ev("h1_staged"), c + 1)
                for q in range(4):
                    last = nc.tensor.transpose(bank[4][:, q * P:(q + 1) * P], turned_in[0][:, q * P:(q + 1) * P],
                                               ident[:, :])
                last.then_inc(ev("h1_turned"), 1)
                for e in range(EXPERTS):
                    pe.wait_ge(ev("hidden_ready"), c * EXPERTS + e)
                    mm(bank[e][:, :], w1s[:, e, :], XT[:, ds(c * CH, CH)], start=True, stop=True)\
                        .then_inc(ev("hidden_product"), 1)
                pe.wait_ge(ev("hidden_ready"), c * EXPERTS + EXPERTS)
                pe.wait_ge(ev("h1_kept"), c + 1)
                for q in range(4):
                    for e in range(EXPERTS):
                        mm(bank[4 + q][:, e * C:(e + 1) * C], hid[:, e, q * P:(q + 1) * P], w2s[:, e, :],
                           start=True, stop=False)
                        last = mm(bank[4 + q][:, e * C:(e + 1) * C], ones_row[:, 0:P],
                                  b2row[:, e * C:(e + 1) * C], start=False, stop=True)
                    last.then_inc(ev("expert_product"), 1)



_INS = ["x_t", "conv_wr", "conv_wi", "phases", "in_w", "in_b", "a_w", "b_w", "b_b", "c_w", "c_b", "d_w", "d_b",
        "ln_w", "ln_b", "out_w", "out_b", "w_gat", "att_src", "att_dst", "b_gat", "gamma", "beta",
        "w1", "b1", "w2", "b2", "edges"]


def _laid_out(i):
    import numpy as np

    a = {k.removeprefix("L0_"): np.asarray(v) for k, v in i.items()}
    P = 128

    def taps(w):
        return w.transpose(1, 2, 0).reshape(64, 8, 2, 64).transpose(2, 0, 1, 3).reshape(P, 8, 64)

    def turned(w):
        return w.transpose(2, 0, 1)

    return {
        "x_t": a["x"].transpose(2, 1, 0).reshape(64, 750 * 16),
        "conv_wr": taps(a["tok_w_real"]), "conv_wi": taps(a["tok_w_imag"]),
        "phases": np.repeat(a["tok_phases"].reshape(8, 2).T, 64, axis=0),
        "in_w": a["attn_in_W"].T, "in_b": a["attn_in_b"],
        "a_w": turned(a["attn_A_W"]), "b_w": turned(a["attn_B_W"]), "b_b": a["attn_B_b"].reshape(1, 256),
        "c_w": turned(a["attn_C_W"]), "c_b": a["attn_C_b"].T, "d_w": turned(a["attn_D_W"]), "d_b": a["attn_D_b"].T,
        "ln_w": a["attn_ln_w"].T, "ln_b": a["attn_ln_b"].T,
        "out_w": a["attn_out_W"].T, "out_b": a["attn_out_b"],
        "w_gat": a["ffn_W_gat"], "att_src": a["ffn_att_src"].reshape(16), "att_dst": a["ffn_att_dst"].reshape(16),
        "b_gat": a["ffn_b_gat"], "gamma": a["ffn_ln_gamma"], "beta": a["ffn_ln_beta"],
        "w1": a["ffn_W1"].transpose(1, 0, 2), "b1": a["ffn_b1"].T,
        "w2": a["ffn_W2"].transpose(1, 0, 2), "b2": a["ffn_b2"].reshape(1, 256),
        "edges": a["ffn_edge_index"].reshape(2, P, -1).transpose(1, 0, 2).reshape(P, -1),
    }


def kernel(**inputs):
    import numpy as np
    import concourse.bacc as bacc
    from concourse.bass_utils import run_bass_kernel_spmd

    laid = _laid_out(inputs)
    nc = bacc.Bacc("TRN2", target_bir_lowering=False, num_devices=1)
    arrays, args = {}, []
    for name in _INS:
        a = np.ascontiguousarray(laid[name])
        arrays[f"in_{name}"] = a
        args.append(nc.dram_tensor(f"in_{name}", a.shape, mybir.dt.from_np(a.dtype), kind="ExternalInput").ap())
    out = nc.dram_tensor("out_h", (16, 735, 64), mybir.dt.float32, kind="ExternalOutput").ap()
    audio_tower_program(nc, *args, out)
    r = run_bass_kernel_spmd(nc, [arrays], core_ids=[0])
    return r.results[0]["out_h"]
```

```python
import concourse.bass as bass
from concourse import mybir
from contextlib import ExitStack


def audio_tower_program(nc, x_t, conv_wr, conv_wi, phases, in_w, in_b, a_w, b_w, b_b, c_w, c_b, d_w, d_b,
                        ln_w, ln_b, out_w, out_b, w_gat, att_src, att_dst, b_gat, gamma, beta,
                        w1, b1, w2, b2, edges, out):
    fp32, bf16 = mybir.dt.float32, mybir.dt.bfloat16
    u32, i32 = mybir.dt.uint32, mybir.dt.int32
    ALU, ACT, AX = mybir.AluOpType, mybir.ActivationFunctionType, mybir.AxisListType
    ds = bass.ds

    P = 128
    B, T, C, H = 16, 735, 64, 128
    TAPS = 16
    TP = 736
    M = B * T
    MP = B * TP
    NB = MP // P
    XC = 750 * B
    CH = 512
    NC = MP // CH
    HEADS, EXPERTS = 4, 4
    F = HEADS * EXPERTS
    ROW = HEADS + F
    SLOTS = 40
    RS = SLOTS + ROW + HEADS
    NE = edges.shape[1] * P // 2
    ET = NE // P
    ITERS = 64
    TI = ET // ITERS
    STEPS = 2 * TP // ITERS
    SC = STEPS * B
    GR, GS = 2, TI // 2
    FAR = float(1 << 23)
    EMPTY = 16383
    EPS = 1e-5
    NONE = -1e30
    assert NC * CH == MP and TI * ITERS == ET and STEPS * ITERS == 2 * TP and SC <= 512

    ell = nc.dram_tensor("ell", (MP * RS, 1), u32, kind="Internal").ap()
    ell_rows = ell.rearrange("(m k) o -> m (k o)", k=RS)
    perm_out = nc.dram_tensor("perm", (MP, 1), u32, kind="Internal").ap()
    gates_out = nc.dram_tensor("gates", (MP, EXPERTS), fp32, kind="Internal").ap()
    table = nc.dram_tensor("node_rows", (MP, ROW), fp32, kind="Internal").ap()
    experts_out = nc.dram_tensor("experts_out", (P, NB * EXPERTS * C), fp32, kind="Internal").ap()

    ctx = ExitStack()
    with ctx:
        def sb(name, shape, dt=fp32):
            return ctx.enter_context(nc.sbuf_tensor(name, shape, dt))

        def sem(name):
            return ctx.enter_context(nc.semaphore(name))

        XT = sb("XT", [P, XC])
        X = sb("X", [P, MP])
        HS = sb("HS", [P, B + MP])
        src_ids = sb("src_ids", [P, ET], mybir.dt.uint16)
        dst_lohi = sb("dst_lohi", [P, ET + 8, 2], bf16)
        ranks = sb("ranks", [P, ET])
        rows = sb("rows", [P, NB, ROW])
        adst = sb("adst", [P, NB, HEADS])

        free_at = [NB * C]

        def in_x(*dims):
            n = 1
            for d in dims:
                n *= d
            part = X[:, free_at[0]:free_at[0] + n]
            free_at[0] += n
            assert free_at[0] <= MP
            if len(dims) == 1:
                return part
            letters = "abcd"[:len(dims)]
            return part.rearrange(f"p ({' '.join(letters)}) -> p {' '.join(letters)}",
                                  **dict(zip(letters[1:], dims[1:])))

        acc = in_x(NB, ROW)
        mx = in_x(NB, HEADS)
        G = in_x(2, SLOTS, ROW)
        small4 = in_x(4, NB, EXPERTS)
        gm = in_x(4, NB)

        wr = sb("wr", [P, TAPS // 2, P])
        wi = sb("wi", [P, TAPS // 2, C])
        ph = sb("ph", [P, TAPS // 2])
        trig = sb("trig", [P, 4, TAPS // 2])
        trig_i = sb("trig_i", [P, 2, TAPS // 2], i32)
        inw = sb("inw", [P, H])
        aw, bw, cw, dw = [sb(n, [P, 2, H]) for n in ("aw", "bw", "cw", "dw")]
        cols = sb("cols", [P, 18])
        outw = sb("outw", [P, P])
        wgat = sb("wgat", [P, F])
        vecs = sb("vecs", [P, 5, F])
        w1s = sb("w1s", [P, EXPERTS, H])
        w2s = sb("w2s", [P, EXPERTS, C])
        b2row = sb("b2row", [1, EXPERTS * C])

        iota = sb("iota", [P, P], bf16)
        ident = sb("ident", [P, P])
        ident_b = sb("ident_b", [P, P], bf16)
        before = sb("before", [P, P])
        ones_row = sb("ones_row", [1, CH])
        mean64 = sb("mean64", [P, P])
        mean128 = sb("mean128", [P, P])
        eps_col = sb("eps_col", [P, 1])

        onehot = sb("onehot", [P, 8, 2, P], bf16)
        onehot_T = sb("onehot_T", [P, 4, P])
        earlier = sb("earlier", [P, 2, P], bf16)
        counts = sb("counts", [P, 2, P])
        junk = sb("junk", [P, 2, NB], bf16)
        rank = sb("rank", [P, TI])
        over = sb("over", [P, GS])
        slot_f = sb("slot_f", [P, GS])
        slot_ix = sb("slot_ix", [P, TI], u32)
        src_st = sb("src_st", [P, TI], u32)

        space = sb("space", [P, 5 * SC])
        s_b, s_c, n_b, n_c, s_n = [space[:, k * SC:(k + 1) * SC] for k in range(5)]
        turned_in = [space[:, k * CH:(k + 1) * CH] for k in range(2)]

        EL = sb("EL", [P, 4, RS], u32)
        EL_f = EL[:, :, :].bitcast(fp32)
        perm = sb("perm_in", [P, NB + 4], u32)
        px = sb("px", [P, 4], u32)
        gate_st = sb("gate_st", [P, 4, EXPERTS])
        FILL = HS[:, 2 * ET:2 * ET + NB * RS].bitcast(u32)
        CONSTS = 18
        INIT_STEPS = 4
        ATT_STEPS = 15
        RG = ET // GS
        MAX_ROUNDS = -(-ET * P // SLOTS)
        window = sb("window", [P, 1])
        degree = sb("degree", [P, 2])
        degrees = sb("degrees", [P, 2, NB])
        block_degree = sb("block_degree", [P, NB], i32)
        rounds_i = sb("rounds_i", [P, 1], i32)
        s_rounds = sem("rounds_known")
        s_deg = sem("degree_ready")
        s_dve_round = sem("vector_round_step")
        s_round_part = sem("round_index_step")
        s_round_empty = sem("round_table_emptied")
        s_round_ix = sem("round_indices_ready")
        s_round_sc = sem("round_scattered")
        s_round_put = sem("round_group_scattered")
        s_round_el = sem("round_slots_loaded")
        s_round_ga = sem("round_rows_gathered")
        s_round_rows = sem("round_block_gathered")
        past = max(2 * ET + NB * RS, F * SLOTS + 4 * NB * F)
        pexp, parg = [HS[:, past + k * HEADS * (SLOTS + 1):past + (k + 1) * HEADS * (SLOTS + 1)] for k in range(2)]
        pmask = sb("pmask", [P, SLOTS])
        pe_ = sb("pe_", [P, HEADS, SLOTS])
        small = sb("small", [P, 4, F])
        work = HS[:, F * SLOTS:F * SLOTS + 4 * NB * F].rearrange("p (k n f) -> p k n f", k=4, f=F)
        hid = HS[:, F * SLOTS:F * SLOTS + EXPERTS * CH].rearrange("p (e c) -> p e c", e=EXPERTS)
        stage_at = past + 2 * HEADS * (SLOTS + 1)
        G2_at = F * SLOTS + EXPERTS * CH
        G2 = HS[:, G2_at:G2_at + 2 * SLOTS * ROW].rearrange("p (k s f) -> p k s f", k=2, f=ROW)
        rows_of = [G[:, 0], G[:, 1], G2[:, 0], G2[:, 1]]
        assert G2_at + 2 * SLOTS * ROW <= past
        out_stage = HS[:, stage_at:stage_at + 4 * EXPERTS * C]
        PIECES = 4
        PN = NB // PIECES
        PW = PN * EXPERTS * C
        back = [XT[:, 0:PW], XT[:, PW:2 * PW], HS[:, 0:PW], XT[:, 0:PW]]
        msg = HS[:, 0:F * SLOTS].rearrange("p (h j k) -> p h j k", h=HEADS, k=SLOTS)
        order = sb("order", [P, EXPERTS])

        bank = [ctx.enter_context(nc.psum_tensor(f"bank{k}", [P, 512], fp32)) for k in range(8)]

        IN_B, C_B, D_B, LN_W, LN_B, OUT_B, B1, CD_B, B_B = 0, 1, 3, 5, 7, 9, 10, 14, 16
        ATT_S, ATT_D, BGAT, GAMMA, BETA = range(5)

        s_par = sem("params_loaded")
        s_edge = sem("edges_loaded")
        s_x = [sem(f"x_loaded{k}") for k in range(2)]
        s_const = sem("constants_made")
        s_ellfill = sem("ell_filled_sbuf")
        s_ell0 = sem("ell_emptied")
        s_dve = sem("vector_step")
        s_act = sem("scalar_step")
        s_weff = sem("conv_weights_ready")
        s_prep = sem("edges_prepared")

        s_oh = sem("onehot_ready")
        s_tr = sem("onehot_transposed")
        s_te = sem("onehot_T_copied")
        s_pair = sem("pairs_ready")
        s_early = sem("earlier_ready")
        s_rps = sem("rank_products_ready")
        s_cnt = sem("counts_updated")
        s_cc = sem("counts_copied")
        s_rk = sem("ranks_ready")
        s_ix = sem("slot_indices_ready")
        s_sc = [sem(f"scattered{g}") for g in range(GR)]
        s_bx = sem("scan_input_ready")
        s_pre = sem("scan_product_ready")
        s_h = sem("state_ready")
        s_tab = sem("table_stored")
        s_el = [sem(f"slots_loaded{k}") for k in range(4)]
        s_self = sem("self_rows_stored")
        s_px = sem("first_rows_known")
        s_round_px = sem("round_rows_known")
        s_perm_ix, s_gate_ix = sem("perm_indices_ready"), sem("gate_indices_ready")
        s_perm_sc = [sem(f"perm_scattered{k}") for k in range(2)]
        s_gate_sc = [sem(f"gates_scattered{k}") for k in range(2)]
        s_perm_in, s_gate_in = sem("perm_loaded"), sem("gates_loaded")
        s_ga = [sem(f"rows_gathered{k}") for k in range(4)]
        s_used = sem("rows_used")
        s_arg = sem("exp_arguments_ready")
        s_exp = sem("exp_ready")
        s_parked = sem("experts_out_stored")
        s_back = [sem(f"experts_out_loaded{k}") for k in range(3)]
        s_out = sem("out_stored")

        block = ctx.enter_context(nc.Block())

        class Steps:

            def __init__(self, eng, sem):
                self.eng, self.sem, self.n, self.off, self.loops = eng, sem, 0, None, []

            def did(self, ins):
                ins.then_inc(self.sem, 1)
                self.n += 1
                return ins

            def last(self):
                self.eng.wait_ge(self.sem, self.n if self.off is None else self.off + self.n)

            def link(self, ins):
                self.did(ins)
                self.last()

            def enter(self, off, per):
                self.loops.append((self.off, per, self.n))
                self.off = off

            def leave(self, times):
                self.off, per, at = self.loops.pop()
                assert self.n - at == per, (self.n - at, per)
                self.n = at + times * per

        names = {}

        def ev(name):
            if name not in names:
                names[name] = sem(name)
            return names[name]

        for n in ("conv_ready", "y_ready", "s1_square", "s1_var", "s1_root", "s1_norm",
                  "s1_in", "x1_ready"):
            ev(n)
        for l in range(2):
            for n in ("mix", "centered", "square", "var", "root", "norm"):
                ev(f"l{l}_{n}")
        for n in ("o_product", "h1_ready", "bias_means", "biases_ready", "o_square", "o_var", "o_root", "xn_ready",
                  "xn_staged", "gat_product", "gat_kept", "hist_ready", "hist_sums", "sorted", "h1_staged", "h1_turned", "h1_kept"):
            ev(n)
        for n in ("hidden_product", "hidden_ready", "expert_product", "expert_kept", "gate_ready",
                  "gate_root", "gate_var", "gate_arg", "gate_exp", "out_ready"):
            ev(n)

        NPAR = 28

        LATER = TI
        CK = 32
        S1 = dict(P_conv=0, A_y=8, P_var=10, A_root=27, V_recip=LATER, V_norm=LATER + 8, P_in=LATER + 29, A_x1=LATER + 29)
        MIX = dict(P_mix=23, A_centered=24, P_var=26, A_root=27, V_recip=LATER + 4, V_norm=LATER + 9, V_affine=LATER + 10)
        OUT = dict(P_out=24, V_h1=24, A_square=25, P_var=27, A_root=28, V_recip=LATER, V_xn=LATER + 8)

        SCHEDULE = [("s1", -2, 0), ("s1", -1, LATER), ("mix0", 0, 0), ("mix0", 1, LATER),
                    ("mix1", CK, 0), ("mix1", CK + 1, LATER), ("output", CK + 1, 0), ("output", CK + 2, LATER)]
        BEFORE, AFTER = (-2, -1), (2 * CK, 2 * CK + 1)
        RANGES = [(0, 1), (1, CK - 2), (CK - 2, CK - 1), (CK - 1, CK), (CK, CK + 1), (CK + 1, CK + 2),
                  (CK + 2, 2 * CK)]

        def beside(first, i, j, stages):
            for name, start, slot0 in SCHEDULE:
                if 0 <= first - start < CK:
                    stages[name](i - start, j + slot0)

        def over_ranges(eng, iteration, me=None, per=0):
            for first, end in RANGES:
                if end == first + 1:
                    iteration(first, first)
                else:
                    with eng.Fori(first, end) as i:
                        if me:
                            me.enter((i - first) * per, per)
                        iteration(first, i)
                    if me:
                        me.leave(end - first)

        @block.sync
        def _(sp):
            sp.dma_start(HS[:, 0:2 * ET].bitcast(i32), edges).then_inc(s_edge, 16)
            sp.dma_start(XT[0:C, :], x_t).then_inc(s_x[0], 16)
            sp.dma_start(XT[C:P, 0:XC - B], x_t[:, B:XC]).then_inc(s_x[1], 16)

            sp.wait_ge(s_perm_ix, NB // 2)
            for k in range(2):
                sp.wait_ge(s_perm_sc[k], NB // 2 * 16)
            sp.dma_start(perm[:, 0:NB], perm_out.rearrange("(p b) o -> p (b o)", p=P)).then_inc(s_perm_in, 16)

            def bring(p):
                sp.dma_start(back[p], experts_out[:, p * PW:(p + 1) * PW]).then_inc(s_back[p % 3], 16)

            sp.wait_ge(s_parked, 16 * NC)
            bring(0)
            bring(1)
            sp.wait_ge(s_gate_ix, NB // 2)
            for k in range(2):
                sp.wait_ge(s_gate_sc[k], NB // 2 * 16)
            sp.dma_start(small4[:, 1].rearrange("p n e -> p (n e)"), gates_out.rearrange("(p b) e -> p (b e)", p=P))\
              .then_inc(s_gate_in, 16)
            sp.wait_ge(ev("gate_ready"), 1)
            bring(2)

            h1 = X[:, 0:NB * C].rearrange("p (n c) -> p n c", c=C)
            for p in range(PIECES):
                sp.wait_ge(ev("out_ready"), p + 1)
                if p == 0:
                    bring(3)
                for tl in range(8):
                    first = 8 * PN * p + tl
                    n = len(range(first, min(T, 8 * PN * (p + 1)), 8))
                    sp.dma_start(out[:, first:first + 8 * (n - 1) + 1:8, :], h1[B * tl:B * tl + B, PN * p:PN * p + n, :])\
                      .then_inc(s_out, 16)
            sp.wait_ge(s_out, PIECES * 8 * 16)


        @block.gpsimd
        def _(pool):
            link = Steps(pool, s_const)
            link.did(pool.memset(FILL, EMPTY))
            link.last()
            pool.dma_start(ell.rearrange("(p n) o -> p (n o)", p=P), FILL).then_inc(s_ell0, 16)
            link.last()
            link.link(pool.memset(XT[C:P, XC - B:XC], 0.0))
            link.did(pool.memset(ident[:, :], 0.0))
            link.did(pool.memset(before[:, :], 1.0))
            link.did(pool.memset(ones_row[:, :], 1.0))
            link.did(pool.memset(mean64[:, :], 0.0))
            link.last()
            link.link(pool.memset(mean64[C:P, :], 1.0 / C))
            link.link(pool.memset(inw[0:C, :], 0.0))
            link.link(pool.memset(wgat[0:C, :], 0.0))
            link.link(pool.memset(w1s[0:C, :, :], 0.0))
            link.did(pool.memset(mean128[:, :], 1.0 / H))
            link.did(pool.memset(eps_col[:, :], EPS))
            link.did(pool.memset(dst_lohi[:, ET:ET + 8, :], 200.0))
            link.did(pool.iota(iota[:, :], [[1, P]], base=0, channel_multiplier=0,
                               allow_small_or_imprecise_dtypes=True))
            link.last()
            link.did(pool.affine_select(out=ident[:, :], in_=ident[:, :], compare_op=ALU.not_equal, fill=1.0,
                                        base=0, pattern=[[-1, P]], channel_multiplier=1))
            link.did(pool.affine_select(out=before[:, :], in_=before[:, :], compare_op=ALU.is_gt, fill=0.0,
                                        base=0, pattern=[[1, P]], channel_multiplier=-1))
            link.last()
            link.did(pool.tensor_copy(ident_b[:, :], ident[:, :]))
            link.did(pool.memset(space[:, :], 0.0))

            none = pool.alloc_register("none")
            last_slot = pool.alloc_register("last_slot")
            last_row = pool.alloc_register("last_row")
            pool.reg_mov(none, 0)
            pool.wait_ge(s_ell0, 16)
            with pool.Fori(0, ITERS) as i:
                for g in range(GR):
                    pool.wait_ge(s_ix, i * GR + (g + 1))
                    pool.reg_add(last_slot, none, MP * RS - 1)
                    for u in range(g * GS, g * GS + GS):
                        pool.indirect_dma_start(ell, bass.IndirectOffsetOnAxis(ap=slot_ix[:, u:u + 1], axis=0),
                                                src_st[:, u:u + 1], None, bounds_check=last_slot,
                                                oob_is_err=False).then_inc(s_sc[g], 16)

            pool.wait_ge(s_deg, 1)
            pool.partition_all_reduce(degrees[:, 1, :], degrees[:, 0, :], P, bass.bass_isa.ReduceOp.max).then_inc(s_deg, 1)
            pool.wait_ge(s_rounds, 1)
            pool.wait_ge(ev("gat_kept"), NC + 1)
            link.did(pool.memset(G[:, :, :, :], 0.0))
            link.last()
            pool.wait_ge(s_tab, 16)

            for g in range(GR):
                pool.wait_ge(s_sc[g], ITERS * GS * 16)
            pool.wait_ge(s_self, 32)

            def scatter_all(to, data, ready, done):
                with pool.Fori(0, NB // 4) as c:
                    for h in range(2):
                        pool.wait_ge(ready, c * 2 + (h + 1))
                        pool.reg_add(last_row, none, MP - 1)
                        for u in (2 * h, 2 * h + 1):
                            pool.indirect_dma_start(to, bass.IndirectOffsetOnAxis(ap=slot_ix[:, u:u + 1], axis=0),
                                                    data(u), None, bounds_check=last_row, oob_is_err=False)\
                                .then_inc(done[h], 16)

            scatter_all(perm_out, lambda u: src_st[:, u:u + 1], s_perm_ix, s_perm_sc)

            def slots_of(ring):
                pool.indirect_dma_start(EL[:, ring, :], None, ell_rows,
                                        bass.IndirectOffsetOnAxis(ap=px[:, ring:ring + 1], axis=0),
                                        bounds_check=last_row, oob_is_err=False).then_inc(s_el[ring], 16)

            def gather(b, q):
                if not (isinstance(b, int) and b < 3):
                    pool.wait_ge(s_used, b - 2)
                pool.reg_add(last_row, none, MP - 1)
                slots_of((q + 1) % 4)
                pool.wait_ge(s_el[q], (b - q) * 4 + 16)
                pool.reg_add(last_row, none, MP - 1)
                filled = pool.value_load(block_degree[0:1, ds(b, 1)], min_val=0, max_val=ET * P)

                def from_slot(s):
                    if s == SLOTS:
                        return
                    with pool.If(filled > s):
                        pool.indirect_dma_start(rows_of[q][:, s, :], None, table,
                                                bass.IndirectOffsetOnAxis(ap=EL[:, q, s:s + 1], axis=0),
                                                bounds_check=last_row, oob_is_err=False).then_inc(s_ga[q], 16)
                        from_slot(s + 1)
                    with pool.Else():
                        pool.inc_swdge_sem([s_ga[q]], [16 * (SLOTS - s)], mode="add")

                from_slot(0)

            pool.wait_ge(s_px, 1)
            link.link(pool.memset(G2[:, :, :, :], 0.0))
            pool.reg_add(last_row, none, MP - 1)
            slots_of(0)
            for q in range(4):
                gather(q, q)
            with pool.Fori(1, NB // 4) as i:
                for q in range(4):
                    gather(i * 4 + q, q)
            pool.wait_ge(s_el[0], NB * 4 + 16)

            pool.wait_ge(s_rounds, 1)
            rounds = pool.value_load(rounds_i[0:1, 0:1], min_val=0, max_val=MAX_ROUNDS)
            with pool.If(rounds > 1):
                pool.wait_ge(s_used, NB)
                link.link(pool.memset(FILL, EMPTY))
                with pool.Fori(1, rounds) as r:
                    pool.dma_start(ell.rearrange("(p n) o -> p (n o)", p=P), FILL).then_inc(s_round_empty, 16)
                    pool.wait_ge(s_round_empty, 16)
                    pool.inc_swdge_sem([s_round_empty], [16], mode="sub")
                    with pool.Fori(0, RG) as g:
                        pool.wait_ge(s_round_ix, (r - 1) * RG + g + 1)
                        pool.reg_add(last_slot, none, MP * RS - 1)
                        for u in range(GS):
                            pool.indirect_dma_start(ell, bass.IndirectOffsetOnAxis(ap=slot_ix[:, u:u + 1], axis=0),
                                                    src_st[:, u:u + 1], None, bounds_check=last_slot,
                                                    oob_is_err=False).then_inc(s_round_sc, 16)
                        pool.wait_ge(s_round_sc, GS * 16)
                        pool.inc_swdge_sem([s_round_sc], [GS * 16], mode="sub")
                        pool.sem_inc(s_round_put, 1)
                    with pool.Fori(0, NB) as b:
                        pool.wait_ge(s_round_px, (r - 1) * NB + b + 1)
                        pool.reg_add(last_row, none, MP - 1)
                        pool.indirect_dma_start(EL[:, 0, :], None, ell_rows,
                                                bass.IndirectOffsetOnAxis(ap=px[:, 0:1], axis=0),
                                                bounds_check=last_row, oob_is_err=False).then_inc(s_round_el, 16)
                        pool.wait_ge(s_round_el, 16)
                        pool.inc_swdge_sem([s_round_el], [16], mode="sub")
                        pool.reg_add(last_row, none, MP - 1)
                        for s in range(SLOTS):
                            pool.indirect_dma_start(G[:, 0, s, :], None, table,
                                                    bass.IndirectOffsetOnAxis(ap=EL[:, 0, s:s + 1], axis=0),
                                                    bounds_check=last_row, oob_is_err=False)\
                                .then_inc(s_round_ga, 16)
                        pool.wait_ge(s_round_ga, SLOTS * 16)
                        pool.inc_swdge_sem([s_round_ga], [SLOTS * 16], mode="sub")
                        pool.sem_inc(s_round_rows, 1)

            scatter_all(gates_out, lambda u: gate_st[:, u, :], s_gate_ix, s_gate_sc)

        @block.scalar
        def _(act):
            def col(v):
                return v.rearrange("(n o) -> n o", o=1)

            def bc(v, n):
                return v.rearrange("(o n) -> o n", o=1).to_broadcast([n, v.shape[0]])

            loads = [(wr[:, :, 0:C], conv_wr), (wi[:, :, :], conv_wi), (ph[:, :], phases), (inw[C:P, :], in_w),
                     (cols[:, IN_B:IN_B + 1], col(in_b)), (outw[:, 0:C], out_w),
                     (outw[:, C:P], out_w), (cols[0:C, OUT_B:OUT_B + 1], col(out_b)),
                     (cols[C:P, OUT_B:OUT_B + 1], col(out_b)),
                     (wgat[C:P, :], w_gat), (cols[:, B_B:B_B + 2], b_b), (b2row[:, :], b2),
                     (cols[:, C_B:C_B + 2], c_b), (cols[:, D_B:D_B + 2], d_b), (cols[:, LN_W:LN_W + 2], ln_w),
                     (cols[:, LN_B:LN_B + 2], ln_b), (cols[:, B1:B1 + 4], b1),
                     (w1s[C:P, :, :], w1), (w2s[:, :, :], w2),
                     (aw[:, :, :], a_w), (bw[:, :, :], b_w), (cw[:, :, :], c_w), (dw[:, :, :], d_w),
                     (vecs[:, ATT_S, :], bc(att_src, P)), (vecs[:, ATT_D, :], bc(att_dst, P)),
                     (vecs[:, BGAT, :], bc(b_gat, P)), (vecs[:, GAMMA, :], bc(gamma, P)),
                     (vecs[:, BETA, :], bc(beta, P))]
            assert len(loads) == NPAR
            for dst, src in loads:
                act.dma_start(dst, src).then_inc(s_par, 16)
            act.wait_ge(s_weff, 1)
            act.activation(trig[:, 0:2, :], trig[:, 2:4, :], ACT.Sin).then_inc(s_weff, 1)

            act.wait_ge(s_const, CONSTS)

            def s1(c, j):
                if j == S1["A_y"]:
                    act.wait_ge(ev("conv_ready"), c + 1)
                    act.activation(XT[:, ds(c * SC, SC)], bank[3][:, 0:SC], ACT.Copy).then_inc(ev("y_ready"), 1)
                    act.activation(s_b, bank[3][:, 0:SC], ACT.Square).then_inc(ev("s1_square"), 1)
                if j == S1["A_root"]:
                    act.wait_ge(ev("s1_var"), c + 1)
                    act.wait_ge(ev("s1_norm"), c)
                    act.activation(s_c, bank[3][:, 0:SC], ACT.Sqrt, bias=eps_col[:, :]).then_inc(ev("s1_root"), 1)
                if j == S1["A_x1"]:
                    act.wait_ge(ev("s1_in"), c + 1)
                    act.activation(X[:, ds(c * SC, SC)], bank[3][:, 0:SC], ACT.Identity,
                                   bias=cols[:, IN_B:IN_B + 1]).then_inc(ev("x1_ready"), 1)

            def mix(l, c, j):
                if j == MIX["A_centered"]:
                    bias = cols[:, CD_B + l:CD_B + l + 1]
                    act.wait_ge(ev(f"l{l}_mix"), c + 1)
                    act.activation(X[:, ds(c * SC, SC)], bank[0][:, 0:SC], ACT.Identity, bias=bias)\
                       .then_inc(ev(f"l{l}_centered"), 1)
                    act.activation(n_b, bank[0][:, 0:SC], ACT.Square, bias=bias).then_inc(ev(f"l{l}_square"), 1)
                if j == MIX["A_root"]:
                    act.wait_ge(ev(f"l{l}_var"), c + 1)
                    act.activation(n_c, bank[0][:, 0:SC], ACT.Sqrt, bias=eps_col[:, :])\
                       .then_inc(ev(f"l{l}_root"), 1)

            def output(c, j):
                if j == OUT["A_square"]:
                    act.wait_ge(ev("h1_ready"), c + 1)
                    act.activation(s_b, XT[:, ds(c * SC, SC)], ACT.Square).then_inc(ev("o_square"), 1)
                if j == OUT["A_root"]:
                    act.wait_ge(ev("o_var"), c + 1)
                    act.activation(s_c, bank[3][:, 0:SC], ACT.Sqrt, bias=eps_col[:, :]).then_inc(ev("o_root"), 1)

            stages = {"s1": s1, "output": output, "mix0": lambda c, j: mix(0, c, j), "mix1": lambda c, j: mix(1, c, j)}
            act.wait_ge(s_prep, 1)
            act.wait_ge(ev("biases_ready"), 1)
            for i in BEFORE:
                for j in range(TI):
                    beside(i, i, j, stages)

            def onehot_copy(k):
                act.activation(onehot_T[:, k % 4, :], bank[2][:, :].bitcast(bf16)[:, 0:P],
                               ACT.Copy).then_inc(s_te, 1)

            def count_copy(k):
                act.activation(counts[:, k % 2, :], bank[1][:, 0:P], ACT.Copy).then_inc(s_cc, 1)

            act.wait_ge(s_cnt, 1)
            count_copy(0)
            for k in range(2):
                act.wait_ge(s_tr, k + 1)
                onehot_copy(k)

            def iteration(first, i):
                l = first // CK
                col0 = i * SC + (B - l * MP)
                if not isinstance(i, int):
                    col0 = act.snap(col0)
                for j in range(TI):
                    if j < STEPS:
                        act.wait_ge(s_pre, i * STEPS + (j + 1))
                        act.activation(HS[:, ds(col0 + j * B, B)], bank[0][:, j * B:j * B + B], ACT.Tanh,
                                       bias=cols[:, B_B + l:B_B + l + 1])\
                           .then_inc(s_h, 1)
                    act.wait_ge(s_tr, i * TI + (j + 3))
                    onehot_copy(j + 2)
                    act.wait_ge(s_cnt, i * TI + (j + 2))
                    count_copy(j + 1)
                    beside(first, i, j, stages)

            over_ranges(act, iteration)
            for i in AFTER:
                for j in range(TI):
                    beside(i, i, j, stages)

            def stage_xn(c, k):
                act.activation(turned_in[k], XT[:, ds(c * CH, CH)], ACT.Copy).then_inc(ev("xn_staged"), 1)

            act.wait_ge(ev("xn_ready"), 32)
            stage_xn(0, 0)
            stage_xn(1, 1)
            with act.Fori(1, NC // 2) as i:
                for k in range(2):
                    act.wait_ge(ev("gat_product"), i * 2 + (k - 1))
                    stage_xn(i * 2 + k, k)
            act.wait_ge(ev("gat_product"), NC - 2)
            stage_xn(NC - 1, 0)

            act.wait_ge(ev("gat_kept"), NC + 1)
            act.dma_start(table.rearrange("(b p) f -> p b f", p=P), rows[:, :, :]).then_inc(s_tab, 16)
            own = ell.rearrange("(p b k) o -> p b (k o)", p=P, k=RS)
            act.dma_start(own[:, :, SLOTS:SLOTS + ROW], rows[:, :, :].bitcast(u32)).then_inc(s_self, 16)
            act.dma_start(own[:, :, SLOTS + ROW:RS], adst[:, :, :].bitcast(u32)).then_inc(s_self, 16)

            with act.Fori(0, NC) as c:
                act.activation(turned_in[0], XT[:, ds(c * CH, CH)], ACT.Copy).then_inc(ev("h1_staged"), 1)
                act.wait_ge(ev("h1_turned"), c + 1)
                act.activation(X[:, ds(c * (4 * C), 4 * C)].rearrange("p (q c) -> p q c", q=4),
                               bank[4][:, :].rearrange("p (q c) -> p q c", q=4)[:, :, 0:C], ACT.Copy)\
                   .then_inc(ev("h1_kept"), 1)
                for q in range(4):
                    act.wait_ge(s_arg, c * 4 + (q + 1))
                    act.activation(pexp[:, :], parg[:, :], ACT.Exp).then_inc(s_exp, 1)
                    act.wait_ge(ev("hidden_product"), c * 4 + (q + 1))
                    act.activation(hid[:, q, :], bank[q][:, :], ACT.Gelu, bias=cols[:, B1 + q:B1 + q + 1])\
                       .then_inc(ev("hidden_ready"), 1)
                act.wait_ge(s_parked, c * 16)
                for q in range(4):
                    act.wait_ge(ev("expert_product"), c * 4 + (q + 1))
                    act.activation(out_stage[:, q * EXPERTS * C:(q + 1) * EXPERTS * C], bank[4 + q][:, 0:EXPERTS * C],
                                   ACT.Copy).then_inc(ev("expert_kept"), 1)
                act.wait_ge(ev("expert_kept"), c * 4 + 4)
                act.dma_start(experts_out[:, ds(c * (4 * EXPERTS * C), 4 * EXPERTS * C)], out_stage)\
                   .then_inc(s_parked, 16)

            act.wait_ge(s_rounds, 1)
            rounds = act.value_load(rounds_i[0:1, 0:1], min_val=0, max_val=MAX_ROUNDS)
            with act.If(rounds > 1):
                with act.Fori(1, rounds) as r:
                    with act.Fori(0, NB) as b:
                        act.wait_ge(s_arg, r * NB + b + 1)
                        act.activation(pexp[:, :], parg[:, :], ACT.Exp).then_inc(s_exp, 1)

            act.wait_ge(ev("gate_var"), 1)
            act.activation(gm[:, 1, :], gm[:, 0, :], ACT.Sqrt, bias=eps_col[:, :]).then_inc(ev("gate_root"), 1)
            act.wait_ge(ev("gate_arg"), 1)
            act.activation(gm[:, 1, :], gm[:, 0, :], ACT.Exp).then_inc(ev("gate_exp"), 1)

        @block.vector
        def _(dve):
            me = Steps(dve, s_dve)
            link, did = me.link, me.did

            TAU = 6.283185307179586
            dve.wait_ge(s_par, 16 * NPAR)
            did(dve.tensor_scalar(trig[:, 0, :], ph[:, :], TAU / 4, None, ALU.add))
            link(dve.tensor_copy(trig[:, 1, :], ph[:, :]))
            link(dve.tensor_scalar(trig_i[:, :, :], trig[:, 0:2, :], 1 / TAU, None, ALU.mult))
            link(dve.tensor_copy(trig[:, 2:4, :], trig_i[:, :, :]))
            link(dve.scalar_tensor_tensor(out=trig[:, 2:4, :], in0=trig[:, 2:4, :], scalar=-TAU,
                                          in1=trig[:, 0:2, :], op0=ALU.mult, op1=ALU.add))
            for side, op in ((-TAU, ALU.is_gt), (TAU, ALU.is_lt)):
                link(dve.tensor_scalar(trig[:, 0:2, :], trig[:, 2:4, :], -side / 2, side, op, ALU.mult))
                link(dve.tensor_tensor(out=trig[:, 2:4, :], in0=trig[:, 2:4, :], in1=trig[:, 0:2, :], op=ALU.add))
            link(dve.tensor_scalar(trig[:, 2:4, :], trig[:, 2:4, :], 3.1415925, -3.1415925, ALU.min, ALU.max))
            dve.tensor_tensor(out=cols[:, CD_B:CD_B + 2], in0=cols[:, C_B:C_B + 2], in1=cols[:, D_B:D_B + 2],
                              op=ALU.add).then_inc(s_weff, 1)
            dve.wait_ge(s_weff, 2)
            cos = trig[:, 0, :].unsqueeze(2).to_broadcast([P, TAPS // 2, C])
            sin = trig[:, 1, :].unsqueeze(2).to_broadcast([P, TAPS // 2, C])
            did(dve.tensor_tensor(out=wr[:, :, 0:C], in0=wr[:, :, 0:C], in1=cos, op=ALU.mult))
            link(dve.tensor_tensor(out=wi[:, :, :], in0=wi[:, :, :], in1=sin, op=ALU.mult))
            link(dve.tensor_tensor(out=wr[:, :, 0:C], in0=wr[:, :, 0:C], in1=wi[:, :, :], op=ALU.subtract))
            dve.wait_ge(s_const, CONSTS)
            link(dve.tensor_tensor(out=dw[:, :, :], in0=dw[:, :, :],
                                   in1=ident[:, :].unsqueeze(1).to_broadcast([P, 2, H]), op=ALU.add))
            means = [trig[:, 0, :], trig[:, 1, 0:2], trig[:, 2, 0:2], trig[:, 3, 0:1]]
            for m, w, n in zip(means, (wr[:, :, 0:C], cw[:, :, :], dw[:, :, :], outw[:, 0:C]), (C, H, H, C)):
                link(dve.tensor_reduce(out=m, in_=w, axis=AX.X, op=ALU.add))
                link(dve.tensor_scalar(m, m, 1.0 / n, None, ALU.mult))
            did(dve.tensor_tensor(out=cw[:, :, :], in0=cw[:, :, :],
                                  in1=means[1].unsqueeze(2).to_broadcast([P, 2, H]), op=ALU.subtract))
            did(dve.tensor_tensor(out=dw[:, :, :], in0=dw[:, :, :],
                                  in1=means[2].unsqueeze(2).to_broadcast([P, 2, H]), op=ALU.subtract))
            did(dve.tensor_scalar(outw[:, C:P], outw[:, 0:C], means[3], None, ALU.subtract))
            me.last()
            dve.tensor_tensor(out=wr[:, :, C:P], in0=wr[:, :, 0:C],
                              in1=means[0].unsqueeze(2).to_broadcast([P, TAPS // 2, C]), op=ALU.subtract)\
               .then_inc(s_weff, 1)
            dve.wait_ge(ev("bias_means"), 1)
            link(dve.tensor_tensor(out=cols[:, CD_B:CD_B + 2], in0=cols[:, CD_B:CD_B + 2], in1=bank[4][:, 0:2],
                                   op=ALU.subtract))
            dve.tensor_tensor(out=cols[C:P, OUT_B:OUT_B + 1], in0=cols[C:P, OUT_B:OUT_B + 1],
                              in1=bank[4][C:P, 2:3], op=ALU.subtract).then_inc(ev("biases_ready"), 1)
            dve.wait_ge(ev("biases_ready"), 1)

            dve.wait_ge(s_edge, 16)
            Nn, Q, R, Z = [X[:, k * ET:(k + 1) * ET] for k in range(4)]
            QI = X[:, 4 * ET:5 * ET].bitcast(i32)

            def divide(n, by, half):
                link(dve.tensor_scalar(QI, n, half, 1.0 / by, ALU.add, ALU.mult))
                link(dve.tensor_copy(Q, QI))
                link(dve.scalar_tensor_tensor(out=R, in0=Q, scalar=-float(by), in1=n, op0=ALU.mult, op1=ALU.add))
                link(dve.tensor_scalar(Z, R, 0.0, None, ALU.is_lt))
                did(dve.tensor_tensor(out=Q, in0=Q, in1=Z, op=ALU.subtract))
                link(dve.scalar_tensor_tensor(out=R, in0=Z, scalar=float(by), in1=R, op0=ALU.mult, op1=ALU.add))

            for side in range(2):
                ids = HS[:, side * ET:(side + 1) * ET].bitcast(i32)
                link(dve.tensor_copy(Nn, ids))
                if side == 0:
                    link(dve.tensor_scalar(Nn, Nn, float(M - 1), None, ALU.min))
                divide(Nn, T, 0.25)
                link(dve.scalar_tensor_tensor(out=R, in0=R, scalar=float(B), in1=Q, op0=ALU.mult, op1=ALU.add))
                if side == 0:
                    link(dve.tensor_copy(src_ids[:, :], R))
            link(dve.tensor_scalar(Z, Nn, float(M), float(P * 16384), ALU.is_ge, ALU.mult))
            link(dve.tensor_tensor(out=Nn, in0=R, in1=Z, op=ALU.add))
            divide(Nn, P, 0.5)
            link(dve.tensor_copy(dst_lohi[:, 0:ET, 0], R))
            did(dve.tensor_copy(dst_lohi[:, 0:ET, 1], Q))
            me.last()
            dve.memset(HS[:, 0:B], 0.0).then_inc(s_prep, 1)

            RECIP = 4

            def reciprocal(root, part, ready, c):
                if 0 <= part < RECIP:
                    if part == 0:
                        dve.wait_ge(ready, c + 1)
                    w = SC // RECIP
                    did(dve.reciprocal(root[:, part * w:part * w + w], root[:, part * w:part * w + w]))

            def s1(c, j):
                reciprocal(s_c, j - S1["V_recip"], ev("s1_root"), c)
                if j == S1["V_norm"]:
                    me.last()
                    dve.tensor_tensor(out=s_n, in0=XT[:, ds(c * SC, SC)], in1=s_c, op=ALU.mult).then_inc(ev("s1_norm"), 1)

            def mix(l, c, j):
                chunk = X[:, ds(c * SC, SC)]
                reciprocal(n_c, j - MIX["V_recip"], ev(f"l{l}_root"), c)
                if j == MIX["V_norm"]:
                    me.last()
                    did(dve.tensor_tensor(out=chunk, in0=chunk, in1=n_c, op=ALU.mult))
                if j == MIX["V_affine"]:
                    me.last()
                    dve.tensor_scalar(chunk, chunk, cols[:, LN_W + l:LN_W + l + 1],
                                      cols[:, LN_B + l:LN_B + l + 1], ALU.mult, ALU.add)\
                       .then_inc(ev(f"l{l}_norm"), 1)

            def output(c, j):
                if j == OUT["V_h1"]:
                    dve.wait_ge(ev("o_product"), c + 1)
                    y = XT[:, ds(c * SC, SC)]
                    dve.scalar_tensor_tensor(out=y, in0=bank[3][:, 0:SC], scalar=cols[:, OUT_B:OUT_B + 1], in1=y,
                                             op0=ALU.add, op1=ALU.add).then_inc(ev("h1_ready"), 1)
                reciprocal(s_c, j - OUT["V_recip"], ev("o_root"), c)
                if j == OUT["V_xn"]:
                    me.last()
                    dve.tensor_tensor(out=XT[C:P, ds(c * SC, SC)], in0=XT[C:P, ds(c * SC, SC)], in1=s_c[C:P, :],
                                      op=ALU.mult)\
                       .then_inc(ev("xn_ready"), 1)

            stages = {"s1": s1, "output": output, "mix0": lambda c, j: mix(0, c, j), "mix1": lambda c, j: mix(1, c, j)}
            dve.wait_ge(s_const, CONSTS)
            for i in BEFORE:
                for j in range(TI):
                    beside(i, i, j, stages)

            def make_onehot(t, k):
                dve.tensor_tensor(out=onehot[:, k % 8, :, :],
                                  in0=iota[:, :].unsqueeze(1).to_broadcast([P, 2, P]),
                                  in1=dst_lohi[:, ds(t, 1), :].rearrange("p a b -> p (a b)").unsqueeze(2)
                                  .to_broadcast([P, 2, P]), op=ALU.is_equal).then_inc(s_oh, 1)

            def keep_earlier(k):
                dve.tensor_tensor(out=earlier[:, k % 2, :], in0=bank[4 + k % 2][:, 0:P],
                                  in1=before[:, :], op=ALU.mult).then_inc(s_early, 1)

            for k in range(3):
                make_onehot(k, k)
            dve.wait_ge(s_pair, 1)
            keep_earlier(0)

            def iteration(first, i):
                for j in range(TI):
                    dve.wait_ge(s_cnt, i * TI + (j + 1))
                    make_onehot(i * TI + (j + 3), j + 3)
                    dve.wait_ge(s_pair, i * TI + (j + 2))
                    keep_earlier(j + 1)
                    dve.wait_ge(s_rps, i * TI + (j + 1))
                    dve.tensor_tensor_reduce(out=junk[:, j % 2, :], in0=bank[6 + j % 2][:, 0:NB],
                                             in1=onehot[:, j % 8, 1, 0:NB], scale=1.0, scalar=0.0,
                                             op0=ALU.mult, op1=ALU.add, accum_out=rank[:, j:j + 1])\
                       .then_inc(s_rk, 1)
                    g = j // GS
                    part = slice(g * GS, g * GS + GS)
                    if j % GS == GS - 3:
                        lohi = dst_lohi[:, ds(i * TI + g * GS, GS), :]
                        did(dve.scalar_tensor_tensor(out=slot_f[:, :], in0=lohi[:, :, 0], scalar=float(NB),
                                                     in1=lohi[:, :, 1], op0=ALU.mult, op1=ALU.add))
                        dve.wait_ge(s_sc[g], i * (GS * 16))
                        did(dve.tensor_scalar(src_st[:, part], src_ids[:, ds(i * TI + g * GS, GS)], 1.0, None,
                                              ALU.mult))
                    if j % GS == GS - 1:
                        dve.wait_ge(s_rk, i * TI + (j + 1))
                        me.last()
                        did(dve.tensor_scalar(over[:, :], rank[:, part], float(SLOTS), FAR, ALU.is_ge, ALU.mult))
                        did(dve.tensor_scalar(ranks[:, ds(i * TI + g * GS, GS)], rank[:, part], 1.0, None, ALU.mult))
                        link(dve.scalar_tensor_tensor(out=slot_f[:, :], in0=slot_f[:, :],
                                                     scalar=float(RS), in1=rank[:, part],
                                                     op0=ALU.mult, op1=ALU.add))
                        dve.tensor_tensor(out=slot_ix[:, part], in0=slot_f[:, :], in1=over[:, :], op=ALU.add)\
                           .then_inc(s_ix, 1)
                    beside(first, i, j, stages)

            over_ranges(dve, iteration, me, 5 * GR + RECIP + (RECIP + 1))
            for i in AFTER:
                for j in range(TI):
                    beside(i, i, j, stages)

            def keep_h(c, k):
                dve.wait_ge(ev("gat_product"), c + 1)
                dve.tensor_scalar(rows[:, ds(c * 4, 4), HEADS:ROW],
                                  bank[4 + k][:, 0:4 * F].rearrange("p (q f) -> p q f", f=F), 1.0, None, ALU.mult)\
                   .then_inc(ev("gat_kept"), 1)

            with dve.Fori(0, NC // 2) as i:
                for k in range(2):
                    keep_h(i * 2 + k, k)
            keep_h(NC - 1, 0)

            did(dve.memset(window[:, :], 0.0))
            dve.tensor_copy(degrees[:, 0, :], bank[1][:, 0:NB]).then_inc(s_deg, 1)
            dve.wait_ge(s_deg, 2)
            link(dve.tensor_reduce(out=degree[:, 0:1], in_=degrees[:, 1, :], axis=AX.X, op=ALU.max))
            link(dve.tensor_scalar(degree[:, 0:1], degree[:, 0:1], -1.0, None, ALU.add))
            link(dve.tensor_scalar(rounds_i[:, :], degree[:, 0:1], 0.5, 1.0 / SLOTS, ALU.add, ALU.mult))
            link(dve.tensor_copy(degree[:, 1:2], rounds_i[:, :]))
            link(dve.scalar_tensor_tensor(out=degree[:, 0:1], in0=degree[:, 1:2], scalar=-float(SLOTS),
                                          in1=degree[:, 0:1], op0=ALU.mult, op1=ALU.add))
            link(dve.tensor_scalar(degree[:, 0:1], degree[:, 0:1], 0.0, None, ALU.is_ge))
            dve.tensor_tensor(out=rounds_i[:, :], in0=degree[:, 1:2], in1=degree[:, 0:1], op=ALU.add)\
               .then_inc(s_rounds, 1)
            dve.wait_ge(s_rounds, 1)

            dve.wait_ge(ev("gat_kept"), NC)
            hh = rows[:, :, HEADS:ROW]

            def all_nodes(v):
                return vecs[:, v, :].unsqueeze(1).to_broadcast([P, NB, F])

            def per_head(a):
                return a.rearrange("p n (h j) -> p n h j", h=HEADS)

            me.last()
            did(dve.tensor_tensor(out=work[:, 0], in0=hh, in1=all_nodes(ATT_S), op=ALU.mult))
            link(dve.tensor_tensor(out=work[:, 1], in0=hh, in1=all_nodes(ATT_D), op=ALU.mult))
            did(dve.tensor_reduce(out=rows[:, :, 0:HEADS], in_=per_head(work[:, 0]), axis=AX.X, op=ALU.add))
            link(dve.tensor_reduce(out=adst[:, :, :], in_=per_head(work[:, 1]), axis=AX.X, op=ALU.add))
            dve.memset(acc[:, :, 0:HEADS], 1.0).then_inc(ev("gat_kept"), 1)
            dve.wait_ge(ev("gat_kept"), NC + 1)

            at = [0]

            def scratch(*dims):
                n = 1
                for d in dims:
                    n *= d
                part = HS[:, at[0]:at[0] + n]
                at[0] += n
                assert at[0] <= MP
                return part if len(dims) == 1 else part.rearrange("p (a b) -> p a b", b=dims[1])

            K, KP = SLOTS + 1, 64
            cmp_flat = scratch(NB * NB)
            cmp = cmp_flat.rearrange("p (a b) -> p a b", b=NB)
            mask = cmp_flat[:, 0:NB * K].rearrange("p (a k) -> p a k", k=K)
            over_b = cmp_flat[:, 0:NB * SLOTS].rearrange("p (a k) -> p a k", k=SLOTS)
            key, comp, ahead, place, quot, fix, node = [scratch(NB) for _ in range(7)]
            count_up = scratch(P)
            hist = scratch(KP)
            more = [scratch(2, 2 * KP) for _ in range(2)]
            base = scratch(K)

            def over_nodes(v, n):
                return v.unsqueeze(1).to_broadcast([P, NB, n])

            def along(v, n):
                return v.unsqueeze(2).to_broadcast([P, NB, n])

            did(dve.memset(hist, 0.0))
            did(dve.memset(more[0], 0.0))
            did(dve.memset(more[1], 0.0))
            did(dve.memset(perm[:, NB:NB + 4], 0))
            did(dve.tensor_copy(count_up, iota[:, :]))
            link(dve.tensor_scalar(key, degrees[:, 0, :], float(SLOTS), None, ALU.min))
            link(dve.scalar_tensor_tensor(out=comp, in0=key, scalar=float(P), in1=count_up[:, 0:NB], op0=ALU.mult,
                                          op1=ALU.subtract))
            link(dve.tensor_tensor(out=cmp, in0=over_nodes(comp, NB), in1=along(comp, NB), op=ALU.is_gt))
            link(dve.tensor_reduce(out=ahead, in_=cmp, axis=AX.X, op=ALU.add))
            link(dve.tensor_tensor(out=mask, in0=along(key, K), in1=over_nodes(count_up[:, 0:K], K), op=ALU.is_equal))
            dve.tensor_reduce(out=hist[:, 0:K], in_=mask.rearrange("p a k -> p k a"), axis=AX.X, op=ALU.add)\
               .then_inc(ev("hist_ready"), 1)
            dve.wait_ge(ev("hist_sums"), 1)
            did(dve.tensor_scalar(more[0][:, 0, 0:KP], bank[4][:, 0:KP], float(P), None, ALU.mult))
            link(dve.tensor_scalar(more[0][:, 1, 0:KP], hist, 1.0, None, ALU.mult))
            step, now = 1, 0
            while step < KP:
                link(dve.tensor_tensor(out=more[1 - now][:, :, 0:KP], in0=more[now][:, :, 0:KP],
                                       in1=more[now][:, :, step:step + KP], op=ALU.add))
                step, now = 2 * step, 1 - now
            total, own = more[now][:, 0, 1:K + 1], more[now][:, 1, 1:K + 1]
            link(dve.tensor_tensor(out=base, in0=total, in1=own, op=ALU.subtract))
            link(dve.tensor_tensor(out=base, in0=base, in1=bank[5][:, 0:K], op=ALU.add))
            link(dve.tensor_tensor(out=mask, in0=mask, in1=over_nodes(base, K), op=ALU.mult))
            link(dve.tensor_reduce(out=place, in_=mask, axis=AX.X, op=ALU.add))
            did(dve.tensor_tensor(out=place, in0=place, in1=ahead, op=ALU.add))
            link(dve.tensor_scalar(comp, count_up[:, 0:NB], float(P), None, ALU.mult))
            link(dve.tensor_tensor(out=over_b, in0=over_nodes(total[:, 0:SLOTS], SLOTS), in1=along(comp, SLOTS),
                                   op=ALU.is_gt))
            link(dve.tensor_reduce(out=fix, in_=over_b, axis=AX.X, op=ALU.add))
            link(dve.tensor_copy(block_degree[:, :], fix))
            quot_i = comp.bitcast(i32)
            link(dve.tensor_scalar(quot_i, place, 0.5, 1.0 / P, ALU.add, ALU.mult))
            link(dve.tensor_copy(quot, quot_i))
            link(dve.scalar_tensor_tensor(out=place, in0=quot, scalar=-float(P), in1=place, op0=ALU.mult, op1=ALU.add))
            link(dve.tensor_scalar(fix, place, 0.0, None, ALU.is_lt))
            did(dve.tensor_tensor(out=quot, in0=quot, in1=fix, op=ALU.subtract))
            link(dve.scalar_tensor_tensor(out=place, in0=fix, scalar=float(P), in1=place, op0=ALU.mult, op1=ALU.add))
            link(dve.scalar_tensor_tensor(out=place, in0=place, scalar=float(NB), in1=quot, op0=ALU.mult, op1=ALU.add))
            link(dve.tensor_scalar(base[:, 0:1], bank[4][:, KP:KP + 1], float(P * NB), None, ALU.mult))
            link(dve.tensor_scalar(node, count_up[:, 0:NB], base[:, 0:1], None, ALU.add))

            def stage_all(indices, data, to, ready, done):
                with dve.Fori(0, NB // 4) as c:
                    me.enter(c * 2, 2)
                    for h in range(2):
                        dve.wait_ge(done[h], c * 32)
                        did(dve.tensor_scalar(to[:, 2 * h:2 * h + 2], data[:, ds(c * 4 + 2 * h, 2)], 1.0, None,
                                              ALU.mult))
                        me.last()
                        dve.tensor_scalar(slot_ix[:, 2 * h:2 * h + 2], indices[:, ds(c * 4 + 2 * h, 2)], 1.0, None,
                                          ALU.mult).then_inc(ready, 1)
                me.leave(NB // 4)

            for g in range(GR):
                dve.wait_ge(s_sc[g], ITERS * GS * 16)
            stage_all(place, node, src_st, s_perm_ix, s_perm_sc)
            dve.wait_ge(s_perm_ix, NB // 2)
            did(dve.memset(order[:, 0:1], 0.0))
            me.last()
            dve.tensor_copy(window[:, :], order[:, 0:1]).then_inc(ev("sorted"), 1)
            dve.wait_ge(s_perm_in, 16)
            dve.tensor_copy(px[:, :], perm[:, 0:4]).then_inc(s_px, 1)
            dve.wait_ge(s_self, 32)

            HK = HEADS * SLOTS

            def begin(b, q):
                a_s, h_s, a_d = [EL_f[:, q, SLOTS + v:SLOTS + v + n] for v, n in ((0, HEADS), (HEADS, F), (ROW, HEADS))]
                m_b = mx[:, ds(b, 1), :].rearrange("p a h -> p (a h)")
                did(dve.tensor_scalar(adst[:, ds(b, 1), :].rearrange("p a h -> p (a h)"), a_d, 1.0, None, ALU.mult))
                did(dve.tensor_scalar(acc[:, ds(b, 1), HEADS:ROW].rearrange("p a f -> p (a f)"), h_s, 1.0, None,
                                      ALU.mult))
                link(dve.tensor_tensor(out=m_b, in0=a_s, in1=a_d, op=ALU.add))
                link(dve.scalar_tensor_tensor(out=m_b, in0=m_b, scalar=0.2, in1=m_b, op0=ALU.mult, op1=ALU.max))

            def attend(me, b, q, nth):
                did, link = me.did, me.link
                a_d = adst[:, ds(b, 1), :].rearrange("p a h -> p (a h)")
                m_b = mx[:, ds(b, 1), :].rearrange("p a h -> p (a h)")
                den = acc[:, ds(b, 1), 0:HEADS].rearrange("p a h -> p (a h)")
                num = acc[:, ds(b, 1), HEADS:ROW].rearrange("p a f -> p (a f)")
                arg = parg[:, 0:HK].rearrange("p (h k) -> p h k", h=HEADS)
                m_new, s_den, s_num = small[:, 0, 0:HEADS], small[:, 1, 0:HEADS], small[:, 2, :]
                did(dve.tensor_scalar(pmask[:, :], EL[:, q, 0:SLOTS], float(MP), NONE, ALU.is_ge, ALU.mult))
                link(dve.tensor_tensor(out=pe_[:, :, :], in0=rows_of[q][:, :, 0:HEADS].rearrange("p k h -> p h k"),
                                       in1=a_d.unsqueeze(2).to_broadcast([P, HEADS, SLOTS]), op=ALU.add))
                link(dve.scalar_tensor_tensor(out=pe_[:, :, :], in0=pe_[:, :, :], scalar=0.2,
                                              in1=pe_[:, :, :], op0=ALU.mult, op1=ALU.max))
                link(dve.tensor_tensor(out=pe_[:, :, :], in0=pe_[:, :, :],
                                       in1=pmask[:, :].unsqueeze(1).to_broadcast([P, HEADS, SLOTS]),
                                       op=ALU.add))
                link(dve.tensor_reduce(out=small[:, 3, 0:HEADS], in_=pe_[:, :, :], axis=AX.X, op=ALU.max))
                link(dve.tensor_tensor(out=m_new, in0=small[:, 3, 0:HEADS], in1=m_b, op=ALU.max))
                did(dve.tensor_tensor(out=arg, in0=pe_[:, :, :],
                                      in1=m_new.unsqueeze(2).to_broadcast([P, HEADS, SLOTS]),
                                      op=ALU.subtract))
                dve.tensor_tensor(out=parg[:, HK:HK + HEADS], in0=m_b, in1=m_new, op=ALU.subtract)\
                   .then_inc(s_arg, 1)
                dve.wait_ge(s_arg, nth)
                did(dve.tensor_scalar(m_b, m_new, 1.0, None, ALU.mult))
                dve.wait_ge(s_exp, nth)
                pk = pexp[:, 0:HK].rearrange("p (h k) -> p h k", h=HEADS)
                old = pexp[:, HK:HK + HEADS]
                did(dve.tensor_tensor(out=msg.rearrange("p h j k -> p h j k"),
                                      in0=rows_of[q][:, :, HEADS:ROW].rearrange("p k (h j) -> p h j k", h=HEADS),
                                      in1=pk.unsqueeze(2).to_broadcast([P, HEADS, EXPERTS, SLOTS]),
                                      op=ALU.mult))
                did(dve.tensor_reduce(out=s_den, in_=pk, axis=AX.X, op=ALU.add))
                did(dve.tensor_tensor(out=den, in0=den, in1=old, op=ALU.mult))
                did(dve.tensor_tensor(out=num.rearrange("p (h j) -> p h j", h=HEADS),
                                      in0=num.rearrange("p (h j) -> p h j", h=HEADS),
                                      in1=old.unsqueeze(2).to_broadcast([P, HEADS, EXPERTS]), op=ALU.mult))
                me.last()
                did(dve.tensor_reduce(out=s_num, in_=HS[:, 0:F * SLOTS].rearrange("p (f k) -> p f k", k=SLOTS),
                                      axis=AX.X, op=ALU.add))
                link(dve.tensor_tensor(out=den, in0=den, in1=s_den, op=ALU.add))
                me.did(dve.tensor_tensor(out=num, in0=num, in1=s_num, op=ALU.add))
                me.last()

            with dve.Fori(0, NB // 4) as i:
                me.enter(i * (4 * (ATT_STEPS + INIT_STEPS)), 4 * (ATT_STEPS + INIT_STEPS))
                for q in range(4):
                    dve.wait_ge(s_el[q], i * 16 + 16)
                    begin(i * 4 + q, q)
                    dve.wait_ge(s_ga[q], i * (16 * SLOTS) + 16 * SLOTS)
                    attend(me, i * 4 + q, q, i * 4 + (q + 1))
                    dve.tensor_scalar(px[:, q:q + 1], perm[:, ds(i * 4 + (q + 4), 1)], 1.0, None, ALU.mult)\
                       .then_inc(s_used, 1)
            me.leave(NB // 4)

            rounds = dve.value_load(rounds_i[0:1, 0:1], min_val=0, max_val=MAX_ROUNDS)
            with dve.If(rounds > 1):
                again = Steps(dve, s_dve_round)
                with dve.Fori(1, rounds) as r:
                    per_round = 1 + RG * 5 + NB * ATT_STEPS
                    again.enter((r - 1) * per_round, per_round)
                    again.did(dve.tensor_scalar(window[:, :], window[:, :], float(SLOTS), None, ALU.add))
                    with dve.Fori(0, RG) as g:
                        again.enter((r - 1) * per_round + g * 5, 5)
                        lohi = dst_lohi[:, ds(g * GS, GS), :]
                        dve.wait_ge(s_dve_round, (r - 1) * per_round + 1)
                        dve.wait_ge(s_round_put, (r - 1) * RG + g)
                        again.did(dve.tensor_scalar(src_st[:, 0:GS], src_ids[:, ds(g * GS, GS)], 1.0, None, ALU.mult))
                        again.did(dve.scalar_tensor_tensor(out=slot_f[:, :], in0=lohi[:, :, 0], scalar=float(NB),
                                                           in1=lohi[:, :, 1], op0=ALU.mult, op1=ALU.add))
                        again.link(dve.tensor_scalar(rank[:, 0:GS], ranks[:, ds(g * GS, GS)], window[:, 0:1], None,
                                                     ALU.subtract))
                        again.did(dve.tensor_scalar(over[:, :], rank[:, 0:GS], float(SLOTS), FAR, ALU.is_ge,
                                                    ALU.mult))
                        dve.tensor_scalar(rank[:, GS:2 * GS], rank[:, 0:GS], 0.0, FAR, ALU.is_lt, ALU.mult)\
                           .then_inc(s_round_part, 1)
                        dve.wait_ge(s_round_part, ((r - 1) * RG + g) * 3 + 1)
                        again.link(dve.tensor_tensor(out=over[:, :], in0=over[:, :], in1=rank[:, GS:2 * GS],
                                                     op=ALU.max))
                        dve.scalar_tensor_tensor(out=slot_f[:, :], in0=slot_f[:, :], scalar=float(RS),
                                                 in1=rank[:, 0:GS], op0=ALU.mult, op1=ALU.add)\
                           .then_inc(s_round_part, 1)
                        dve.wait_ge(s_round_part, ((r - 1) * RG + g) * 3 + 2)
                        dve.tensor_scalar(slot_f[:, :], slot_f[:, :], -FAR / 2, FAR - 1, ALU.max, ALU.min)\
                           .then_inc(s_round_part, 1)
                        dve.wait_ge(s_round_part, ((r - 1) * RG + g) * 3 + 3)
                        dve.tensor_tensor(out=slot_ix[:, 0:GS], in0=slot_f[:, :], in1=over[:, :], op=ALU.add)\
                           .then_inc(s_round_ix, 1)
                    again.leave(RG)
                    with dve.Fori(0, NB) as b:
                        again.enter((r - 1) * per_round + b * ATT_STEPS, ATT_STEPS)
                        dve.tensor_scalar(px[:, 0:1], perm[:, ds(b, 1)], 1.0, None, ALU.mult).then_inc(s_round_px, 1)
                        dve.wait_ge(s_round_rows, (r - 1) * NB + b + 1)
                        attend(again, b, 0, r * NB + b + 1)
                    again.leave(NB)
                    again.leave(1)


            W = [work[:, k] for k in range(4)]
            den_all = acc[:, :, 0:HEADS]
            dve.wait_ge(ev("expert_kept"), 4 * NC)
            sc4 = small4
            link(dve.tensor_scalar(sc4[:, 0], den_all, 1e-16, None, ALU.add))
            link(dve.reciprocal(sc4[:, 0], sc4[:, 0]))
            link(dve.tensor_tensor(out=per_head(W[0]), in0=per_head(acc[:, :, HEADS:ROW]),
                                   in1=sc4[:, 0].unsqueeze(3).to_broadcast([P, NB, HEADS, EXPERTS]), op=ALU.mult))
            link(dve.tensor_tensor(out=W[0], in0=W[0], in1=all_nodes(BGAT), op=ALU.add))
            link(dve.tensor_reduce(out=gm[:, 0, :], in_=W[0], axis=AX.X, op=ALU.add))
            link(dve.tensor_scalar(gm[:, 0, :], gm[:, 0, :], 1.0 / F, None, ALU.mult))
            link(dve.tensor_tensor(out=W[0], in0=W[0], in1=gm[:, 0, :].unsqueeze(2).to_broadcast([P, NB, F]),
                                   op=ALU.subtract))
            link(dve.tensor_tensor(out=W[1], in0=W[0], in1=W[0], op=ALU.mult))
            link(dve.tensor_reduce(out=gm[:, 0, :], in_=W[1], axis=AX.X, op=ALU.add))
            dve.tensor_scalar(gm[:, 0, :], gm[:, 0, :], 1.0 / F, None, ALU.mult).then_inc(ev("gate_var"), 1)
            dve.wait_ge(ev("gate_root"), 1)
            link(dve.reciprocal(gm[:, 2, :], gm[:, 1, :]))
            link(dve.tensor_tensor(out=W[0], in0=W[0], in1=gm[:, 2, :].unsqueeze(2).to_broadcast([P, NB, F]),
                                   op=ALU.mult))
            link(dve.tensor_tensor(out=W[0], in0=W[0], in1=all_nodes(GAMMA), op=ALU.mult))
            link(dve.tensor_tensor(out=W[0], in0=W[0], in1=all_nodes(BETA), op=ALU.add))
            link(dve.tensor_reduce(out=sc4[:, 0], in_=W[0].rearrange("p n (h j) -> p n j h", h=HEADS),
                                   axis=AX.X, op=ALU.add))
            link(dve.tensor_scalar(sc4[:, 0], sc4[:, 0], 1.0 / HEADS, None, ALU.mult))

            def best(top, pick):
                link(dve.tensor_reduce(out=top, in_=sc4[:, 0], axis=AX.X, op=ALU.max))
                link(dve.tensor_tensor(out=sc4[:, 2], in0=sc4[:, 0],
                                       in1=top.unsqueeze(2).to_broadcast([P, NB, EXPERTS]), op=ALU.is_equal))
                link(dve.tensor_tensor(out=sc4[:, 2], in0=sc4[:, 2],
                                       in1=order[:, :].unsqueeze(1).to_broadcast([P, NB, EXPERTS]), op=ALU.mult))
                link(dve.tensor_reduce(out=gm[:, 3, :], in_=sc4[:, 2], axis=AX.X, op=ALU.max))
                link(dve.tensor_tensor(out=pick, in0=sc4[:, 2],
                                       in1=gm[:, 3, :].unsqueeze(2).to_broadcast([P, NB, EXPERTS]),
                                       op=ALU.is_equal))

            for e in range(EXPERTS):
                did(dve.memset(order[:, e:e + 1], float(EXPERTS - e)))
            me.last()
            best(gm[:, 1, :], sc4[:, 1])
            link(dve.tensor_scalar(sc4[:, 2], sc4[:, 1], NONE, None, ALU.mult))
            link(dve.tensor_tensor(out=sc4[:, 0], in0=sc4[:, 0], in1=sc4[:, 2], op=ALU.add))
            best(gm[:, 2, :], sc4[:, 3])
            dve.tensor_tensor(out=gm[:, 0, :], in0=gm[:, 2, :], in1=gm[:, 1, :], op=ALU.subtract)\
               .then_inc(ev("gate_arg"), 1)
            dve.wait_ge(ev("gate_exp"), 1)
            link(dve.tensor_scalar(gm[:, 2, :], gm[:, 1, :], 1.0, None, ALU.add))
            link(dve.reciprocal(gm[:, 2, :], gm[:, 2, :]))
            link(dve.tensor_tensor(out=gm[:, 3, :], in0=gm[:, 1, :], in1=gm[:, 2, :], op=ALU.mult))
            did(dve.tensor_tensor(out=sc4[:, 1], in0=sc4[:, 1],
                                  in1=gm[:, 2, :].unsqueeze(2).to_broadcast([P, NB, EXPERTS]), op=ALU.mult))
            link(dve.tensor_tensor(out=sc4[:, 3], in0=sc4[:, 3],
                                   in1=gm[:, 3, :].unsqueeze(2).to_broadcast([P, NB, EXPERTS]), op=ALU.mult))
            dve.tensor_tensor(out=sc4[:, 0], in0=sc4[:, 1], in1=sc4[:, 3], op=ALU.add).then_inc(ev("gate_ready"), 1)
            dve.wait_ge(ev("gate_ready"), 1)
            stage_all(perm, sc4[:, 0], gate_st, s_gate_ix, s_gate_sc)
            dve.wait_ge(s_gate_in, 16)

            h1 = X[:, 0:NB * C].rearrange("p (n c) -> p n c", c=C)
            for p in range(PIECES):
                part = back[p].rearrange("p (n e c) -> p n e c", e=EXPERTS, c=C)
                n0 = p * PN
                dve.wait_ge(s_back[p % 3], 16 * (p // 3 + 1))
                link(dve.tensor_tensor(out=part, in0=part, in1=sc4[:, 1, n0:n0 + PN, :].unsqueeze(3)
                                       .to_broadcast([P, PN, EXPERTS, C]), op=ALU.mult))
                link(dve.tensor_tensor(out=part[:, :, 0:2, :], in0=part[:, :, 0:2, :], in1=part[:, :, 2:4, :],
                                       op=ALU.add))
                link(dve.tensor_tensor(out=part[:, :, 0, :], in0=part[:, :, 0, :], in1=part[:, :, 1, :], op=ALU.add))
                dve.tensor_tensor(out=h1[:, n0:n0 + PN, :], in0=h1[:, n0:n0 + PN, :], in1=part[:, :, 0, :],
                                  op=ALU.add).then_inc(ev("out_ready"), 1)

        @block.tensor
        def _(pe):
            mm = nc.tensor.matmul

            def s1(c, j):
                at3 = bank[3][:, 0:SC]
                tap = j - S1["P_conv"]
                if 0 <= tap < TAPS // 2:
                    if tap == 0:
                        pe.wait_ge(ev("s1_root"), c)
                    if tap == 0 and not (isinstance(c, int) and c == 0):
                        pe.wait_ge(ev("x1_ready"), c - 1)
                    ins = mm(at3, wr[:, tap, :], XT[:, ds(c * SC + 2 * tap * B, SC)],
                             start=(tap == 0), stop=(tap == TAPS // 2 - 1))
                    if tap == TAPS // 2 - 1:
                        ins.then_inc(ev("conv_ready"), 1)
                if j == S1["P_var"]:
                    pe.wait_ge(ev("y_ready"), c + 1)
                    pe.wait_ge(ev("s1_square"), c + 1)
                    mm(at3, mean64[:, :], s_b, start=True, stop=True).then_inc(ev("s1_var"), 1)
                if j == S1["P_in"]:
                    pe.wait_ge(ev("s1_norm"), c + 1)
                    pe.wait_ge(ev("s1_root"), min(c + 2, CK) if isinstance(c, int) else c + 2)
                    mm(at3, inw[:, :], s_n, start=True, stop=True).then_inc(ev("s1_in"), 1)

            def mix(l, c, j):
                at0 = bank[0][:, 0:SC]
                if j == MIX["P_mix"]:
                    pe.wait_ge(s_h, c * STEPS + (l * TP + STEPS))
                    mm(at0, cw[:, l, :], HS[:, ds(c * SC + B, SC)], start=True, stop=False)
                    mm(at0, dw[:, l, :], X[:, ds(c * SC, SC)], start=False, stop=True).then_inc(ev(f"l{l}_mix"), 1)
                if j == MIX["P_var"]:
                    pe.wait_ge(ev(f"l{l}_centered"), c + 1)
                    pe.wait_ge(ev(f"l{l}_square"), c + 1)
                    mm(at0, mean128[:, :], n_b, start=True, stop=True).then_inc(ev(f"l{l}_var"), 1)

            def output(c, j):
                at3 = bank[3][:, 0:SC]
                if j == OUT["P_out"]:
                    pe.wait_ge(ev("xn_ready"), c)
                    pe.wait_ge(ev("l1_norm"), c + 1)
                    mm(at3, outw[:, :], X[:, ds(c * SC, SC)], start=True, stop=True).then_inc(ev("o_product"), 1)
                if j == OUT["P_var"]:
                    pe.wait_ge(ev("o_square"), c + 1)
                    mm(at3, mean64[:, :], s_b, start=True, stop=True).then_inc(ev("o_var"), 1)

            pe.wait_ge(s_const, CONSTS)
            mm(bank[1][:, 0:P], space[0:1, 0:P], ones_row[:, 0:P], start=True, stop=True).then_inc(s_cnt, 1)
            pe.wait_ge(s_x[0], 16)
            pe.wait_ge(s_x[1], 16)
            pe.wait_ge(s_weff, 3)
            mm(bank[4][:, 0:2], mean128[:, :], cols[:, CD_B:CD_B + 2], start=True, stop=True)
            mm(bank[4][:, 2:3], mean64[:, :], cols[:, OUT_B:OUT_B + 1], start=True, stop=True)\
                .then_inc(ev("bias_means"), 1)
            pe.wait_ge(ev("biases_ready"), 1)
            stages = {"s1": s1, "output": output, "mix0": lambda c, j: mix(0, c, j), "mix1": lambda c, j: mix(1, c, j)}
            for i in BEFORE:
                for j in range(TI):
                    beside(i, i, j, stages)

            def turn(k):
                nc.tensor.transpose(bank[2][:, :].bitcast(bf16)[:, 0:P],
                                    onehot[:, k % 8, 0, :], ident_b[:, :]).then_inc(s_tr, 1)

            def pairs(k):
                mm(bank[4 + k % 2][:, 0:P], onehot_T[:, k % 4, :], onehot_T[:, k % 4, :],
                   start=True, stop=True).then_inc(s_pair, 1)

            pe.wait_ge(s_oh, 1)
            turn(0)
            pe.wait_ge(s_te, 1)
            pairs(0)
            pe.wait_ge(s_oh, 2)
            turn(1)

            def iteration(first, i):
                l = first // CK
                c = i - CK * l
                if l == 0:
                    pe.wait_ge(ev("x1_ready"), c + 1)
                    pe.wait_ge(ev("l0_root"), c)
                else:
                    pe.wait_ge(ev("l0_norm"), c + 1)
                    if first == CK:
                        pe.wait_ge(ev("l0_root"), CK)
                    else:
                        pe.wait_ge(ev("l1_root"), c)
                mm(bank[0][:, 0:SC], bw[:, l, :], X[:, ds(c * SC, SC)], start=True, stop=True)
                col0 = c * SC if isinstance(i, int) else pe.snap(c * SC)
                for j in range(TI):
                    if j < STEPS:
                        if j:
                            pe.wait_ge(s_h, i * STEPS + j)
                        mm(bank[0][:, j * B:j * B + B], aw[:, l, :], HS[:, ds(col0 + j * B, B)],
                           start=False, stop=True, skip_group_check=True).then_inc(s_pre, 1)
                    beside(first, i, j, stages)
                    pe.wait_ge(s_te, i * TI + (j + 2))
                    pairs(j + 1)
                    pe.wait_ge(s_oh, i * TI + (j + 3))
                    turn(j + 2)
                    pe.wait_ge(s_early, i * TI + (j + 1))
                    pe.wait_ge(s_cc, i * TI + (j + 1))
                    r = bank[6 + j % 2][:, 0:P]
                    mm(r, onehot_T[:, j % 4, :], counts[:, j % 2, :], start=True, stop=False)
                    mm(r, earlier[:, j % 2, :], onehot[:, j % 8, 1, :], start=False, stop=True)\
                        .then_inc(s_rps, 1)
                    mm(bank[1][:, 0:P], onehot[:, j % 8, 0, :], onehot[:, j % 8, 1, :],
                       start=False, stop=True, skip_group_check=True).then_inc(s_cnt, 1)

            over_ranges(pe, iteration)
            for i in AFTER:
                for j in range(TI):
                    beside(i, i, j, stages)

            def gat(c, k):
                pe.wait_ge(ev("xn_staged"), c + 1)
                for q in range(4):
                    last = mm(bank[4 + k][:, q * F:(q + 1) * F], turned_in[k][:, q * P:(q + 1) * P], wgat[:, :],
                              start=True, stop=True)
                last.then_inc(ev("gat_product"), 1)

            pe.wait_ge(s_early, ITERS * TI + 1)
            gat(0, 0)
            gat(1, 1)
            with pe.Fori(1, NC // 2) as i:
                for k in range(2):
                    pe.wait_ge(ev("gat_kept"), i * 2 + (k - 1))
                    gat(i * 2 + k, k)
            pe.wait_ge(ev("gat_kept"), NC - 2)
            gat(NC - 1, 0)

            pe.wait_ge(ev("gat_kept"), NC)
            pe.wait_ge(ev("hist_ready"), 1)
            hist = HS[:, NB * NB + 7 * NB + P:NB * NB + 7 * NB + P + 64]
            mm(bank[4][:, 0:64], mean128[:, :], hist, start=True, stop=True)
            mm(bank[5][:, 0:64], before[:, :], hist, start=True, stop=True)
            mm(bank[4][:, 64:65], before[:, :], mean128[:, 0:1], start=True, stop=True).then_inc(ev("hist_sums"), 1)
            pe.wait_ge(ev("sorted"), 1)

            pe.wait_ge(s_deg, 1)
            pe.wait_ge(s_rk, ITERS * TI)
            pe.wait_ge(s_te, ITERS * TI + 2)
            pe.wait_ge(ev("gat_kept"), NC + 1)
            with pe.Fori(0, NC) as c:
                pe.wait_ge(ev("expert_kept"), c * 4)
                pe.wait_ge(ev("h1_staged"), c + 1)
                for q in range(4):
                    last = nc.tensor.transpose(bank[4][:, q * P:(q + 1) * P], turned_in[0][:, q * P:(q + 1) * P],
                                               ident[:, :])
                last.then_inc(ev("h1_turned"), 1)
                for e in range(EXPERTS):
                    pe.wait_ge(ev("hidden_ready"), c * EXPERTS + e)
                    mm(bank[e][:, :], w1s[:, e, :], XT[:, ds(c * CH, CH)], start=True, stop=True)\
                        .then_inc(ev("hidden_product"), 1)
                pe.wait_ge(ev("hidden_ready"), c * EXPERTS + EXPERTS)
                pe.wait_ge(ev("h1_kept"), c + 1)
                for q in range(4):
                    for e in range(EXPERTS):
                        mm(bank[4 + q][:, e * C:(e + 1) * C], hid[:, e, q * P:(q + 1) * P], w2s[:, e, :],
                           start=True, stop=False)
                        last = mm(bank[4 + q][:, e * C:(e + 1) * C], ones_row[:, 0:P],
                                  b2row[:, e * C:(e + 1) * C], start=False, stop=True)
                    last.then_inc(ev("expert_product"), 1)



_INS = ["x_t", "conv_wr", "conv_wi", "phases", "in_w", "in_b", "a_w", "b_w", "b_b", "c_w", "c_b", "d_w", "d_b",
        "ln_w", "ln_b", "out_w", "out_b", "w_gat", "att_src", "att_dst", "b_gat", "gamma", "beta",
        "w1", "b1", "w2", "b2", "edges"]


def _laid_out(i):
    import numpy as np

    a = {k.removeprefix("L0_"): np.asarray(v) for k, v in i.items()}
    P = 128

    def taps(w):
        return w.transpose(1, 2, 0).reshape(64, 8, 2, 64).transpose(2, 0, 1, 3).reshape(P, 8, 64)

    def turned(w):
        return w.transpose(2, 0, 1)

    return {
        "x_t": a["x"].transpose(2, 1, 0).reshape(64, 750 * 16),
        "conv_wr": taps(a["tok_w_real"]), "conv_wi": taps(a["tok_w_imag"]),
        "phases": np.repeat(a["tok_phases"].reshape(8, 2).T, 64, axis=0),
        "in_w": a["attn_in_W"].T, "in_b": a["attn_in_b"],
        "a_w": turned(a["attn_A_W"]), "b_w": turned(a["attn_B_W"]), "b_b": a["attn_B_b"].T,
        "c_w": turned(a["attn_C_W"]), "c_b": a["attn_C_b"].T, "d_w": turned(a["attn_D_W"]), "d_b": a["attn_D_b"].T,
        "ln_w": a["attn_ln_w"].T, "ln_b": a["attn_ln_b"].T,
        "out_w": a["attn_out_W"].T, "out_b": a["attn_out_b"],
        "w_gat": a["ffn_W_gat"], "att_src": a["ffn_att_src"].reshape(16), "att_dst": a["ffn_att_dst"].reshape(16),
        "b_gat": a["ffn_b_gat"], "gamma": a["ffn_ln_gamma"], "beta": a["ffn_ln_beta"],
        "w1": a["ffn_W1"].transpose(1, 0, 2), "b1": a["ffn_b1"].T,
        "w2": a["ffn_W2"].transpose(1, 0, 2), "b2": a["ffn_b2"].reshape(1, 256),
        "edges": a["ffn_edge_index"].reshape(2, P, -1).transpose(1, 0, 2).reshape(P, -1),
    }


def kernel(**inputs):
    import numpy as np
    import concourse.bacc as bacc
    from concourse.bass_utils import run_bass_kernel_spmd

    laid = _laid_out(inputs)
    nc = bacc.Bacc("TRN2", target_bir_lowering=False, num_devices=1)
    arrays, args = {}, []
    for name in _INS:
        a = np.ascontiguousarray(laid[name])
        arrays[f"in_{name}"] = a
        args.append(nc.dram_tensor(f"in_{name}", a.shape, mybir.dt.from_np(a.dtype), kind="ExternalInput").ap())
    out = nc.dram_tensor("out_h", (16, 735, 64), mybir.dt.float32, kind="ExternalOutput").ap()
    audio_tower_program(nc, *args, out)
    r = run_bass_kernel_spmd(nc, [arrays], core_ids=[0])
    return r.results[0]["out_h"]
```
